# Optimizing a Trainium2 kernel written in Bass

```python
import numpy as np
import jax
import jax.numpy as jnp

def _softmax(x, axis=-1):
    return jax.nn.softmax(x, axis=axis)

def _gelu(x):
    return jax.nn.gelu(x, approximate=True)

def _silu(x):
    return jax.nn.silu(x)

def _sigmoid(x):
    return jax.nn.sigmoid(x)

def _layernorm(x, axis=-1, eps=1e-05):
    m = jnp.mean(x, axis=axis, keepdims=True)
    v = jnp.var(x, axis=axis, keepdims=True)
    return (x - m) / jnp.sqrt(v + eps)

def _scatter_add(tgt, idx, src, axis=0):
    return tgt.at[idx].add(src)

def _segment_sum(src, seg, n):
    return jax.ops.segment_sum(src, seg, n)
kernel_name = 'mk_macaron_d2_jaxref_r8_6fb5b3'

def setup_inputs(seed: int=0):
    np.random.seed(seed)
    _w = jnp.asarray

    def _L0_attn_setup():
        import math
        import jax, jax.numpy as jnp
        import numpy as np
        B, S, E, H = (1, 256, 256, 16)
        QL, KL = (192, 64)
        DN, DR, DV = (128, 64, 128)
        DQ = DN + DR
        ROPE_BASE = 10000.0
        EPS = 1e-06

        def _rope_cache(seq_len):
            inv_freq = 1.0 / ROPE_BASE ** (np.arange(0, DR, 2, dtype=np.float32) / DR)
            t = np.arange(seq_len, dtype=np.float32)
            freqs = np.outer(t, inv_freq)
            emb = np.concatenate([freqs, freqs], axis=-1)
            return (jnp.asarray(np.cos(emb)), jnp.asarray(np.sin(emb)))

        def _rmsnorm(x, w):
            return x * jax.lax.rsqrt(jnp.mean(x * x, axis=-1, keepdims=True) + EPS) * w

        def _apply_rope(x, cos, sin):
            b, s, h, d = x.shape
            xr = x.reshape(b, s, h, d // 2, 2)
            x = jnp.concatenate([xr[..., 0], xr[..., 1]], axis=-1)
            rot = jnp.concatenate([-x[..., d // 2:], x[..., :d // 2]], axis=-1)
            return x * cos[None, :, None, :] + rot * sin[None, :, None, :]
        key = jax.random.key(seed)
        ks = jax.random.split(key, 8)
        w = lambda k, shape, fan_in: jax.random.normal(k, shape, jnp.float32) / math.sqrt(fan_in)
        return {'x': jax.random.normal(ks[0], (B, S, E), jnp.float32), 'w_q_a': w(ks[1], (E, QL), E), 'q_a_ln': jnp.ones((QL,), jnp.float32), 'w_q_b': w(ks[2], (QL, H * DQ), QL), 'w_kv_a': w(ks[3], (E, KL + DR), E), 'kv_a_ln': jnp.ones((KL,), jnp.float32), 'w_kv_b': w(ks[4], (KL, H * (DN + DV)), KL), 'w_out': w(ks[5], (H * DV, E), H * DV)}
    _L0_attn_in = _L0_attn_setup()

    def _L0_ffn_setup():
        import jax, jax.numpy as jnp
        import numpy as np
        B, S, D = (4, 512, 256)
        DFF = 4 * D
        CAPACITY = 0.125
        K = int(CAPACITY * S)
        key = jax.random.key(seed)
        ks = jax.random.split(key, 8)
        sc = 1.0 / np.sqrt(D)
        return {'x': jax.random.normal(ks[0], (B, S, D), dtype=jnp.float32), 'W_r': jax.random.normal(ks[1], (D, 1), dtype=jnp.float32) * sc, 'b_r': jnp.zeros((1,), dtype=jnp.float32), 'W1': jax.random.normal(ks[2], (D, DFF), dtype=jnp.float32) * sc, 'b1': jnp.zeros((DFF,), dtype=jnp.float32), 'W2': jax.random.normal(ks[3], (DFF, D), dtype=jnp.float32) * (1.0 / np.sqrt(DFF)), 'b2': jnp.zeros((D,), dtype=jnp.float32), 'position_ids': jnp.arange(B * S, dtype=jnp.int64 if jax.config.jax_enable_x64 else jnp.int32).reshape(B, S), 'cache_position': jnp.arange(S, dtype=jnp.int64 if jax.config.jax_enable_x64 else jnp.int32)}
    _L0_ffn_in = _L0_ffn_setup()

    def _L1_attn_setup():
        import math
        import jax, jax.numpy as jnp
        import numpy as np
        N_HEADS = 16
        ROPE_BASE = 10000.0

        def _rope(x):
            B, H, S, D = x.shape
            half = D // 2
            inv_freq = 1.0 / ROPE_BASE ** (jnp.arange(half, dtype=jnp.float32) / half)
            ang = jnp.arange(S, dtype=jnp.float32)[:, None] * inv_freq[None, :]
            cos, sin = (jnp.cos(ang), jnp.sin(ang))
            x1 = x[..., 0::2]
            x2 = x[..., 1::2]
            o1 = x1 * cos - x2 * sin
            o2 = x1 * sin + x2 * cos
            return jnp.stack([o1, o2], axis=-1).reshape(B, H, S, D)
        key = jax.random.key(seed)
        ks = jax.random.split(key, 5)
        B, S, E = (2, 256, 256)
        scale = 1.0 / math.sqrt(E)
        return {'x': jax.random.normal(ks[0], (B, S, E), dtype=jnp.float32), 'Wq': jax.random.normal(ks[1], (E, E), dtype=jnp.float32) * scale, 'Wk': jax.random.normal(ks[2], (E, E), dtype=jnp.float32) * scale, 'Wv': jax.random.normal(ks[3], (E, E), dtype=jnp.float32) * scale, 'Wo': jax.random.normal(ks[4], (E, E), dtype=jnp.float32) * scale}
    _L1_attn_in = _L1_attn_setup()

    def _L1_ffn_setup():
        import math
        import jax, jax.numpy as jnp
        import numpy as np
        DIM = 256
        RANK = 8
        B, T = (4, 512)

        def _orthogonal(key, n):
            a = jax.random.normal(key, (n, n), dtype=jnp.float32)
            q, r = jnp.linalg.qr(a)
            q = q * jnp.sign(jnp.diagonal(r))[None, :]
            return q
        key = jax.random.key(seed)
        kx, kf = jax.random.split(key)
        x = jax.random.normal(kx, (B, T, DIM), dtype=jnp.float32)
        fkeys = jax.random.split(kf, RANK)
        factors = jnp.stack([_orthogonal(fkeys[r], DIM) * (r + 1) ** (-0.5) for r in range(RANK)])
        bias = jnp.zeros((DIM,), dtype=jnp.float32)
        return {'x': x, 'factors': factors, 'bias': bias}
    _L1_ffn_in = _L1_ffn_setup()
    _d = {'L0_attn_x': _L0_attn_in['x'], 'L0_attn_w_q_a': _L0_attn_in['w_q_a'], 'L0_attn_q_a_ln': _L0_attn_in['q_a_ln'], 'L0_attn_w_q_b': _L0_attn_in['w_q_b'], 'L0_attn_w_kv_a': _L0_attn_in['w_kv_a'], 'L0_attn_kv_a_ln': _L0_attn_in['kv_a_ln'], 'L0_attn_w_kv_b': _L0_attn_in['w_kv_b'], 'L0_attn_w_out': _L0_attn_in['w_out'], 'L0_ffn_W_r': _L0_ffn_in['W_r'], 'L0_ffn_b_r': _L0_ffn_in['b_r'], 'L0_ffn_W1': _L0_ffn_in['W1'], 'L0_ffn_b1': _L0_ffn_in['b1'], 'L0_ffn_W2': _L0_ffn_in['W2'], 'L0_ffn_b2': _L0_ffn_in['b2'], 'L0_ffn_position_ids': _L0_ffn_in['position_ids'], 'L0_ffn_cache_position': _L0_ffn_in['cache_position'], 'L1_attn_Wq': _L1_attn_in['Wq'], 'L1_attn_Wk': _L1_attn_in['Wk'], 'L1_attn_Wv': _L1_attn_in['Wv'], 'L1_attn_Wo': _L1_attn_in['Wo'], 'L1_ffn_factors': _L1_ffn_in['factors'], 'L1_ffn_bias': _L1_ffn_in['bias']}
    _x0 = _d['L0_attn_x']
    _d['L0_attn_x'] = jax.random.normal(jax.random.fold_in(jax.random.key(seed), 1), (1, 2048, 256), dtype=_x0.dtype)
    del _x0
    return _d

def reference(L0_attn_x, L0_attn_w_q_a, L0_attn_q_a_ln, L0_attn_w_q_b, L0_attn_w_kv_a, L0_attn_kv_a_ln, L0_attn_w_kv_b, L0_attn_w_out, L0_ffn_W_r, L0_ffn_b_r, L0_ffn_W1, L0_ffn_b1, L0_ffn_W2, L0_ffn_b2, L0_ffn_position_ids, L0_ffn_cache_position, L1_attn_Wq, L1_attn_Wk, L1_attn_Wv, L1_attn_Wo, L1_ffn_factors, L1_ffn_bias):

    def _L0_attn_ref(x, w_q_a, q_a_ln, w_q_b, w_kv_a, kv_a_ln, w_kv_b, w_out):
        import math
        import jax, jax.numpy as jnp
        import numpy as np
        B, S, E, H = (1, 256, 256, 16)
        QL, KL = (192, 64)
        DN, DR, DV = (128, 64, 128)
        DQ = DN + DR
        ROPE_BASE = 10000.0
        EPS = 1e-06

        def _rope_cache(seq_len):
            inv_freq = 1.0 / ROPE_BASE ** (np.arange(0, DR, 2, dtype=np.float32) / DR)
            t = np.arange(seq_len, dtype=np.float32)
            freqs = np.outer(t, inv_freq)
            emb = np.concatenate([freqs, freqs], axis=-1)
            return (jnp.asarray(np.cos(emb)), jnp.asarray(np.sin(emb)))

        def _rmsnorm(x, w):
            return x * jax.lax.rsqrt(jnp.mean(x * x, axis=-1, keepdims=True) + EPS) * w

        def _apply_rope(x, cos, sin):
            b, s, h, d = x.shape
            xr = x.reshape(b, s, h, d // 2, 2)
            x = jnp.concatenate([xr[..., 0], xr[..., 1]], axis=-1)
            rot = jnp.concatenate([-x[..., d // 2:], x[..., :d // 2]], axis=-1)
            return x * cos[None, :, None, :] + rot * sin[None, :, None, :]
        b, s, _ = x.shape
        q = (_rmsnorm(x @ w_q_a, q_a_ln) @ w_q_b).reshape(b, s, H, DQ)
        q_nope, q_pe = (q[..., :DN], q[..., DN:])
        ckv = x @ w_kv_a
        c_kv, k_pe = (ckv[..., :KL], ckv[..., KL:])
        kv = (_rmsnorm(c_kv, kv_a_ln) @ w_kv_b).reshape(b, s, H, DN + DV)
        k_nope, v = (kv[..., :DN], kv[..., DN:])
        cos, sin = _rope_cache(s)
        q_pe = _apply_rope(q_pe, cos, sin)
        k_pe = _apply_rope(k_pe.reshape(b, s, 1, DR), cos, sin)
        qf = jnp.concatenate([q_nope, q_pe], axis=-1)
        kf = jnp.concatenate([k_nope, jnp.broadcast_to(k_pe, (b, s, H, DR))], axis=-1)
        scale = 1.0 / math.sqrt(DQ)
        scores = jnp.einsum('bqhd,bkhd->bhqk', qf, kf) * scale
        mask = jnp.tril(jnp.ones((s, s), dtype=bool))
        scores = jnp.where(mask[None, None], scores, jnp.finfo(scores.dtype).min)
        p = jax.nn.softmax(scores, axis=-1)
        o = jnp.einsum('bhqk,bkhd->bqhd', p, v).reshape(b, s, H * DV)
        return o @ w_out

    def _L0_ffn_ref(x, W_r, b_r, W1, b1, W2, b2, position_ids, cache_position):
        import jax, jax.numpy as jnp
        import numpy as np
        B, S, D = (4, 512, 256)
        DFF = 4 * D
        CAPACITY = 0.125
        K = int(CAPACITY * S)
        b, s, d = x.shape
        weights = jnp.einsum('bsd,do->bso', x, W_r).squeeze(-1) + b_r
        topk_vals, topk_idx = jax.lax.top_k(weights, K)
        threshold = topk_vals[:, -1]
        sel_mask = weights > threshold[:, None]
        xg = jnp.take_along_axis(x, topk_idx[..., None], axis=1)
        h = jax.nn.gelu(jnp.einsum('bkd,df->bkf', xg, W1) + b1)
        blk = jnp.einsum('bkf,fd->bkd', h, W2) + b2
        gate = (topk_vals > threshold[:, None]).astype(x.dtype)
        wg = jnp.take_along_axis(weights, topk_idx, axis=1)
        vals = blk * (wg * gate)[..., None]
        bidx = jnp.arange(b)[:, None]
        processed = jnp.zeros_like(x).at[bidx, topk_idx].add(vals)
        return processed + x * (~sel_mask)[..., None].astype(x.dtype)

    def _L1_attn_ref(x, Wq, Wk, Wv, Wo):
        import math
        import jax, jax.numpy as jnp
        import numpy as np
        N_HEADS = 16
        ROPE_BASE = 10000.0

        def _rope(x):
            B, H, S, D = x.shape
            half = D // 2
            inv_freq = 1.0 / ROPE_BASE ** (jnp.arange(half, dtype=jnp.float32) / half)
            ang = jnp.arange(S, dtype=jnp.float32)[:, None] * inv_freq[None, :]
            cos, sin = (jnp.cos(ang), jnp.sin(ang))
            x1 = x[..., 0::2]
            x2 = x[..., 1::2]
            o1 = x1 * cos - x2 * sin
            o2 = x1 * sin + x2 * cos
            return jnp.stack([o1, o2], axis=-1).reshape(B, H, S, D)
        B, S, E = x.shape
        H = N_HEADS
        D = E // H
        attn_scale = 1.0 / math.sqrt(E)

        def proj(W):
            return (x @ W.T).reshape(B, S, H, D).transpose(0, 2, 1, 3)
        q = _rope(proj(Wq))
        k = _rope(proj(Wk))
        v = proj(Wv)
        scores = jnp.einsum('bhsd,bhtd->bhst', q, k) * attn_scale
        causal = jnp.triu(jnp.ones((S, S), dtype=bool), k=1)
        scores = jnp.where(causal, -jnp.inf, scores)
        probs = jax.nn.softmax(scores, axis=-1)
        out = jnp.einsum('bhst,bhtd->bhsd', probs, v)
        out = out.transpose(0, 2, 1, 3).reshape(B, S, E)
        return out @ Wo.T

    def _L1_ffn_ref(x, factors, bias):
        import math
        import jax, jax.numpy as jnp
        import numpy as np
        DIM = 256
        RANK = 8
        B, T = (4, 512)

        def _orthogonal(key, n):
            a = jax.random.normal(key, (n, n), dtype=jnp.float32)
            q, r = jnp.linalg.qr(a)
            q = q * jnp.sign(jnp.diagonal(r))[None, :]
            return q
        rank = factors.shape[0]
        mixed = jnp.einsum('btd,rde->bte', x, factors)
        mixed = mixed / math.sqrt(rank) + bias
        return mixed
    x = L0_attn_x
    x = x + 0.5 * _L0_ffn_ref(_layernorm(x, axis=-1), L0_ffn_W_r, L0_ffn_b_r, L0_ffn_W1, L0_ffn_b1, L0_ffn_W2, L0_ffn_b2, L0_ffn_position_ids, L0_ffn_cache_position)
    x = x + _L0_attn_ref(_layernorm(x, axis=-1), L0_attn_w_q_a, L0_attn_q_a_ln, L0_attn_w_q_b, L0_attn_w_kv_a, L0_attn_kv_a_ln, L0_attn_w_kv_b, L0_attn_w_out)
    x = x + 0.5 * _L0_ffn_ref(_layernorm(x, axis=-1), L0_ffn_W_r, L0_ffn_b_r, L0_ffn_W1, L0_ffn_b1, L0_ffn_W2, L0_ffn_b2, L0_ffn_position_ids, L0_ffn_cache_position)
    x = x + 0.5 * _L1_ffn_ref(_layernorm(x, axis=-1), L1_ffn_factors, L1_ffn_bias)
    x = x + _L1_attn_ref(_layernorm(x, axis=-1), L1_attn_Wq, L1_attn_Wk, L1_attn_Wv, L1_attn_Wo)
    x = x + 0.5 * _L1_ffn_ref(_layernorm(x, axis=-1), L1_ffn_factors, L1_ffn_bias)
    return x

_drawn_inputs = setup_inputs


def setup_inputs(seed=0):
    import zlib

    import numpy as np

    out = dict(_drawn_inputs(seed))
    spreads = {'L0_attn_q_a_ln': (1.0, 0.542),
     'L0_attn_kv_a_ln': (1.0, 0.549),
     'L0_ffn_b1': (0.0, 0.412),
     'L0_ffn_b2': (0.0, 0.338),
     'L1_ffn_bias': (0.0, 0.1)}
    factors = {'L1_attn_Wq': 6.16, 'L1_attn_Wk': 5.503}
    for name, (base, spread) in spreads.items():
        noise = np.random.default_rng([zlib.crc32(name.encode()), seed]).standard_normal(out[name].shape)
        drawn = base * np.exp(spread * noise) if base else spread * noise
        out[name] = jnp.asarray(drawn.astype(out[name].dtype))
    for name, factor in factors.items():
        out[name] = (out[name] * factor).astype(out[name].dtype)
    return out
```

```python
import numpy as np
from contextlib import ExitStack

import concourse.bass as bass
from concourse import mybir

F32 = mybir.dt.float32
F32R = mybir.dt.float32r
BF16 = mybir.dt.bfloat16
ALU = mybir.AluOpType
ACT = mybir.ActivationFunctionType
AX = mybir.AxisListType

P = 128
TOKENS = 2048
DIM = 256
NT = TOKENS // P
ND = DIM // P
CH = 512
NCH = TOKENS // CH
TPC = CH // P

DFF = 1024
NF = DFF // P
CAPACITY = 64

H0 = 16
QL, KL = 192, 64
DN, DR, DV = 128, 64, 128
DQ = DN + DR
SCALE0 = 1.0 / float(np.sqrt(DQ))
RMS_EPS = 1e-6
PAIRS = H0 // 2
KT_PER_PAIR = sum(TPC * (j + 1) for j in range(NCH))

H1, D1 = 16, 16
SCALE1 = 1.0 / float(np.sqrt(DIM))
GROUP = 4
NG = H1 // GROUP
SLOT = 64

RANK = 8
LN_EPS = 1e-5
MASKED = -1e30


def shape_constants():
    eye = np.eye(P, dtype=np.float32)
    row = np.arange(P)
    before = (row[:, None] < row[None, :]).astype(np.float32)
    iota = np.broadcast_to(row.astype(np.float32), (P, P))
    square = np.concatenate([eye, before, iota, np.ones((P, P), np.float32)], axis=1)
    ahead = np.where(row[None, :] > row[:, None], MASKED, 0.0)
    masks = np.concatenate([eye, ahead, ahead.T], axis=1).astype(np.float32)
    t = np.arange(TOKENS, dtype=np.float32)
    f0 = np.outer(t, (1.0 / 10000.0 ** (np.arange(0, DR, 2, dtype=np.float32) / DR)).astype(np.float32)).astype(np.float32)
    cos0, sin0 = np.cos(f0), np.sin(f0)
    half0 = DR // 2
    col0 = np.zeros((P, 2, TOKENS), np.float32)
    col0[DR:DR + half0, 0], col0[DR + half0:, 0] = cos0.T, cos0.T
    col0[DR:DR + half0, 1], col0[DR + half0:, 1] = sin0.T, -sin0.T
    tok0 = np.stack([cos0, sin0], axis=1).reshape(NT, P, 2, half0).transpose(1, 2, 0, 3)
    half1 = D1 // 2
    f1 = np.outer(t, (1.0 / 10000.0 ** (np.arange(half1, dtype=np.float32) / half1)).astype(np.float32)).astype(np.float32)
    both = np.stack([np.repeat(np.cos(f1), 2, axis=1), np.repeat(np.sin(f1), 2, axis=1)], axis=1)
    tok1 = both.reshape(NT, P, 2, D1).transpose(1, 2, 0, 3)
    return {"c_square": np.ascontiguousarray(square), "c_masks": masks,
            "c_rope0_feature": col0, "c_rope0_token": np.ascontiguousarray(tok0),
            "c_rope1_token": np.ascontiguousarray(tok1)}


class Core:

    def __init__(self, nc, ctx, inp):
        self.nc, self.ctx, self.inp = nc, ctx, inp
        self.step_semaphores = []
        self.mixed_ready = False
        self.x = self.sb("x", [P, NT, DIM], F32)
        self.square = self.sb("square", [P, 4, P], F32)
        self.masks = self.sb("masks", [P, 3, P], BF16)
        self.mixed = self.sb("mixed", [P, ND, DIM], F32)
        self.half_bias = self.sb("half_bias", [P, DIM], F32)
        self.ident = self.square[:, 0, :]
        self.before = self.square[:, 1, :]
        self.iota = self.square[:, 2, :]
        self.ones = self.square[:, 3, :]
        self.ident_b = self.masks[:, 0, :]
        self.mask_qk = self.masks[:, 1, :]
        self.mask_kq = self.masks[:, 2, :]

    def sb(self, name, shape, dt, ctx=None):
        return (ctx or self.ctx).enter_context(self.nc.sbuf_tensor(name, shape, dt))

    def sem(self, name):
        s = self.nc.alloc_semaphore(name)
        self.step_semaphores.append(s)
        return s

    def end_step(self):
        self.nc.clear_and_free_semaphores(self.step_semaphores)
        self.nc.all_engine_barrier()
        self.step_semaphores = []


class Link:

    def __init__(self, core, engine, name):
        self.sem, self.engine, self.n = core.sem(name), engine, 0

    def __call__(self, instruction):
        instruction.then_inc(self.sem, 1)
        self.n += 1
        self.engine.wait_ge(self.sem, self.n)


def load_stage(core):
    nc, inp = core.nc, core.inp
    with ExitStack() as ctx:
        masks = core.sb("masks_whole", [P, 3, P], F32, ctx)
        x_loaded, square_loaded, masks_loaded = (core.sem(n) for n in ("x_loaded", "square_loaded", "masks_loaded"))
        masks_ready = core.sem("masks_ready")
        rows = inp["L0_attn_x"][0].rearrange("(t p) d -> p t d", p=P)
        with nc.Block() as block:
            @block.sync
            def _(sp):
                for c in range(0, NCH, 2):
                    sp.dma_start(core.x[:, TPC * c:TPC * (c + 1), :], rows[:, TPC * c:TPC * (c + 1), :]).then_inc(x_loaded, 16)
                sp.dma_start(core.square[:], inp["c_square"].rearrange("p (a b) -> p a b", b=P)).then_inc(square_loaded, 16)
                sp.wait_ge(x_loaded, 16 * NCH)
                sp.wait_ge(square_loaded, 16)

            @block.scalar
            def _(act):
                for c in range(1, NCH, 2):
                    act.dma_start(core.x[:, TPC * c:TPC * (c + 1), :], rows[:, TPC * c:TPC * (c + 1), :]).then_inc(x_loaded, 16)
                act.dma_start(masks[:], inp["c_masks"].rearrange("p (a b) -> p a b", b=P)).then_inc(masks_loaded, 16)

            @block.vector
            def _(dve):
                dve.wait_ge(masks_loaded, 16)
                nc.vector.tensor_copy(core.masks[:], masks[:]).then_inc(masks_ready, 1)
                dve.wait_ge(masks_ready, 1)
    core.end_step()


class Turn:

    def __init__(self, core, tag, source, target, banks, source_complete=False):
        self.core, self.source, self.target, self.banks = core, source, target, banks
        self.source_ready = None if source_complete else core.sem(f"{tag}_source_ready")
        self.turned = core.sem(f"{tag}_turned")
        self.evac_dve = core.sem(f"{tag}_evac_dve")
        self.evac_act = core.sem(f"{tag}_evac_act")

    def place(self, b):
        c, d = divmod(b, ND)
        return self.target[:, d, c * CH:(c + 1) * CH]

    def vector(self, dve):
        for b in range(0, 2 * NCH, 2):
            dve.wait_ge(self.turned, b + 1)
            self.core.nc.vector.tensor_copy(self.place(b), self.banks[b % len(self.banks)][:]).then_inc(self.evac_dve, 1)

    def scalar(self, act):
        for b in range(1, 2 * NCH, 2):
            act.wait_ge(self.turned, b + 1)
            self.core.nc.scalar.activation(self.place(b), self.banks[b % len(self.banks)][:], ACT.Copy).then_inc(self.evac_act, 1)

    def tensor(self, pe):
        nc, n = self.core.nc, len(self.banks)
        for b in range(2 * NCH):
            c, d = divmod(b, ND)
            if self.source_ready is not None:
                pe.wait_ge(self.source_ready, TPC * (c + 1))
            if b >= n:
                pe.wait_ge(self.evac_act if b % 2 else self.evac_dve, (b - n) // 2 + 1)
            for i in range(TPC):
                last = nc.tensor.transpose(self.banks[b % n][:, i * P:(i + 1) * P],
                                           self.source[:, TPC * c + i, d * P:(d + 1) * P], self.core.ident)
            last.then_inc(self.turned, 1)

    def wait_chunk(self, engine, c):
        engine.wait_ge(self.evac_dve, c + 1)
        engine.wait_ge(self.evac_act, c + 1)


class Norm:

    def __init__(self, core, ctx, tag, xn, xn_t, banks):
        self.core, self.xn = core, xn
        self.stats = core.sb(f"{tag}_stats", [P, NT, 6], F32, ctx)
        self.moments = core.sb(f"{tag}_moments", [P, NT, 2], F32, ctx)
        self.var = core.sb(f"{tag}_var", [P, NT], F32, ctx)
        self.root = core.sb(f"{tag}_root", [P, NT], F32, ctx)
        self.rstd = core.sb(f"{tag}_rstd", [P, NT], F32, ctx)
        self.scratch = core.sb(f"{tag}_scratch", [P, NT], F32, ctx)
        self.var_ready = core.sem(f"{tag}_var_ready")
        self.root_ready = core.sem(f"{tag}_root_ready")
        self.turn = Turn(core, tag, xn, xn_t, banks)
        self.xn_ready = self.turn.source_ready

    def vector(self, dve, link):
        nc, x = self.core.nc, self.core.x
        for t in range(NT):
            s = nc.vector.bn_stats(self.stats[:, t, :], x[:, t, :])
        link(s)
        for t in range(NT):
            s = nc.vector.bn_aggr(self.moments[:, t, :], self.stats[:, t, :])
        link(s)
        nc.vector.tensor_scalar(self.var[:], self.moments[:, :, 1], LN_EPS, None, ALU.add).then_inc(self.var_ready, 1)
        dve.wait_ge(self.root_ready, 1)
        reciprocal_of_root(nc, link, self.rstd[:], self.root[:], self.var[:], self.scratch[:])
        for t in range(NT):
            nc.vector.tensor_scalar(self.xn[:, t, :], x[:, t, :], self.moments[:, t, 0:1], self.rstd[:, t:t + 1],
                                    ALU.subtract, ALU.mult).then_inc(self.xn_ready, 1)
        self.turn.vector(dve)

    def scalar(self, act):
        act.wait_ge(self.var_ready, 1)
        self.core.nc.scalar.activation(self.root[:], self.var[:], ACT.Sqrt).then_inc(self.root_ready, 1)
        self.turn.scalar(act)

    def tensor(self, pe):
        self.turn.tensor(pe)


def reciprocal_of_root(nc, link, out, root, value, scratch):
    link(nc.vector.reciprocal(out, root))
    link(nc.vector.tensor_tensor(scratch, out, out, ALU.mult))
    link(nc.vector.tensor_tensor(scratch, scratch, value, ALU.mult))
    link(nc.vector.tensor_scalar(scratch, scratch, -0.5, 1.5, ALU.mult, ALU.add))
    link(nc.vector.tensor_tensor(out, out, scratch, ALU.mult))


def routed_ffn_stage(core, tag):
    nc, inp, x = core.nc, core.inp, core.x
    with ExitStack() as ctx:
        def sb(name, shape, dt=F32):
            return core.sb(f"{tag}_{name}", shape, dt, ctx)
        xn, xn_t = sb("xn", [P, NT, DIM]), sb("xn_t", [P, ND, TOKENS])
        w_r, w_r_wide = sb("w_r", [P, ND]), sb("w_r_wide", [P, ND, P])
        b_r = sb("b_r", [P, 1])
        w1, w2 = sb("w1", [P, ND, DFF]), sb("w2", [P, NF, DIM])
        b1, b2 = sb("b1", [P, NF]), sb("b2", [P, DIM])
        weight_row = sb("weight_row", [P, TOKENS])
        weight = sb("weight", [P, NT])
        not_below = sb("not_below", [P, 2, TOKENS], BF16)
        count = sb("count", [P, NT])
        chosen, keep_scale, take_scale = sb("chosen", [P, NT]), sb("keep_scale", [P, NT]), sb("take_scale", [P, NT])
        ranks = sb("ranks", [P, 3, NT])
        onehot, onehot_t = sb("onehot", [P, NT, P]), sb("onehot_t", [P, NT, P])
        picked, picked_t = sb("picked", [P, DIM]), sb("picked_t", [P, ND, P])
        hidden = sb("hidden", [P, NF, P])
        block_out = sb("block_out", [P, DIM])
        bank = [ctx.enter_context(nc.psum_tensor(f"{tag}_bank{i}", [P, CH], F32)) for i in range(8)]
        norm = Norm(core, ctx, tag, xn, xn_t, bank)
        names = ("weights_loaded ffn_loaded wide_ready weight_bank row_ready weight_turned counted chosen_ready"
                 " prefix_done onehot_ready picked_done picked_copied picked_turned picked_t_ready hidden_done"
                 " hidden_ready block_done block_ready onehot_turned onehot_t_act onehot_t_dve scattered added").split()
        s = {n: core.sem(f"{tag}_{n}") for n in names}

        with nc.Block() as block:
            @block.sync
            def _(sp):
                sp.dma_start(w_r[:], inp["L0_ffn_W_r"].rearrange("(k p) o -> p (k o)", p=P),
                             allow_slow_non_contiguous=True).then_inc(s["weights_loaded"], 16)
                sp.dma_start(b_r[:], inp["L0_ffn_b_r"].partition_broadcast(P)).then_inc(s["weights_loaded"], 16)
                sp.dma_start(w1[:], inp["L0_ffn_W1"].rearrange("(k p) f -> p k f", p=P)).then_inc(s["ffn_loaded"], 16)
                sp.dma_start(w2[:], inp["L0_ffn_W2"].rearrange("(k p) d -> p k d", p=P)).then_inc(s["ffn_loaded"], 16)
                sp.dma_start(b1[:], inp["L0_ffn_b1"].rearrange("(k p) -> p k", p=P),
                             allow_slow_non_contiguous=True).then_inc(s["ffn_loaded"], 16)
                sp.dma_start(b2[:], inp["L0_ffn_b2"].partition_broadcast(P)).then_inc(s["ffn_loaded"], 16)

            @block.vector
            def _(dve):
                link = Link(core, dve, f"{tag}_dve_link")
                dve.wait_ge(s["weights_loaded"], 32)
                nc.vector.tensor_copy(w_r_wide[:], w_r[:].unsqueeze(2).broadcast_to([P, ND, P])).then_inc(s["wide_ready"], 1)
                norm.vector(dve, link)
                for c in range(NCH):
                    dve.wait_ge(s["weight_turned"], c + 1)
                    w = nc.vector.tensor_copy(weight[:, TPC * c:TPC * (c + 1)],
                                              bank[4 + c][:].rearrange("p (t q) -> p t q", q=P)[:, :, 0])
                link(w)
                for t in range(NT):
                    if t >= 2:
                        dve.wait_ge(s["counted"], t - 1)
                    nc.vector.tensor_scalar(not_below[:, t % 2], weight_row[:], weight[:, t:t + 1], None,
                                            ALU.is_ge, ALU.add, accum_out=count[:, t:t + 1]).then_inc(s["counted"], 1)
                dve.wait_ge(s["counted"], NT)
                nc.vector.tensor_scalar(chosen[:], count[:], CAPACITY - 0.5, None, ALU.is_lt).then_inc(s["chosen_ready"], 1)
                dve.wait_ge(s["chosen_ready"], 1)
                nc.vector.tensor_scalar(keep_scale[:], chosen[:], -0.5, 0.5, ALU.mult, ALU.add)
                link(nc.vector.tensor_scalar(take_scale[:], weight[:], 0.5, None, ALU.mult))
                dve.wait_ge(s["prefix_done"], 1)
                link(nc.vector.memset(ranks[:, 0, 0:1], 0.0))
                link(nc.vector.tensor_copy(ranks[:, 0, 1:NT], bank[1][:, 0:NT - 1]))
                src = 0
                for step in (1, 2, 4, 8):
                    link(nc.vector.tensor_copy(ranks[:, 1 - src, 0:step], ranks[:, src, 0:step]))
                    link(nc.vector.tensor_tensor(ranks[:, 1 - src, step:NT], ranks[:, src, step:NT],
                                                 ranks[:, src, 0:NT - step], ALU.add))
                    src = 1 - src
                link(nc.vector.tensor_tensor(ranks[:, 2, :], bank[0][:, 0:NT], ranks[:, src, :], ALU.add))
                for t in range(NT):
                    nc.vector.tensor_scalar(onehot[:, t, :], core.iota, ranks[:, 2, t:t + 1], chosen[:, t:t + 1],
                                            ALU.is_equal, ALU.mult).then_inc(s["onehot_ready"], 1)
                dve.wait_ge(s["picked_done"], 1)
                nc.vector.tensor_copy(picked[:], bank[2][:, 0:DIM]).then_inc(s["picked_copied"], 1)
                dve.wait_ge(s["picked_turned"], 1)
                nc.vector.tensor_copy(picked_t[:], bank[3][:, 0:DIM].rearrange("p (k q) -> p k q", q=P)).then_inc(s["picked_t_ready"], 1)
                for t in range(NT):
                    kept = nc.vector.scalar_tensor_tensor(x[:, t, :], xn[:, t, :], keep_scale[:, t:t + 1], x[:, t, :],
                                                          ALU.mult, ALU.add)
                link(kept)
                for c in range(0, NCH, 2):
                    dve.wait_ge(s["onehot_turned"], c + 1)
                    nc.vector.tensor_copy(onehot_t[:, TPC * c:TPC * (c + 1), :],
                                          bank[4 + c][:].rearrange("p (t q) -> p t q", q=P)).then_inc(s["onehot_t_dve"], 1)
                dve.wait_ge(s["block_done"], 1)
                dve.wait_ge(s["ffn_loaded"], 64)
                nc.vector.tensor_tensor(block_out[:], bank[2][:, 0:DIM], b2[:], ALU.add).then_inc(s["block_ready"], 1)
                for t in range(NT):
                    dve.wait_ge(s["scattered"], t // 2 + 1)
                    half = bank[(t // 2) % 2 * 4][:, (t % 2) * DIM:(t % 2 + 1) * DIM]
                    nc.vector.scalar_tensor_tensor(x[:, t, :], half, take_scale[:, t:t + 1], x[:, t, :],
                                                   ALU.mult, ALU.add).then_inc(s["added"], 1)
                dve.wait_ge(s["added"], NT)

            @block.scalar
            def _(act):
                norm.scalar(act)
                act.wait_ge(s["weights_loaded"], 32)
                for c in range(NCH):
                    act.wait_ge(s["weight_bank"], c + 1)
                    nc.scalar.activation(weight_row[:, c * CH:(c + 1) * CH], bank[c][:], ACT.Identity,
                                         bias=b_r[:, 0:1]).then_inc(s["row_ready"], 1)
                act.wait_ge(s["ffn_loaded"], 64)
                for h in range(2):
                    act.wait_ge(s["hidden_done"], h + 1)
                    for i in range(TPC):
                        f = TPC * h + i
                        nc.scalar.activation(hidden[:, f, :], bank[h][:, i * P:(i + 1) * P], ACT.Gelu_apprx_tanh,
                                             bias=b1[:, f:f + 1]).then_inc(s["hidden_ready"], 1)
                for c in range(1, NCH, 2):
                    act.wait_ge(s["onehot_turned"], c + 1)
                    nc.scalar.activation(onehot_t[:, TPC * c:TPC * (c + 1), :],
                                         bank[4 + c][:].rearrange("p (t q) -> p t q", q=P), ACT.Copy).then_inc(s["onehot_t_act"], 1)

            @block.tensor
            def _(pe):
                norm.tensor(pe)
                pe.wait_ge(s["wide_ready"], 1)
                for c in range(NCH):
                    norm.turn.wait_chunk(pe, c)
                    for k in range(ND):
                        last = nc.tensor.matmul(bank[c][:], w_r_wide[:, k, :], xn_t[:, k, c * CH:(c + 1) * CH],
                                                start=(k == 0), stop=(k == ND - 1))
                    last.then_inc(s["weight_bank"], 1)
                for c in range(NCH):
                    pe.wait_ge(s["row_ready"], c + 1)
                    for i in range(TPC):
                        last = nc.tensor.transpose(bank[4 + c][:, i * P:(i + 1) * P],
                                                   weight_row[:, c * CH + i * P:c * CH + (i + 1) * P], core.ident)
                    last.then_inc(s["weight_turned"], 1)
                pe.wait_ge(s["chosen_ready"], 1)
                nc.tensor.matmul(bank[0][:, 0:NT], core.before, chosen[:], start=True, stop=True)
                nc.tensor.matmul(bank[1][:, 0:NT], core.ones, chosen[:], start=True, stop=True).then_inc(s["prefix_done"], 1)
                for t in range(NT):
                    pe.wait_ge(s["onehot_ready"], t + 1)
                    last = nc.tensor.matmul(bank[2][:, 0:DIM], onehot[:, t, :], xn[:, t, :], start=(t == 0), stop=(t == NT - 1))
                last.then_inc(s["picked_done"], 1)
                for c in range(NCH):
                    for i in range(TPC):
                        last = nc.tensor.transpose(bank[4 + c][:, i * P:(i + 1) * P], onehot[:, TPC * c + i, :], core.ident)
                    last.then_inc(s["onehot_turned"], 1)
                pe.wait_ge(s["picked_copied"], 1)
                for k in range(ND):
                    last = nc.tensor.transpose(bank[3][:, k * P:(k + 1) * P], picked[:, k * P:(k + 1) * P], core.ident)
                last.then_inc(s["picked_turned"], 1)
                pe.wait_ge(s["picked_t_ready"], 1)
                pe.wait_ge(s["ffn_loaded"], 64)
                for h in range(2):
                    for i in range(TPC):
                        f = TPC * h + i
                        for k in range(ND):
                            last = nc.tensor.matmul(bank[h][:, i * P:(i + 1) * P], w1[:, k, f * P:(f + 1) * P], picked_t[:, k, :],
                                                    start=(k == 0), stop=(k == ND - 1))
                    last.then_inc(s["hidden_done"], 1)
                for f in range(NF):
                    pe.wait_ge(s["hidden_ready"], f + 1)
                    last = nc.tensor.matmul(bank[2][:, 0:DIM], hidden[:, f, :], w2[:, f, :], start=(f == 0), stop=(f == NF - 1))
                last.then_inc(s["block_done"], 1)
                pe.wait_ge(s["block_ready"], 1)
                pe.wait_ge(s["onehot_t_dve"], 2)
                pe.wait_ge(s["onehot_t_act"], 2)
                for t in range(NT):
                    if t >= 4 and t % 2 == 0:
                        pe.wait_ge(s["added"], t - 2)
                    last = nc.tensor.matmul(bank[(t // 2) % 2 * 4][:, (t % 2) * DIM:(t % 2 + 1) * DIM], onehot_t[:, t, :], block_out[:],
                                            start=True, stop=True)
                    if t % 2:
                        last.then_inc(s["scattered"], 1)
    core.end_step()


def mixed_ffn_stage(core, tag, out=None):
    nc, x, inp = core.nc, core.x, core.inp
    with ExitStack() as ctx:
        first = not core.mixed_ready
        core.mixed_ready = True
        factors = core.sb(f"{tag}_factors", [P, RANK, ND, DIM], F32, ctx) if first else None
        xn = core.sb(f"{tag}_xn", [P, NT, DIM], F32, ctx)
        xn_t = core.sb(f"{tag}_xn_t", [P, ND, TOKENS], F32, ctx)
        bank = [ctx.enter_context(nc.psum_tensor(f"{tag}_bank{i}", [P, CH], F32)) for i in range(8)]
        norm = Norm(core, ctx, tag, xn, xn_t, bank[:4])
        mixed_done, added, stored = (core.sem(f"{tag}_{n}") for n in ("mixed_done", "added", "stored"))
        factors_loaded, bias_loaded, summed = (core.sem(f"{tag}_{n}") for n in ("factors_loaded", "bias_loaded", "summed"))
        with nc.Block() as block:
            @block.gpsimd
            def _(pool):
                if first:
                    for r in range(1, RANK):
                        pool.wait_ge(factors_loaded, 16 * RANK)
                        earlier = factors[:, 0] if r == 1 else core.mixed[:]
                        if r > 1:
                            pool.wait_ge(summed, r - 1)
                        nc.gpsimd.tensor_tensor(core.mixed[:], earlier, factors[:, r], ALU.add).then_inc(summed, 1)

            @block.vector
            def _(dve):
                norm.vector(dve, Link(core, dve, f"{tag}_dve_link"))
                if first:
                    dve.wait_ge(bias_loaded, 16)
                    nc.vector.tensor_scalar(core.half_bias[:], core.half_bias[:], 0.5, None, ALU.mult).then_inc(bias_loaded, 1)
                    dve.wait_ge(bias_loaded, 17)
                dve.wait_ge(norm.xn_ready, NT)
                bias = core.half_bias[:].unsqueeze(1).broadcast_to([P, NT // 2, DIM])
                link = Link(core, dve, f"{tag}_biased")
                for h in range(2):
                    tiles = x[:, h * NT // 2:(h + 1) * NT // 2, :]
                    last = nc.vector.tensor_tensor(tiles, tiles, bias, ALU.add)
                link(last)
                for b in range(NT // 2):
                    dve.wait_ge(mixed_done, b + 1)
                    pair = x[:, 2 * b:2 * b + 2, :]
                    nc.vector.scalar_tensor_tensor(pair, bank[4 + b % 4][:].rearrange("p (t d) -> p t d", d=DIM),
                                                   0.5 / float(np.sqrt(RANK)), pair, ALU.mult, ALU.add).then_inc(added, 1)
                dve.wait_ge(added, NT // 2)

            @block.scalar
            def _(act):
                norm.scalar(act)

            @block.tensor
            def _(pe):
                norm.tensor(pe)
                if first:
                    pe.wait_ge(summed, RANK - 1)
                for b in range(NT // 2):
                    norm.turn.wait_chunk(pe, 2 * b // TPC)
                    if b >= 4:
                        pe.wait_ge(added, b - 3)
                    for i in range(2):
                        t = 2 * b + i
                        for k in range(ND):
                            last = nc.tensor.matmul(bank[4 + b % 4][:, i * DIM:(i + 1) * DIM], xn_t[:, k, t * P:(t + 1) * P],
                                                    core.mixed[:, k, :], start=(k == 0), stop=(k == ND - 1))
                    last.then_inc(mixed_done, 1)

            @block.sync
            def _(sp):
                if first:
                    for r in range(RANK):
                        sp.dma_start(factors[:, r], inp["L1_ffn_factors"][r].rearrange("(k p) e -> p k e", p=P)).then_inc(factors_loaded, 16)
                    sp.dma_start(core.half_bias[:], inp["L1_ffn_bias"].partition_broadcast(P)).then_inc(bias_loaded, 16)
                if out is not None:
                    rows = out[0].rearrange("(t p) d -> p t d", p=P)
                    for b in range(0, NT // 2, 2):
                        sp.wait_ge(added, b + 2)
                        sp.dma_start(rows[:, 2 * b:2 * b + 4, :], x[:, 2 * b:2 * b + 4, :]).then_inc(stored, 16)
                    sp.wait_ge(stored, 16 * (NT // 4))
    core.end_step()


def wait(engine, sem, value):
    if not isinstance(value, int) or value > 0:
        engine.wait_ge(sem, value)


def latent_attention_stage(core):
    with ExitStack() as ctx:
        def sb(name, shape, dt=F32):
            return core.sb(f"lat_{name}", shape, dt, ctx)
        qa_t = sb("qa_t", [P, 2, TOKENS])
        key_hi, key_lo = sb("key_hi", [P, TOKENS], F32R), sb("key_lo", [P, TOKENS], F32R)
        latent = sb("latent", [P, NT, P])
        latent_projections(core, qa_t, key_hi, key_lo, latent)
        latent_heads(core, qa_t, key_hi, key_lo, latent)


def latent_projections(core, qa_t, key_hi, key_lo, latent):
    nc, inp = core.nc, core.inp
    W = QL + KL + DR
    with ExitStack() as ctx:
        def sb(name, shape, dt=F32):
            return core.sb(f"latp_{name}", shape, dt, ctx)
        xn, xn_t = sb("xn", [P, NT, DIM]), sb("xn_t", [P, ND, TOKENS])
        w_down = sb("w_down", [P, ND, W])
        q_ln, kv_ln = sb("q_ln", [P, QL]), sb("kv_ln", [P, KL])
        rope = sb("rope", [P, 2, NT, DR // 2])
        down = sb("down", [P, NT, W])
        squares = sb("squares", [P, 2, QL])
        sums, mean_sq, root, rstd, scratch = (sb(n, [P, NT, 2]) for n in ("sums", "mean_sq", "root", "rstd", "scratch"))
        part = [sb(f"part{i}", [P, NT, DR // 2]) for i in range(4)]
        bank = [ctx.enter_context(nc.psum_tensor(f"latp_bank{i}", [P, CH], F32)) for i in range(8)]
        norm = Norm(core, ctx, "latn", xn, xn_t, bank[:4])
        names = ("loaded down_done down_copied squared mean_ready root_ready q_scaled latent_ready key_turned"
                 " key_hi_done key_lo_done q_turned q_turned_2 q_copied q_copied_2").split()
        s = {n: core.sem(f"latp_{n}") for n in names}
        with nc.Block() as block:
            @block.sync
            def _(sp):
                sp.dma_start(w_down[:, :, 0:QL], inp["L0_attn_w_q_a"].rearrange("(k p) e -> p k e", p=P)).then_inc(s["loaded"], 16)
                sp.dma_start(w_down[:, :, QL:W], inp["L0_attn_w_kv_a"].rearrange("(k p) e -> p k e", p=P)).then_inc(s["loaded"], 16)
                sp.dma_start(q_ln[:], inp["L0_attn_q_a_ln"].partition_broadcast(P)).then_inc(s["loaded"], 16)
                sp.dma_start(kv_ln[:], inp["L0_attn_kv_a_ln"].partition_broadcast(P)).then_inc(s["loaded"], 16)
                sp.dma_start(rope[:], inp["c_rope0_token"]).then_inc(s["loaded"], 16)

            @block.vector
            def _(dve):
                link = Link(core, dve, "latp_link")
                nc.vector.memset(qa_t[64:P, 1, :], 0.0)
                norm.vector(dve, link)
                for t in range(NT):
                    dve.wait_ge(s["down_done"], t + 1)
                    nc.vector.tensor_copy(down[:, t, :], bank[4 + t % 4][:, 0:W]).then_inc(s["down_copied"], 1)
                dve.wait_ge(s["loaded"], 80)
                dve.wait_ge(s["down_copied"], NT)
                even, odd = down[:, :, QL + KL:W:2], down[:, :, QL + KL + 1:W:2]
                cos, sin = rope[:, 0], rope[:, 1]
                for out, a, b in zip(part, (even, odd, odd, even), (cos, sin, cos, sin)):
                    last = nc.vector.tensor_tensor(out[:], a, b, ALU.mult)
                link(last)
                half = DR // 2
                nc.vector.tensor_tensor(latent[:, :, KL:KL + half], part[0][:], part[1][:], ALU.subtract)
                nc.vector.tensor_tensor(latent[:, :, KL + half:P], part[2][:], part[3][:], ALU.add)
                dve.wait_ge(s["squared"], 2 * NT)
                for i, width in enumerate((QL, KL)):
                    mean = nc.vector.tensor_scalar(mean_sq[:, :, i], sums[:, :, i], 1.0 / width, RMS_EPS, ALU.mult, ALU.add)
                mean.then_inc(s["mean_ready"], 1)
                dve.wait_ge(s["root_ready"], 1)
                reciprocal_of_root(nc, link, rstd[:], root[:], mean_sq[:], scratch[:])
                for t in range(NT):
                    nc.vector.scalar_tensor_tensor(latent[:, t, 0:KL], down[:, t, QL:QL + KL], rstd[:, t, 1:2], kv_ln[:],
                                                   ALU.mult, ALU.mult).then_inc(s["latent_ready"], 1)
                for t in range(NT):
                    nc.vector.scalar_tensor_tensor(down[:, t, 0:QL], down[:, t, 0:QL], rstd[:, t, 0:1], q_ln[:],
                                                   ALU.mult, ALU.mult).then_inc(s["q_scaled"], 1)
                for c in range(NCH):
                    dve.wait_ge(s["key_hi_done"], c + 1)
                    cols = slice(c * CH, (c + 1) * CH)
                    nc.vector.tensor_tensor(key_lo[:, cols], bank[c][:], key_hi[:, cols].bitcast(F32),
                                            ALU.subtract).then_inc(s["key_lo_done"], 1)
                for c in range(NCH):
                    dve.wait_ge(s["q_turned_2"], c + 1)
                    nc.vector.tensor_copy(qa_t[0:QL - P, 1, c * CH:(c + 1) * CH], bank[c][0:QL - P, :]).then_inc(s["q_copied_2"], 1)
                dve.wait_ge(s["q_copied_2"], NCH)

            @block.scalar
            def _(act):
                norm.scalar(act)
                for t in range(NT):
                    act.wait_ge(s["down_copied"], t + 1)
                    if t >= 1:
                        act.wait_ge(s["squared"], 2 * t)
                    nc.scalar.activation(squares[:, 0, 0:QL], down[:, t, 0:QL], ACT.Square,
                                         accum_out=sums[:, t, 0:1]).then_inc(s["squared"], 1)
                    nc.scalar.activation(squares[:, 1, 0:KL], down[:, t, QL:QL + KL], ACT.Square,
                                         accum_out=sums[:, t, 1:2]).then_inc(s["squared"], 1)
                act.wait_ge(s["mean_ready"], 1)
                nc.scalar.activation(root[:], mean_sq[:], ACT.Sqrt).then_inc(s["root_ready"], 1)
                for c in range(NCH):
                    act.wait_ge(s["key_turned"], c + 1)
                    nc.scalar.activation(key_hi[:, c * CH:(c + 1) * CH], bank[c][:], ACT.Copy).then_inc(s["key_hi_done"], 1)
                for c in range(NCH):
                    act.wait_ge(s["q_turned"], c + 1)
                    nc.scalar.activation(qa_t[:, 0, c * CH:(c + 1) * CH], bank[4 + c][:], ACT.Copy).then_inc(s["q_copied"], 1)
                act.wait_ge(s["q_copied"], NCH)

            @block.tensor
            def _(pe):
                norm.tensor(pe)
                pe.wait_ge(s["loaded"], 80)
                for t in range(NT):
                    norm.turn.wait_chunk(pe, t // TPC)
                    if t >= 4:
                        pe.wait_ge(s["down_copied"], t - 3)
                    for k in range(ND):
                        last = nc.tensor.matmul(bank[4 + t % 4][:, 0:W], xn_t[:, k, t * P:(t + 1) * P], w_down[:, k, :],
                                                start=(k == 0), stop=(k == ND - 1))
                    last.then_inc(s["down_done"], 1)
                for c in range(NCH):
                    pe.wait_ge(s["latent_ready"], TPC * (c + 1))
                    for i in range(TPC):
                        last = nc.tensor.transpose(bank[c][:, i * P:(i + 1) * P], latent[:, TPC * c + i, :], core.ident)
                    last.then_inc(s["key_turned"], 1)
                pe.wait_ge(s["down_copied"], NT)
                for c in range(NCH):
                    pe.wait_ge(s["q_scaled"], TPC * (c + 1))
                    for i in range(TPC):
                        last = nc.tensor.transpose(bank[4 + c][:, i * P:(i + 1) * P], down[:, TPC * c + i, 0:P], core.ident)
                    last.then_inc(s["q_turned"], 1)
                for c in range(NCH):
                    pe.wait_ge(s["key_lo_done"], c + 1)
                    for i in range(TPC):
                        last = nc.tensor.transpose(bank[c][0:QL - P, i * P:(i + 1) * P], down[:, TPC * c + i, P:QL], core.ident)
                    last.then_inc(s["q_turned_2"], 1)
    core.end_step()


def key_tiles(j):
    return TPC * (j + 1)


STEPS_BEFORE = [sum(key_tiles(i) for i in range(j)) for j in range(NCH)]


def latent_schedule(first, last):
    events, side_uses = [], 0

    def numbered(kind, *rest):
        nonlocal side_uses
        side_uses += 1
        return (kind, *rest, side_uses - 1)

    for j in range(NCH):
        steps = key_tiles(j)
        slots = [[] for _ in range(steps)]
        main = []
        if not (last and j == NCH - 1):
            nj = (j + 1) % NCH
            for h in range(2):
                main += [("maxima", j + 1, h, i, kc) for i in range(TPC) for kc in range(nj + 1)]
                main += [("shift", j + 1, h)]
        for n, event in enumerate(main):
            slots[n * steps // len(main)].append(event)
        side = []
        if not (first and j == 0):
            side += [("sums", j - 1)] + [("project", j - 1, i) for i in range(TPC)]
        if j == 0:
            side += [("fold_out",)]
        if not (last and j >= 2):
            side += [(kind, j + 2, h) for h in range(2) for kind in ("query", "split")]
        if j == 1 and not last:
            side += [("turn_q_weights",), ("turn_kv_weights",), ("fold_query",)]
        for n, event in enumerate(side):
            slots[2 + n * (steps - 2) // len(side)].append(event)
        if main:
            slots[-1] += [("spread", j + 1, 0), ("spread", j + 1, 1)]
        for kt in range(steps):
            events.append(("scores", j, kt))
            events += slots[kt][:len(slots[kt]) // 2] if kt % 2 else slots[kt]
            if kt % 2:
                if kt > 1:
                    events.append(("values", j, kt // 2 - 1))
                elif not (first and j == 0):
                    events += [("values", j - 1, key_tiles((j - 1) % NCH) // 2 - 1), ("drain", j - 1)]
                events += slots[kt][len(slots[kt]) // 2:]
    on_side = ("fold_out", "query", "turn_q_weights", "turn_kv_weights", "fold_query", "spread")
    return [numbered(*e) if e[0] in on_side else e for e in events]


LATENT_PROLOGUE = ([("turn_q_weights", 0), ("turn_kv_weights", 1), ("fold_query", 2)]
                   + [e for n in range(2) for h in range(2) for e in [("query", n, h, 3 + 2 * n + h), ("split", n, h)]]
                   + [e for h in range(2) for e in [("maxima", 0, h, i, 0) for i in range(TPC)] + [("shift", 0, h)]]
                   + [("spread", 0, 0, 7), ("spread", 0, 1, 8)])
PROLOGUE_SIDE = 9
LATENT_EPILOGUE = ([("values", -1, key_tiles(NCH - 1) // 2 - 1), ("drain", -1), ("sums", -1)]
                   + [("project", -1, i) for i in range(TPC)])


def latent_heads(core, qa_t, key_hi, key_lo, latent):
    nc, inp, x = core.nc, core.inp, core.x
    w_qb = inp["L0_attn_w_q_b"]
    w_kvb = inp["L0_attn_w_kv_b"]
    w_out = inp["L0_attn_w_out"]
    QW, KVW = 2 * DQ, 2 * (DN + DV)
    with ExitStack() as ctx:
        def sb(name, shape, dt=F32):
            return core.sb(f"lath_{name}", shape, dt, ctx)
        rope = sb("rope", [P, 2, TOKENS])
        ones_r, minus_ident = sb("ones_r", [P, P], F32R), sb("minus_ident", [P, P])
        zeros32 = sb("zeros32", [P, 32])
        raw_q, raw_kv, raw_out = sb("raw_q", [P, 2, QW]), sb("raw_kv", [P, KVW]), sb("raw_out", [P, 2, DIM])
        q_w_t, kv_w_t = sb("q_w_t", [P, 2, QL]), sb("kv_w_t", [P, 2, 2, KL])
        w_query = sb("w_query", [P, 2, 2, P])
        w_value = sb("w_value", [P, DIM])
        turn_a, turn_b = sb("turn_a", [P, CH]), sb("turn_b", [P, CH])
        query = sb("query", [P, CH])
        query_hi, query_lo = sb("query_hi", [P, NCH, 2, CH], F32R), sb("query_lo", [P, NCH, 2, CH], F32R)
        maxima = sb("maxima", [P, 2, TPC, NCH])
        row_max = sb("row_max", [P, 2, TPC])
        shift_diag = sb("shift_diag", [P, 2, TPC, P], F32R)
        shift = sb("shift", [P, 2, 2, CH])
        shifted = sb("shifted", [P, 4, CH])
        probs = sb("probs", [P, 8, CH])
        out_t = sb("out_t", [P, 2, CH])
        sums_t = sb("sums_t", [P, CH])
        total, inverse = sb("total", [P, TPC, 2]), sb("inverse", [P, TPC, 2])
        score_bank = [ctx.enter_context(nc.psum_tensor(f"lath_score{i}", [P, CH], F32)) for i in range(2)]
        max_bank = [ctx.enter_context(nc.psum_tensor(f"lath_max{i}", [P, CH], F32)) for i in range(2)]
        out_bank = ctx.enter_context(nc.psum_tensor("lath_out", [P, CH], F32))
        sum_bank = ctx.enter_context(nc.psum_tensor("lath_sum", [P, CH], F32))
        end_bank = ctx.enter_context(nc.psum_tensor("lath_end", [P, CH], F32))
        side_bank = ctx.enter_context(nc.psum_tensor("lath_side", [P, CH], F32))
        names = ("tables_loaded q_kv_loaded out_loaded vector_constants"
                 " scores_done shift_added exp_done values_done"
                 " maxima_done maxima_taken row_max_done diag_ready side_done side_free"
                 " cosine_done sine_done query_whole query_hi_done query_lo_done"
                 " rotation_weights_ready query_weights_ready"
                 " drained end_done end_free inverse_ready first_added").split()
        s = {n: core.sem(f"lath_{n}") for n in names}
        schedules = {"first": latent_schedule(True, False), "middle": latent_schedule(False, False),
                     "last": latent_schedule(False, True)}

        def pairs(engine, run):
            run(LATENT_PROLOGUE, 0, prologue=True)
            run(schedules["first"], 0)
            with engine.Fori(1, PAIRS - 1) as pair:
                run(schedules["middle"], pair)
            run(schedules["last"], PAIRS - 1)
            run(LATENT_EPILOGUE, PAIRS)

        def chunk(pair, j):
            return pair * NCH + j

        def score_unit(pair, j, kt, h):
            return pair * (2 * KT_PER_PAIR) + 2 * (KT_PER_PAIR * (j // NCH) + STEPS_BEFORE[j % NCH] + kt) + h

        def values_unit(pair, j, m):
            return pair * (KT_PER_PAIR // 2) + (KT_PER_PAIR * (j // NCH) + STEPS_BEFORE[j % NCH]) // 2 + m

        def maxima_unit(pair, j, h, i, kc):
            nj = j % NCH
            return (pair * (2 * KT_PER_PAIR) + 2 * (KT_PER_PAIR * (j // NCH) + STEPS_BEFORE[nj])
                    + h * key_tiles(nj) + i * (nj + 1) + kc)

        def side_use(pair, local, prologue):
            return local if prologue else pair * (NCH * 5) + PROLOGUE_SIDE + local

        with nc.Block() as block:
            @block.sync
            def _(sp):
                sp.dma_start(rope[64:P], inp["c_rope0_feature"][64:P]).then_inc(s["tables_loaded"], 16)
                sp.dma_start(raw_q[:, 0, :], w_qb[0:P, 0:QW]).then_inc(s["q_kv_loaded"], 16)
                sp.dma_start(raw_q[0:QL - P, 1, :], w_qb[P:QL, 0:QW]).then_inc(s["q_kv_loaded"], 16)
                sp.dma_start(raw_kv[0:KL, :], w_kvb[:, 0:KVW]).then_inc(s["q_kv_loaded"], 16)
                sp.dma_start(raw_out[:], w_out[0:2 * DV, :].rearrange("(h p) e -> p h e", p=P)).then_inc(s["out_loaded"], 16)
                with sp.Fori(1, PAIRS) as pair:
                    sp.wait_ge(s["query_weights_ready"], pair)
                    sp.wait_ge(s["rotation_weights_ready"], pair)
                    sp.dma_start(raw_q[:, 0, :], w_qb[0:P, bass.ds(pair * QW, QW)]).then_inc(s["q_kv_loaded"], 16)
                    sp.dma_start(raw_q[0:QL - P, 1, :], w_qb[P:QL, bass.ds(pair * QW, QW)]).then_inc(s["q_kv_loaded"], 16)
                    sp.dma_start(raw_kv[0:KL, :], w_kvb[:, bass.ds(pair * KVW, KVW)]).then_inc(s["q_kv_loaded"], 16)
                    sp.wait_ge(s["side_free"], side_use(pair - 1, 0, False) + 1)
                    sp.dma_start(raw_out[:], w_out[bass.ds(pair * 2 * DV, 2 * DV), :].rearrange("(h p) e -> p h e", p=P))\
                      .then_inc(s["out_loaded"], 16)

            @block.tensor
            def _(pe):
                def run(events, pair, prologue=False):
                    for kind, *a in events:
                        if kind == "scores":
                            j, kt = a
                            for h in range(2):
                                u = score_unit(pair, j, kt, h)
                                if h == 0 and kt == 0:
                                    wait(pe, s["query_lo_done"], 2 * chunk(pair, j) + 2)
                                wait(pe, s["shift_added"], u - 1)
                                diagonal = kt - TPC * j
                                q0 = max(diagonal, 0) * P
                                out = score_bank[h][:, q0:CH]
                                hi, lo = query_hi[:, j, h, q0:CH], query_lo[:, j, h, q0:CH]
                                keys = slice(kt * P, (kt + 1) * P)
                                nc.tensor.matmul(out, key_hi[:, keys], hi, start=True, stop=False)
                                nc.tensor.matmul(out, key_hi[:, keys], lo, start=False, stop=False)
                                if diagonal >= 0:
                                    nc.tensor.matmul(score_bank[h][:, q0:q0 + P], core.ident_b, core.mask_kq, start=False, stop=False)
                                nc.tensor.matmul(out, key_lo[:, keys], hi, start=False, stop=True).then_inc(s["scores_done"], 1)
                        elif kind == "values":
                            j, m = a
                            nj = j % NCH
                            steps = key_tiles(nj)
                            wait(pe, s["exp_done"], score_unit(pair, j, 2 * m + 1, 1) + 1)
                            if m == 0:
                                wait(pe, s["drained"], 3 * chunk(pair, j))
                            for kt in (2 * m, 2 * m + 1):
                                q0 = max(kt - TPC * nj, 0) * P
                                for h in range(2):
                                    nc.tensor.matmul(out_bank[64 * h:64 * h + 64, q0:CH], latent[:, kt, 0:KL],
                                                     probs[:, 2 * (kt % 4) + h, q0:CH], start=(kt == 0), stop=(kt == steps - 1))
                            for kt in (2 * m, 2 * m + 1):
                                q0 = max(kt - TPC * nj, 0) * P
                                for h in range(2):
                                    row = 32 * (2 * (kt % 2) + h)
                                    if nj == 0 and kt == 1:
                                        nc.tensor.matmul(sum_bank[row:row + 32, :], zeros32[:], probs[:, h, :], start=True, stop=False)
                                    last = nc.tensor.matmul(sum_bank[row:row + 32, q0:CH], core.ones[:, 0:32],
                                                            probs[:, 2 * (kt % 4) + h, q0:CH],
                                                            start=(kt == 0 or (kt == 1 and nj > 0)), stop=(kt >= steps - 2))
                            last.then_inc(s["values_done"], 1)
                        elif kind == "maxima":
                            j, h, i, kc = a
                            nj = j % NCH
                            v = maxima_unit(pair, j, h, i, kc)
                            if i == 0 and kc == 0:
                                wait(pe, s["query_hi_done"], 2 * chunk(pair, j) + h + 1)
                            wait(pe, s["maxima_taken"], v - 1)
                            width = (i + 1) * P if kc == nj else CH
                            bank = max_bank[(i * (nj + 1) + kc) % 2]
                            mm = nc.tensor.matmul(bank[:, 0:width], query_hi[:, nj, h, i * P:(i + 1) * P],
                                                  key_hi[:, kc * CH:kc * CH + width], start=True, stop=(kc < nj))
                            if kc == nj:
                                mm = nc.tensor.matmul(bank[:, width - P:width], core.ident_b, core.mask_qk, start=False, stop=True)
                            mm.then_inc(s["maxima_done"], 1)
                        elif kind == "spread":
                            j, h, local = a
                            d = 2 * chunk(pair, j) + h
                            wait(pe, s["side_free"], side_use(pair, local, prologue))
                            wait(pe, s["diag_ready"], d + 1)
                            nc.tensor.matmul(side_bank[:], ones_r[:], shift_diag[:, h].rearrange("p t q -> p (t q)"),
                                             start=True, stop=True).then_inc(s["side_done"], 1)
                        elif kind == "query":
                            n, h, local = a
                            if h == 0:
                                wait(pe, s["rotation_weights_ready"], pair + n // NCH + 1)
                            wait(pe, s["side_free"], side_use(pair, local, prologue))
                            cols = slice((n % NCH) * CH, (n % NCH + 1) * CH)
                            for k in range(2):
                                mm = nc.tensor.matmul(side_bank[:], w_query[:, k, h, :], qa_t[:, k, cols], start=(k == 0), stop=(k == 1))
                            mm.then_inc(s["side_done"], 1)
                        elif kind == "turn_q_weights":
                            wait(pe, s["q_kv_loaded"], 48 * (pair + 1) if prologue else 48 * (pair + 2))
                            wait(pe, s["side_free"], side_use(pair, a[0], prologue))
                            for h in range(2):
                                nc.tensor.transpose(side_bank[:, h * QL:h * QL + P], raw_q[:, 0, h * DQ:h * DQ + DN], core.ident)
                                mm = nc.tensor.transpose(side_bank[:, h * QL + P:(h + 1) * QL], raw_q[0:QL - P, 1, h * DQ:h * DQ + DN],
                                                         core.ident[0:QL - P, 0:QL - P])
                            mm.then_inc(s["side_done"], 1)
                        elif kind == "turn_kv_weights":
                            wait(pe, s["side_free"], side_use(pair, a[0], prologue))
                            for n in range(4):
                                mm = nc.tensor.transpose(side_bank[:, n * P:(n + 1) * P], raw_kv[:, n * P:(n + 1) * P], core.ident)
                            mm.then_inc(s["side_done"], 1)
                        elif kind == "fold_query":
                            wait(pe, s["side_free"], side_use(pair, a[0], prologue))
                            for h in range(2):
                                nc.tensor.matmul(side_bank[:, h * P:h * P + KL], q_w_t[:, h, 0:P], kv_w_t[:, h, 0, :], start=True, stop=True)
                                mm = nc.tensor.matmul(side_bank[0:QL - P, h * P + KL:(h + 1) * P], q_w_t[:, h, P:QL], kv_w_t[:, h, 0, :],
                                                      start=True, stop=True)
                            mm.then_inc(s["side_done"], 1)
                        elif kind == "fold_out":
                            wait(pe, s["out_loaded"], 16 * (pair + 1))
                            wait(pe, s["side_free"], side_use(pair, a[0], prologue))
                            for h in range(2):
                                mm = nc.tensor.matmul(side_bank[64 * h:64 * h + 64, 0:DIM], kv_w_t[:, h, 1, :], raw_out[:, h, :],
                                                      start=True, stop=True)
                            mm.then_inc(s["side_done"], 1)
                        elif kind == "sums":
                            n = chunk(pair, a[0])
                            wait(pe, s["drained"], 3 * n + 3)
                            wait(pe, s["end_free"], n * (TPC + 1))
                            for i in range(TPC):
                                mm = nc.tensor.transpose(end_bank[:, i * P:(i + 1) * P], sums_t[:, i * P:(i + 1) * P], core.ident)
                            mm.then_inc(s["end_done"], 1)
                        elif kind == "project":
                            j, i = a
                            n = chunk(pair, j)
                            wait(pe, s["end_free"], n * (TPC + 1) + 1 + i)
                            for h in range(2):
                                mm = nc.tensor.matmul(end_bank[:, h * DIM:(h + 1) * DIM], out_t[:, h, i * P:(i + 1) * P], w_value[:],
                                                      start=True, stop=True)
                            mm.then_inc(s["end_done"], 1)

                pe.wait_ge(s["vector_constants"], 1)
                pairs(pe, run)

            @block.scalar
            def _(act):
                def copy_side(use, out, columns, rows=P):
                    wait(act, s["side_done"], use + 1)
                    return nc.scalar.activation(out, side_bank[0:rows, columns], ACT.Copy)

                def run(events, pair, prologue=False):
                    for kind, *a in events:
                        if kind == "scores":
                            j, kt = a
                            for h in range(2):
                                u = score_unit(pair, j, kt, h)
                                q0 = max(kt - TPC * j, 0) * P
                                wait(act, s["shift_added"], u + 1)
                                wait(act, s["values_done"], values_unit(pair, j, kt // 2) - 1)
                                nc.scalar.activation(probs[:, 2 * (kt % 4) + h, q0:CH], shifted[:, 2 * (kt % 2) + h, q0:CH], ACT.Exp,
                                                     scale=SCALE0).then_inc(s["exp_done"], 1)
                        elif kind == "drain":
                            n = chunk(pair, a[0])
                            wait(act, s["values_done"], values_unit(pair, a[0], key_tiles(a[0] % NCH) // 2 - 1) + 1)
                            for h in range(2):
                                rows = slice(64 * h, 64 * h + 64)
                                nc.scalar.activation(out_t[rows, h, :], out_bank[rows, :], ACT.Copy).then_inc(s["drained"], 1)
                            nc.scalar.activation(sums_t[:], sum_bank[:], ACT.Copy).then_inc(s["drained"], 1)
                        elif kind == "spread":
                            j, h, local = a
                            copy_side(side_use(pair, local, prologue), shift[:, j % 2, h, :], slice(0, CH)).then_inc(s["side_free"], 1)
                        elif kind == "query":
                            n, h, local = a
                            r = 2 * chunk(pair, n) + h
                            wait(act, s["query_lo_done"], r)
                            copy_side(side_use(pair, local, prologue), query[:], slice(0, CH)).then_inc(s["side_free"], 1)
                        elif kind == "split":
                            n, h = a
                            r = 2 * chunk(pair, n) + h
                            wait(act, s["query_whole"], r + 1)
                            nc.scalar.activation(query_hi[:, n % NCH, h, :], query[:], ACT.Copy).then_inc(s["query_hi_done"], 1)
                        elif kind == "turn_q_weights":
                            copy_side(side_use(pair, a[0], prologue), q_w_t[:].rearrange("p h r -> p (h r)"), slice(0, 2 * QL)).then_inc(s["side_free"], 1)
                            if prologue:
                                act.wait_ge(s["vector_constants"], 1)
                            for k, rows in enumerate((P, QL - P)):
                                rotated = raw_q[0:rows, k, :].rearrange("p (h c) -> p h c", h=2)[:, :, DN:DQ]
                                for odd in range(2):
                                    last = nc.scalar.activation(w_query[0:rows, k, :, KL + odd * DR // 2:KL + (odd + 1) * DR // 2],
                                                                rotated[:, :, odd:DR:2], ACT.Copy)
                            last.then_inc(s["rotation_weights_ready"], 1)
                        elif kind == "turn_kv_weights":
                            wait(act, s["side_done"], side_use(pair, a[0], prologue) + 1)
                            nc.scalar.activation(kv_w_t[:].rearrange("p h s r -> p (h s) r"),
                                                 side_bank[:].rearrange("p (n r) -> p n r", r=P)[:, :, 0:KL], ACT.Copy).then_inc(s["side_free"], 1)
                        elif kind == "fold_query":
                            use = side_use(pair, a[0], prologue)
                            wait(act, s["side_done"], use + 1)
                            folded = side_bank[:, 0:2 * P].rearrange("p (h k r) -> p h k r", h=2, k=2)
                            nc.scalar.activation(w_query[:, 0, :, 0:KL], folded[:, :, 0, :], ACT.Copy).then_inc(s["query_weights_ready"], 1)
                            nc.scalar.activation(w_query[0:QL - P, 1, :, 0:KL], folded[0:QL - P, :, 1, :], ACT.Copy).then_inc(s["side_free"], 1)
                        elif kind == "fold_out":
                            use = side_use(pair, a[0], prologue)
                            copy_side(use, w_value[:], slice(0, DIM)).then_inc(s["side_free"], 1)

                pairs(act, run)

            @block.gpsimd
            def _(pool):
                def run(events, pair, prologue=False):
                    for kind, *a in events:
                        if kind == "query":
                            n, h, local = a
                            r = 2 * chunk(pair, n) + h
                            if prologue and r == 0:
                                pool.wait_ge(s["tables_loaded"], 16)
                            pool.wait_ge(s["side_free"], side_use(pair, local, prologue) + 1)
                            nc.gpsimd.tensor_tensor(turn_a[64:P], query[64:P], rope[64:P, 0, (n % NCH) * CH:(n % NCH + 1) * CH],
                                                    ALU.mult).then_inc(s["cosine_done"], 1)
                            pool.wait_ge(s["cosine_done"], r + 1)
                            pool.wait_ge(s["sine_done"], 2 * r + 2)
                            nc.gpsimd.tensor_tensor(query[64:P], turn_a[64:P], turn_b[64:P], ALU.add).then_inc(s["query_whole"], 1)
                        elif kind == "split":
                            n, h = a
                            r = 2 * chunk(pair, n) + h
                            pool.wait_ge(s["query_hi_done"], r + 1)
                            nc.gpsimd.tensor_tensor(query_lo[:, n % NCH, h, :], query[:], query_hi[:, n % NCH, h, :].bitcast(F32),
                                                    ALU.subtract).then_inc(s["query_lo_done"], 1)

                pairs(pool, run)

            @block.vector
            def _(dve):
                def run(events, pair, prologue=False):
                    for kind, *a in events:
                        if kind == "scores":
                            j, kt = a
                            for h in range(2):
                                u = score_unit(pair, j, kt, h)
                                q0 = max(kt - TPC * j, 0) * P
                                wait(dve, s["scores_done"], u + 1)
                                wait(dve, s["exp_done"], u - 3)
                                nc.vector.tensor_tensor(shifted[:, 2 * (kt % 2) + h, q0:CH], score_bank[h][:, q0:CH],
                                                        shift[:, j % 2, h, q0:CH], ALU.add).then_inc(s["shift_added"], 1)
                        elif kind == "maxima":
                            j, h, i, kc = a
                            nj = j % NCH
                            v = maxima_unit(pair, j, h, i, kc)
                            width = (i + 1) * P if kc == nj else CH
                            wait(dve, s["maxima_done"], v + 1)
                            nc.vector.reduce_max(maxima[:, h, i, kc:kc + 1], max_bank[(i * (nj + 1) + kc) % 2][:, 0:width],
                                                 AX.X).then_inc(s["maxima_taken"], 1)
                        elif kind == "shift":
                            j, h = a
                            nj = j % NCH
                            d = 2 * chunk(pair, j) + h
                            wait(dve, s["maxima_taken"], maxima_unit(pair, j, h, TPC - 1, nj) + 1)
                            nc.vector.reduce_max(row_max[:, h, :], maxima[:, h, :, 0:nj + 1], AX.X).then_inc(s["row_max_done"], 1)
                            wait(dve, s["row_max_done"], d + 1)
                            nc.vector.tensor_tensor(shift_diag[:, h], minus_ident[:].unsqueeze(1).broadcast_to([P, TPC, P]),
                                                    row_max[:, h, :].unsqueeze(2).broadcast_to([P, TPC, P]), ALU.mult).then_inc(s["diag_ready"], 1)
                        elif kind == "spread":
                            wait(dve, s["side_free"], side_use(pair, a[2], prologue) + 1)
                        elif kind == "query":
                            n, h, local = a
                            r = 2 * chunk(pair, n) + h
                            cols = slice((n % NCH) * CH, (n % NCH + 1) * CH)
                            if prologue and r == 0:
                                dve.wait_ge(s["tables_loaded"], 16)
                            wait(dve, s["side_free"], side_use(pair, local, prologue) + 1)
                            wait(dve, s["query_whole"], r)
                            nc.vector.tensor_tensor(turn_b[64:96], query[96:P], rope[96:P, 1, cols], ALU.mult).then_inc(s["sine_done"], 1)
                            nc.vector.tensor_tensor(turn_b[96:P], query[64:96], rope[64:96, 1, cols], ALU.mult).then_inc(s["sine_done"], 1)
                        elif kind == "sums":
                            n = chunk(pair, a[0])
                            wait(dve, s["end_done"], n * (TPC + 1) + 1)
                            four = end_bank[:].rearrange("p (t r h c) -> p t h r c", t=TPC, r=2, h=2)[:, :, :, :, 0]
                            nc.vector.reduce_sum(total[:], four, AX.X).then_inc(s["end_free"], 1)
                            wait(dve, s["end_free"], n * (TPC + 1) + 1)
                            nc.vector.reciprocal(inverse[:], total[:]).then_inc(s["inverse_ready"], 1)
                            wait(dve, s["inverse_ready"], n + 1)
                        elif kind == "project":
                            j, i = a
                            n = chunk(pair, j)
                            t = TPC * (j % NCH) + i
                            wait(dve, s["end_done"], n * (TPC + 1) + i + 2)
                            nc.vector.scalar_tensor_tensor(x[:, t, :], end_bank[:, 0:DIM], inverse[:, i, 0:1], x[:, t, :],
                                                           ALU.mult, ALU.add).then_inc(s["first_added"], 1)
                            wait(dve, s["first_added"], n * TPC + i + 1)
                            nc.vector.scalar_tensor_tensor(x[:, t, :], end_bank[:, DIM:2 * DIM], inverse[:, i, 1:2], x[:, t, :],
                                                           ALU.mult, ALU.add).then_inc(s["end_free"], 1)

                nc.vector.tensor_scalar(minus_ident[:], core.ident, -1.0, None, ALU.mult)
                nc.vector.memset(w_query[64:P, 1], 0.0)
                nc.vector.memset(zeros32[:], 0.0)
                nc.vector.memset(raw_kv[KL:P, :], 0.0)
                nc.vector.memset(out_t[64:P, 0, :], 0.0)
                nc.vector.memset(out_t[0:64, 1, :], 0.0)
                nc.vector.tensor_copy(ones_r[:], core.ones).then_inc(s["vector_constants"], 1)
                dve.wait_ge(s["vector_constants"], 1)
                pairs(dve, run)
    core.end_step()


def attention_stage(core):
    with ExitStack() as ctx:
        def sb(name, shape, dt=F32):
            return core.sb(f"att_{name}", shape, dt, ctx)
        qk = sb("qk", [P, NT, 2 * DIM])
        v = sb("v", [P, NT, DIM])
        w_o_t = sb("w_o_t", [P, ND, DIM])
        attended = sb("attended", [P, NT, DIM])
        attention_projections(core, qk, v, w_o_t)
        attention_heads(core, qk, v, attended)
        attention_output(core, attended, w_o_t)


def attention_projections(core, qk, v, w_o_t):
    nc, inp = core.nc, core.inp
    with ExitStack() as ctx:
        def sb(name, shape, dt=F32):
            return core.sb(f"attp_{name}", shape, dt, ctx)
        xn, xn_t = sb("xn", [P, NT, DIM]), sb("xn_t", [P, ND, TOKENS])
        raw = sb("raw", [P, 4, ND, DIM])
        w_qkv_t = sb("w_qkv_t", [P, ND, 3 * DIM])
        rope = sb("rope", [P, 2, NT, D1])
        by_cos, by_sin = sb("by_cos", [P, 2, 2 * DIM]), sb("by_sin", [P, 2, 2 * DIM])
        bank = [ctx.enter_context(nc.psum_tensor(f"attp_bank{i}", [P, CH], F32)) for i in range(8)]
        norm = Norm(core, ctx, "attn", xn, xn_t, bank[:4])
        names = "weights_loaded rope_loaded weights_turned weights_copied qk_done v_done products_done rotated v_copied".split()
        s = {n: core.sem(f"attp_{n}") for n in names}
        with nc.Block() as block:
            @block.sync
            def _(sp):
                for m, name in enumerate(("Wq", "Wk", "Wv", "Wo")):
                    sp.dma_start(raw[:, m], inp[f"L1_attn_{name}"].rearrange("(k p) d -> p k d", p=P)).then_inc(s["weights_loaded"], 16)
                sp.dma_start(rope[:], inp["c_rope1_token"]).then_inc(s["rope_loaded"], 16)

            @block.vector
            def _(dve):
                norm.vector(dve, Link(core, dve, "attp_link"))
                dve.wait_ge(s["rope_loaded"], 16)
                heads = 2 * H1
                for t in range(NT):
                    dve.wait_ge(s["qk_done"], t + 1)
                    if t >= 2:
                        dve.wait_ge(s["rotated"], 2 * (t - 1))
                    scores = bank[4 + t % 2][:].rearrange("p (h c) -> p h c", c=D1)
                    for out, table in ((by_cos, 0), (by_sin, 1)):
                        last = nc.vector.tensor_tensor(out[:, t % 2, :].rearrange("p (h c) -> p h c", c=D1), scores,
                                                       rope[:, table, t, :].unsqueeze(1).broadcast_to([P, heads, D1]), ALU.mult)
                    last.then_inc(s["products_done"], 1)

            @block.gpsimd
            def _(pool):
                for t in range(NT):
                    pool.wait_ge(s["products_done"], t + 1)
                    a, b = by_cos[:, t % 2, :], by_sin[:, t % 2, :]
                    nc.gpsimd.tensor_tensor(qk[:, t, 0:2 * DIM:2], a[:, 0:2 * DIM:2], b[:, 1:2 * DIM:2], ALU.subtract).then_inc(s["rotated"], 1)
                    nc.gpsimd.tensor_tensor(qk[:, t, 1:2 * DIM:2], b[:, 0:2 * DIM:2], a[:, 1:2 * DIM:2], ALU.add).then_inc(s["rotated"], 1)
                pool.wait_ge(s["rotated"], 2 * NT)

            @block.scalar
            def _(act):
                for m in range(4):
                    act.wait_ge(s["weights_turned"], m + 1)
                    to = w_o_t[:] if m == 3 else w_qkv_t[:, :, m * DIM:(m + 1) * DIM]
                    nc.scalar.activation(to, bank[4 + m][:].rearrange("p (k e) -> p k e", k=ND), ACT.Copy).then_inc(s["weights_copied"], 1)
                norm.scalar(act)
                for t in range(NT):
                    act.wait_ge(s["v_done"], t + 1)
                    nc.scalar.activation(v[:, t, :], bank[6 + t % 2][:, 0:DIM], ACT.Copy).then_inc(s["v_copied"], 1)
                act.wait_ge(s["v_copied"], NT)

            @block.tensor
            def _(pe):
                pe.wait_ge(s["weights_loaded"], 64)
                for m in range(4):
                    for k in range(ND):
                        for e in range(ND):
                            last = nc.tensor.transpose(bank[4 + m][:, k * DIM + e * P:k * DIM + (e + 1) * P],
                                                       raw[:, m, e, k * P:(k + 1) * P], core.ident)
                    last.then_inc(s["weights_turned"], 1)
                norm.tensor(pe)
                pe.wait_ge(s["weights_copied"], 4)
                for t in range(NT):
                    norm.turn.wait_chunk(pe, t // TPC)
                    if t >= 2:
                        pe.wait_ge(s["products_done"], t - 1)
                    for k in range(ND):
                        last = nc.tensor.matmul(bank[4 + t % 2][:], xn_t[:, k, t * P:(t + 1) * P], w_qkv_t[:, k, 0:2 * DIM],
                                                start=(k == 0), stop=(k == ND - 1))
                    last.then_inc(s["qk_done"], 1)
                    if t >= 2:
                        pe.wait_ge(s["v_copied"], t - 1)
                    for k in range(ND):
                        last = nc.tensor.matmul(bank[6 + t % 2][:, 0:DIM], xn_t[:, k, t * P:(t + 1) * P], w_qkv_t[:, k, 2 * DIM:3 * DIM],
                                                start=(k == 0), stop=(k == ND - 1))
                    last.then_inc(s["v_done"], 1)
    core.end_step()


def attention_schedule():
    events = [("expand",)]
    events += [("turn_keys", pair, c) for c in range(NCH) for pair in range(2)]
    events += [("turn_queries", pair, c) for c in range(NCH) for pair in range(2)]

    def maxima(j):
        return [("maxima", j, h, i, kc) for h in range(GROUP) for i in range(TPC) for kc in range(j + 1)]

    events += maxima(0) + [("shift", 0), ("turn_shifted", 0, 0), ("turn_shifted", 0, 1)]
    for j in range(NCH):
        steps = key_tiles(j)
        main = maxima(j + 1) + [("shift", j + 1)] if j + 1 < NCH else []
        for kt in range(steps):
            events += [("scores", j, kt, 0), ("scores", j, kt, 1)]
            part = main[kt * len(main) // steps:(kt + 1) * len(main) // steps]
            events += part[:len(part) // 2]
            if kt:
                events.append(("values", j, kt - 1))
            elif j:
                events += [("values", j - 1, key_tiles(j - 1) - 1), ("drain", j - 1)]
            events += part[len(part) // 2:]
            if j and kt == 1:
                events.append(("finish", j - 1))
        if main:
            events += [("turn_shifted", j + 1, 0), ("turn_shifted", j + 1, 1)]
    events += [("values", NCH - 1, key_tiles(NCH - 1) - 1), ("drain", NCH - 1), ("finish", NCH - 1)]
    uses, out = 0, []
    for e in events:
        if e[0].startswith("turn") or e[0] == "finish":
            out.append((*e, uses))
            uses += 1
        else:
            out.append(e)
    return out, uses


def attention_heads(core, qk, v, attended):
    nc = core.nc
    schedule, SIDE_USES = attention_schedule()
    MAXIMA_BEFORE = [GROUP * n for n in STEPS_BEFORE]
    with ExitStack() as ctx:
        def sb(name, shape, dt=F32):
            return core.sb(f"atth_{name}", shape, dt, ctx)
        q_slot, k_slot = sb("q_slot", [P, NT, GROUP, SLOT]), sb("k_slot", [P, NT, GROUP, SLOT])
        v_one = sb("v_one", [P, NT, GROUP, 32])
        key = sb("key", [P, GROUP, TOKENS], F32R)
        query = sb("query", [P, 2, TOKENS], F32R)
        query_shifted = sb("query_shifted", [P, 2, 2, CH], F32R)
        maxima = sb("maxima", [P, TPC, GROUP, NCH])
        row_max = sb("row_max", [P, TPC, GROUP])
        probs = sb("probs", [P, 4, 2, CH])
        out_t = sb("out_t", [P, CH])
        inverse = sb("inverse", [P, TPC, GROUP])
        score_bank = [ctx.enter_context(nc.psum_tensor(f"atth_score{i}", [P, 2, CH], F32)) for i in range(2)]
        max_bank = [ctx.enter_context(nc.psum_tensor(f"atth_max{i}", [P, CH], F32)) for i in range(2)]
        out_bank = ctx.enter_context(nc.psum_tensor("atth_out", [P, CH], F32))
        side_bank = ctx.enter_context(nc.psum_tensor("atth_side", [P, CH], F32))
        names = ("constants_ready q_high_done q_expanded k_high_done k_copied k_expanded side_done side_free maxima_done maxima_taken row_max_done"
                 " shift_high_done shift_ready scores_done exp_done values_done drained inverse_ready").split()
        s = {n: core.sem(f"atth_{n}") for n in names}

        def groups(engine, run):
            run(0)
            with engine.Fori(1, NG) as group:
                run(group)

        def side_use(group, local):
            return group * SIDE_USES + local

        def score_unit(group, j, kt, pair):
            return group * (2 * KT_PER_PAIR) + 2 * (STEPS_BEFORE[j] + kt) + pair

        def values_unit(group, j, kt):
            return group * KT_PER_PAIR + STEPS_BEFORE[j] + kt

        def maxima_unit(group, j, h, i, kc):
            return group * (GROUP * KT_PER_PAIR) + MAXIMA_BEFORE[j] + (h * TPC + i) * (j + 1) + kc

        def group_columns(group, base=0):
            return bass.ds(group * GROUP * D1 + base, GROUP * D1) if not isinstance(group, int) else \
                slice(group * GROUP * D1 + base, (group + 1) * GROUP * D1 + base)

        def slots(tensor, part):
            return tensor[:, :, :, part * D1:(part + 1) * D1]

        with nc.Block() as block:
            @block.vector
            def _(dve):
                nc.vector.memset(q_slot[:], 0.0)
                nc.vector.memset(k_slot[:, :, :, 3 * D1:SLOT], 0.0)
                nc.vector.memset(v_one[:, :, :, D1:32], 0.0).then_inc(s["constants_ready"], 1)
                for h in range(GROUP):
                    rows = slice(64, P) if h % 2 == 0 else slice(0, 64)
                    nc.vector.memset(key[rows, h, :].bitcast(F32), 0.0)
                dve.wait_ge(s["constants_ready"], 1)
                nc.vector.memset(k_slot[:, :, :, 3 * D1:3 * D1 + 2], 1.0)
                nc.vector.memset(v_one[:, :, :, D1:D1 + 1], 1.0).then_inc(s["constants_ready"], 1)
                dve.wait_ge(s["constants_ready"], 2)

                def run(group):
                    for kind, *a in schedule:
                        if kind == "expand":
                            source = qk[:, :, group_columns(group)].rearrange("p t (h c) -> p t h c", c=D1)
                            nc.vector.tensor_copy(slots(q_slot, 0).bitcast(F32R), source).then_inc(s["q_high_done"], 1)
                            nc.vector.memset(q_slot[:, :, :, 3 * D1:3 * D1 + 2], 0.0)
                            wait(dve, s["q_high_done"], group + 1)
                            nc.vector.tensor_copy(slots(q_slot, 1), slots(q_slot, 0))
                            nc.vector.tensor_tensor(slots(q_slot, 2), source, slots(q_slot, 0), ALU.subtract).then_inc(s["q_expanded"], 1)
                        elif kind == "turn_keys":
                            pair, c, local = a
                            wait(dve, s["side_done"], side_use(group, local) + 1)
                            nc.vector.tensor_copy(key[64:P, 2 * pair + 1, c * CH:(c + 1) * CH], side_bank[64:P, :]).then_inc(s["side_free"], 1)
                        elif kind == "maxima":
                            j, h, i, kc = a
                            m = maxima_unit(group, j, h, i, kc)
                            width = (i + 1) * P if kc == j else CH
                            wait(dve, s["maxima_done"], m + 1)
                            nc.vector.reduce_max(maxima[:, i, h, kc:kc + 1], max_bank[(i * (j + 1) + kc) % 2][:, 0:width], AX.X)\
                              .then_inc(s["maxima_taken"], 1)
                        elif kind == "shift":
                            j, = a
                            n = group * NCH + j
                            wait(dve, s["maxima_taken"], maxima_unit(group, j, GROUP - 1, TPC - 1, j) + 1)
                            nc.vector.reduce_max(row_max[:], maxima[:, :, :, 0:j + 1], AX.X).then_inc(s["row_max_done"], 1)
                            wait(dve, s["row_max_done"], n + 1)
                            high = q_slot[:, TPC * j:TPC * (j + 1), :, 3 * D1]
                            low = q_slot[:, TPC * j:TPC * (j + 1), :, 3 * D1 + 1]
                            nc.vector.tensor_scalar(high.bitcast(F32R), row_max[:], -1.0, None, ALU.mult).then_inc(s["shift_high_done"], 1)
                            wait(dve, s["shift_high_done"], n + 1)
                            nc.vector.scalar_tensor_tensor(low, row_max[:], -1.0, high, ALU.mult, ALU.subtract).then_inc(s["shift_ready"], 1)
                        elif kind == "finish":
                            j, local = a
                            use = side_use(group, local)
                            wait(dve, s["side_done"], use + 1)
                            ended = side_bank[:].rearrange("p (t h c) -> p t h c", t=TPC, h=GROUP)
                            nc.vector.reciprocal(inverse[:], ended[:, :, :, D1]).then_inc(s["inverse_ready"], 1)
                            wait(dve, s["inverse_ready"], group * NCH + j + 1)
                            to = attended[:, TPC * j:TPC * (j + 1), group_columns(group)].rearrange("p t (h c) -> p t h c", c=D1)
                            nc.vector.tensor_tensor(to, ended[:, :, :, 0:D1], inverse[:].unsqueeze(3).broadcast_to([P, TPC, GROUP, D1]),
                                                    ALU.mult).then_inc(s["side_free"], 2)
                groups(dve, run)

            @block.gpsimd
            def _(pool):
                def run(group):
                    source = qk[:, :, group_columns(group, DIM)].rearrange("p t (h c) -> p t h c", c=D1)
                    wait(pool, s["k_high_done"], group + 1)
                    nc.gpsimd.tensor_tensor(slots(k_slot, 1), source, slots(k_slot, 0), ALU.subtract).then_inc(s["k_expanded"], 1)
                pool.wait_ge(s["constants_ready"], 2)
                groups(pool, run)

            @block.scalar
            def _(act):
                act.wait_ge(s["constants_ready"], 2)

                def run(group):
                    for kind, *a in schedule:
                        if kind == "expand":
                            wait(act, s["side_done"], group * SIDE_USES)
                            wait(act, s["values_done"], group * KT_PER_PAIR)
                            source = qk[:, :, group_columns(group, DIM)].rearrange("p t (h c) -> p t h c", c=D1)
                            nc.scalar.activation(slots(k_slot, 0).bitcast(F32R), source, ACT.Copy).then_inc(s["k_high_done"], 1)
                            nc.scalar.activation(v_one[:, :, :, 0:D1], v[:, :, group_columns(group)].rearrange("p t (h c) -> p t h c", c=D1), ACT.Copy)
                            wait(act, s["k_high_done"], group + 1)
                            nc.scalar.activation(slots(k_slot, 2), slots(k_slot, 0), ACT.Copy).then_inc(s["k_copied"], 1)
                        elif kind == "turn_keys":
                            pair, c, local = a
                            wait(act, s["side_done"], side_use(group, local) + 1)
                            nc.scalar.activation(key[0:64, 2 * pair, c * CH:(c + 1) * CH], side_bank[0:64, :], ACT.Copy).then_inc(s["side_free"], 1)
                        elif kind == "turn_queries":
                            pair, c, local = a
                            wait(act, s["side_done"], side_use(group, local) + 1)
                            nc.scalar.activation(query[:, pair, c * CH:(c + 1) * CH], side_bank[:], ACT.Copy).then_inc(s["side_free"], 2)
                        elif kind == "turn_shifted":
                            j, pair, local = a
                            wait(act, s["side_done"], side_use(group, local) + 1)
                            nc.scalar.activation(query_shifted[:, j % 2, pair, :], side_bank[:], ACT.Copy).then_inc(s["side_free"], 2)
                        elif kind == "scores":
                            j, kt, pair = a
                            q0 = max(kt - TPC * j, 0) * P
                            wait(act, s["scores_done"], score_unit(group, j, kt, pair) + 1)
                            wait(act, s["values_done"], values_unit(group, j, kt) - 1)
                            nc.scalar.activation(probs[:, 2 * (kt % 2) + pair, :, q0:CH], score_bank[pair][:, :, q0:CH], ACT.Exp,
                                                 scale=SCALE1).then_inc(s["exp_done"], 1)
                        elif kind == "drain":
                            j, = a
                            wait(act, s["values_done"], values_unit(group, j, key_tiles(j) - 1) + 1)
                            nc.scalar.activation(out_t[:], out_bank[:], ACT.Copy).then_inc(s["drained"], 1)
                groups(act, run)

            @block.tensor
            def _(pe):
                def run(group):
                    for kind, *a in schedule:
                        if kind.startswith("turn") or kind == "finish":
                            wait(pe, s["side_free"], side_use(group, a[-1]) * 2)
                        if kind == "turn_keys":
                            pair, c, local = a
                            wait(pe, s["k_expanded"], group + 1)
                            wait(pe, s["k_copied"], group + 1)
                            for i in range(TPC):
                                last = nc.tensor.transpose(side_bank[:, i * P:(i + 1) * P], k_slot[:, TPC * c + i, 2 * pair:2 * pair + 2, :]
                                                           .rearrange("p h c -> p (h c)"), core.ident)
                            last.then_inc(s["side_done"], 1)
                        elif kind == "turn_queries":
                            pair, c, local = a
                            wait(pe, s["q_expanded"], group + 1)
                            for i in range(TPC):
                                last = nc.tensor.transpose(side_bank[:, i * P:(i + 1) * P], q_slot[:, TPC * c + i, 2 * pair:2 * pair + 2, :]
                                                           .rearrange("p h c -> p (h c)"), core.ident)
                            last.then_inc(s["side_done"], 1)
                        elif kind == "turn_shifted":
                            j, pair, local = a
                            wait(pe, s["shift_ready"], group * NCH + j + 1)
                            for i in range(TPC):
                                last = nc.tensor.transpose(side_bank[:, i * P:(i + 1) * P], q_slot[:, TPC * j + i, 2 * pair:2 * pair + 2, :]
                                                           .rearrange("p h c -> p (h c)"), core.ident)
                            last.then_inc(s["side_done"], 1)
                        elif kind == "maxima":
                            j, h, i, kc = a
                            m = maxima_unit(group, j, h, i, kc)
                            if j == 0 and h == 0 and i == 0:
                                wait(pe, s["side_free"], 2 * (side_use(group, 0) + 4 * NCH))
                            wait(pe, s["maxima_taken"], m - 1)
                            width = (i + 1) * P if kc == j else CH
                            t = TPC * j + i
                            bank = max_bank[(i * (j + 1) + kc) % 2]
                            mm = nc.tensor.matmul(bank[:, 0:width], query[:, h // 2, t * P:(t + 1) * P], key[:, h, kc * CH:kc * CH + width],
                                                  start=True, stop=(kc < j))
                            if kc == j:
                                mm = nc.tensor.matmul(bank[:, width - P:width], core.ident_b, core.mask_qk, start=False, stop=True)
                            mm.then_inc(s["maxima_done"], 1)
                        elif kind == "scores":
                            j, kt, pair = a
                            u = score_unit(group, j, kt, pair)
                            if kt == 0 and pair == 0:
                                wait(pe, s["side_free"], 2 * (side_use(group, shifted_use[j]) + 1))
                            wait(pe, s["exp_done"], u - 1)
                            diagonal = kt - TPC * j
                            q0 = max(diagonal, 0) * P
                            for n in range(2):
                                h = 2 * pair + n
                                mm = nc.tensor.matmul(score_bank[pair][:, n, q0:CH], key[:, h, kt * P:(kt + 1) * P],
                                                      query_shifted[:, j % 2, pair, q0:CH], start=True, stop=(diagonal < 0))
                                if diagonal >= 0:
                                    mm = nc.tensor.matmul(score_bank[pair][:, n, q0:q0 + P], core.ident_b, core.mask_kq, start=False, stop=True)
                            mm.then_inc(s["scores_done"], 1)
                        elif kind == "values":
                            j, kt = a
                            q0 = max(kt - TPC * j, 0) * P
                            wait(pe, s["exp_done"], score_unit(group, j, kt, 1) + 1)
                            if kt == 0:
                                wait(pe, s["drained"], group * NCH + j)
                            for h in range(GROUP):
                                mm = nc.tensor.matmul(out_bank[32 * h:32 * h + 32, q0:CH], v_one[:, kt, h, :],
                                                      probs[:, 2 * (kt % 2) + h // 2, h % 2, q0:CH],
                                                      start=(kt == 0), stop=(kt == key_tiles(j) - 1))
                            mm.then_inc(s["values_done"], 1)
                        elif kind == "finish":
                            j, local = a
                            wait(pe, s["drained"], group * NCH + j + 1)
                            for i in range(TPC):
                                last = nc.tensor.transpose(side_bank[:, i * P:(i + 1) * P], out_t[:, i * P:(i + 1) * P], core.ident)
                            last.then_inc(s["side_done"], 1)

                shifted_use = {e[1]: e[3] for e in schedule if e[0] == "turn_shifted"}
                pe.wait_ge(s["constants_ready"], 2)
                groups(pe, run)
    core.end_step()


def attention_output(core, attended, w_o_t):
    nc, x = core.nc, core.x
    with ExitStack() as ctx:
        attended_t = core.sb("atto_attended_t", [P, ND, TOKENS], F32, ctx)
        bank = [ctx.enter_context(nc.psum_tensor(f"atto_bank{i}", [P, CH], F32)) for i in range(8)]
        turn = Turn(core, "atto", attended, attended_t, bank[:4], source_complete=True)
        projected, added = core.sem("atto_projected"), core.sem("atto_added")
        with nc.Block() as block:
            @block.vector
            def _(dve):
                turn.vector(dve)
                for b in range(NT // 2):
                    dve.wait_ge(projected, b + 1)
                    pair = x[:, 2 * b:2 * b + 2, :]
                    nc.vector.tensor_tensor(pair, bank[4 + b % 4][:].rearrange("p (t d) -> p t d", d=DIM), pair, ALU.add).then_inc(added, 1)
                dve.wait_ge(added, NT // 2)

            @block.scalar
            def _(act):
                turn.scalar(act)

            @block.tensor
            def _(pe):
                turn.tensor(pe)
                for b in range(NT // 2):
                    turn.wait_chunk(pe, 2 * b // TPC)
                    if b >= 4:
                        pe.wait_ge(added, b - 3)
                    for i in range(2):
                        t = 2 * b + i
                        for k in range(ND):
                            last = nc.tensor.matmul(bank[4 + b % 4][:, i * DIM:(i + 1) * DIM], attended_t[:, k, t * P:(t + 1) * P],
                                                    w_o_t[:, k, :], start=(k == 0), stop=(k == ND - 1))
                    last.then_inc(projected, 1)
    core.end_step()


def macaron_program(nc, inp, out):
    with ExitStack() as ctx:
        core = Core(nc, ctx, inp)
        load_stage(core)
        routed_ffn_stage(core, "ffn_a")
        latent_attention_stage(core)
        routed_ffn_stage(core, "ffn_b")
        mixed_ffn_stage(core, "mix_a")
        attention_stage(core)
        mixed_ffn_stage(core, "mix_b", out)


_INS = ['L0_attn_x', 'L0_attn_w_q_a', 'L0_attn_q_a_ln', 'L0_attn_w_q_b', 'L0_attn_w_kv_a', 'L0_attn_kv_a_ln',
        'L0_attn_w_kv_b', 'L0_attn_w_out', 'L0_ffn_W_r', 'L0_ffn_b_r', 'L0_ffn_W1', 'L0_ffn_b1', 'L0_ffn_W2',
        'L0_ffn_b2', 'L1_attn_Wq', 'L1_attn_Wk', 'L1_attn_Wv', 'L1_attn_Wo', 'L1_ffn_factors', 'L1_ffn_bias']


def kernel(**inputs):
    import concourse.bacc as bacc
    from concourse.bass_utils import run_bass_kernel_spmd

    nc = bacc.Bacc("TRN2", target_bir_lowering=False, num_devices=1)
    arrays = {name: np.ascontiguousarray(inputs[name]) for name in _INS}
    arrays.update(shape_constants())
    aps = {name: nc.dram_tensor(f"in_{name}", a.shape, mybir.dt.from_np(a.dtype), kind="ExternalInput").ap()
           for name, a in arrays.items()}
    out = nc.dram_tensor("out", (1, TOKENS, DIM), F32, kind="ExternalOutput").ap()
    macaron_program(nc, aps, out)
    result = run_bass_kernel_spmd(nc, [{f"in_{name}": a for name, a in arrays.items()}], core_ids=[0])
    return result.results[0]["out"]
```

```python
import numpy as np
from contextlib import ExitStack

import concourse.bass as bass
from concourse import mybir

F32 = mybir.dt.float32
F32R = mybir.dt.float32r
BF16 = mybir.dt.bfloat16
ALU = mybir.AluOpType
ACT = mybir.ActivationFunctionType
AX = mybir.AxisListType

P = 128
TOKENS = 2048
DIM = 256
NT = TOKENS // P
ND = DIM // P
CH = 512
NCH = TOKENS // CH
TPC = CH // P

DFF = 1024
NF = DFF // P
CAPACITY = 64

H0 = 16
QL, KL = 192, 64
DN, DR, DV = 128, 64, 128
DQ = DN + DR
SCALE0 = 1.0 / float(np.sqrt(DQ))
RMS_EPS = 1e-6
PAIRS = H0 // 2
KT_PER_PAIR = sum(TPC * (j + 1) for j in range(NCH))

H1, D1 = 16, 16
SCALE1 = 1.0 / float(np.sqrt(DIM))
GROUP = 4
NG = H1 // GROUP
SLOT = 64

RANK = 8
LN_EPS = 1e-5
MASKED = -1e30


def shape_constants():
    eye = np.eye(P, dtype=np.float32)
    row = np.arange(P)
    before = (row[:, None] < row[None, :]).astype(np.float32)
    iota = np.broadcast_to(row.astype(np.float32), (P, P))
    square = np.concatenate([eye, before, iota, np.ones((P, P), np.float32)], axis=1)
    ahead = np.where(row[None, :] > row[:, None], MASKED, 0.0)
    masks = np.concatenate([eye, ahead, ahead.T], axis=1).astype(np.float32)
    t = np.arange(TOKENS, dtype=np.float32)
    f0 = np.outer(t, (1.0 / 10000.0 ** (np.arange(0, DR, 2, dtype=np.float32) / DR)).astype(np.float32)).astype(np.float32)
    cos0, sin0 = np.cos(f0), np.sin(f0)
    half0 = DR // 2
    col0 = np.zeros((P, 2, TOKENS), np.float32)
    col0[DR:DR + half0, 0], col0[DR + half0:, 0] = cos0.T, cos0.T
    col0[DR:DR + half0, 1], col0[DR + half0:, 1] = sin0.T, -sin0.T
    tok0 = np.stack([cos0, sin0], axis=1).reshape(NT, P, 2, half0).transpose(1, 2, 0, 3)
    half1 = D1 // 2
    f1 = np.outer(t, (1.0 / 10000.0 ** (np.arange(half1, dtype=np.float32) / half1)).astype(np.float32)).astype(np.float32)
    both = np.stack([np.repeat(np.cos(f1), 2, axis=1), np.repeat(np.sin(f1), 2, axis=1)], axis=1)
    tok1 = both.reshape(NT, P, 2, D1).transpose(1, 2, 0, 3)
    return {"c_square": np.ascontiguousarray(square), "c_masks": masks,
            "c_rope0_feature": col0, "c_rope0_token": np.ascontiguousarray(tok0),
            "c_rope1_token": np.ascontiguousarray(tok1)}


class Core:

    def __init__(self, nc, ctx, inp):
        self.nc, self.ctx, self.inp = nc, ctx, inp
        self.step_semaphores = []
        self.mixed_ready = False
        self.x = self.sb("x", [P, NT, DIM], F32)
        self.square = self.sb("square", [P, 4, P], F32)
        self.masks = self.sb("masks", [P, 3, P], BF16)
        self.mixed = self.sb("mixed", [P, ND, DIM], F32)
        self.half_bias = self.sb("half_bias", [P, DIM], F32)
        self.ident = self.square[:, 0, :]
        self.before = self.square[:, 1, :]
        self.iota = self.square[:, 2, :]
        self.ones = self.square[:, 3, :]
        self.ident_b = self.masks[:, 0, :]
        self.mask_qk = self.masks[:, 1, :]
        self.mask_kq = self.masks[:, 2, :]

    def sb(self, name, shape, dt, ctx=None):
        return (ctx or self.ctx).enter_context(self.nc.sbuf_tensor(name, shape, dt))

    def sem(self, name):
        s = self.nc.alloc_semaphore(name)
        self.step_semaphores.append(s)
        return s

    def end_step(self):
        self.nc.clear_and_free_semaphores(self.step_semaphores)
        self.nc.all_engine_barrier()
        self.step_semaphores = []


class Link:

    def __init__(self, core, engine, name):
        self.sem, self.engine, self.n = core.sem(name), engine, 0

    def __call__(self, instruction):
        instruction.then_inc(self.sem, 1)
        self.n += 1
        self.engine.wait_ge(self.sem, self.n)


def load_stage(core):
    nc, inp = core.nc, core.inp
    with ExitStack() as ctx:
        masks = core.sb("masks_whole", [P, 3, P], F32, ctx)
        x_loaded, square_loaded, masks_loaded = (core.sem(n) for n in ("x_loaded", "square_loaded", "masks_loaded"))
        masks_ready = core.sem("masks_ready")
        rows = inp["L0_attn_x"][0].rearrange("(t p) d -> p t d", p=P)
        with nc.Block() as block:
            @block.sync
            def _(sp):
                for c in range(0, NCH, 2):
                    sp.dma_start(core.x[:, TPC * c:TPC * (c + 1), :], rows[:, TPC * c:TPC * (c + 1), :]).then_inc(x_loaded, 16)
                sp.dma_start(core.square[:], inp["c_square"].rearrange("p (a b) -> p a b", b=P)).then_inc(square_loaded, 16)
                sp.wait_ge(x_loaded, 16 * NCH)
                sp.wait_ge(square_loaded, 16)

            @block.scalar
            def _(act):
                for c in range(1, NCH, 2):
                    act.dma_start(core.x[:, TPC * c:TPC * (c + 1), :], rows[:, TPC * c:TPC * (c + 1), :]).then_inc(x_loaded, 16)
                act.dma_start(masks[:], inp["c_masks"].rearrange("p (a b) -> p a b", b=P)).then_inc(masks_loaded, 16)

            @block.vector
            def _(dve):
                dve.wait_ge(masks_loaded, 16)
                nc.vector.tensor_copy(core.masks[:], masks[:]).then_inc(masks_ready, 1)
                dve.wait_ge(masks_ready, 1)
    core.end_step()


class Turn:

    def __init__(self, core, tag, source, target, banks, source_complete=False):
        self.core, self.source, self.target, self.banks = core, source, target, banks
        self.source_ready = None if source_complete else core.sem(f"{tag}_source_ready")
        self.turned = core.sem(f"{tag}_turned")
        self.evac_dve = core.sem(f"{tag}_evac_dve")
        self.evac_act = core.sem(f"{tag}_evac_act")

    def place(self, b):
        c, d = divmod(b, ND)
        return self.target[:, d, c * CH:(c + 1) * CH]

    def vector(self, dve):
        for b in range(0, 2 * NCH, 2):
            dve.wait_ge(self.turned, b + 1)
            self.core.nc.vector.tensor_copy(self.place(b), self.banks[b % len(self.banks)][:]).then_inc(self.evac_dve, 1)

    def scalar(self, act):
        for b in range(1, 2 * NCH, 2):
            act.wait_ge(self.turned, b + 1)
            self.core.nc.scalar.activation(self.place(b), self.banks[b % len(self.banks)][:], ACT.Copy).then_inc(self.evac_act, 1)

    def tensor(self, pe):
        nc, n = self.core.nc, len(self.banks)
        for b in range(2 * NCH):
            c, d = divmod(b, ND)
            if self.source_ready is not None:
                pe.wait_ge(self.source_ready, TPC * (c + 1))
            if b >= n:
                pe.wait_ge(self.evac_act if b % 2 else self.evac_dve, (b - n) // 2 + 1)
            for i in range(TPC):
                last = nc.tensor.transpose(self.banks[b % n][:, i * P:(i + 1) * P],
                                           self.source[:, TPC * c + i, d * P:(d + 1) * P], self.core.ident)
            last.then_inc(self.turned, 1)

    def wait_chunk(self, engine, c):
        engine.wait_ge(self.evac_dve, c + 1)
        engine.wait_ge(self.evac_act, c + 1)


class Norm:

    def __init__(self, core, ctx, tag, xn, xn_t, banks):
        self.core, self.xn = core, xn
        self.stats = core.sb(f"{tag}_stats", [P, NT, 6], F32, ctx)
        self.moments = core.sb(f"{tag}_moments", [P, NT, 2], F32, ctx)
        self.var = core.sb(f"{tag}_var", [P, NT], F32, ctx)
        self.root = core.sb(f"{tag}_root", [P, NT], F32, ctx)
        self.rstd = core.sb(f"{tag}_rstd", [P, NT], F32, ctx)
        self.scratch = core.sb(f"{tag}_scratch", [P, NT], F32, ctx)
        self.var_ready = core.sem(f"{tag}_var_ready")
        self.root_ready = core.sem(f"{tag}_root_ready")
        self.turn = Turn(core, tag, xn, xn_t, banks)
        self.xn_ready = self.turn.source_ready

    def vector(self, dve, link):
        nc, x = self.core.nc, self.core.x
        for t in range(NT):
            s = nc.vector.bn_stats(self.stats[:, t, :], x[:, t, :])
        link(s)
        for t in range(NT):
            s = nc.vector.bn_aggr(self.moments[:, t, :], self.stats[:, t, :])
        link(s)
        nc.vector.tensor_scalar(self.var[:], self.moments[:, :, 1], LN_EPS, None, ALU.add).then_inc(self.var_ready, 1)
        dve.wait_ge(self.root_ready, 1)
        reciprocal_of_root(nc, link, self.rstd[:], self.root[:], self.var[:], self.scratch[:])
        for t in range(NT):
            nc.vector.tensor_scalar(self.xn[:, t, :], x[:, t, :], self.moments[:, t, 0:1], self.rstd[:, t:t + 1],
                                    ALU.subtract, ALU.mult).then_inc(self.xn_ready, 1)
        self.turn.vector(dve)

    def scalar(self, act):
        act.wait_ge(self.var_ready, 1)
        self.core.nc.scalar.activation(self.root[:], self.var[:], ACT.Sqrt).then_inc(self.root_ready, 1)
        self.turn.scalar(act)

    def tensor(self, pe):
        self.turn.tensor(pe)


def reciprocal_of_root(nc, link, out, root, value, scratch):
    link(nc.vector.reciprocal(out, root))
    link(nc.vector.tensor_tensor(scratch, out, out, ALU.mult))
    link(nc.vector.tensor_tensor(scratch, scratch, value, ALU.mult))
    link(nc.vector.tensor_scalar(scratch, scratch, -0.5, 1.5, ALU.mult, ALU.add))
    link(nc.vector.tensor_tensor(out, out, scratch, ALU.mult))


def routed_ffn_stage(core, tag):
    nc, inp, x = core.nc, core.inp, core.x
    with ExitStack() as ctx:
        def sb(name, shape, dt=F32):
            return core.sb(f"{tag}_{name}", shape, dt, ctx)
        xn, xn_t = sb("xn", [P, NT, DIM]), sb("xn_t", [P, ND, TOKENS])
        w_r, w_r_wide = sb("w_r", [P, ND]), sb("w_r_wide", [P, ND, P])
        b_r = sb("b_r", [P, 1])
        w1, w2 = sb("w1", [P, ND, DFF]), sb("w2", [P, NF, DIM])
        b1, b2 = sb("b1", [P, NF]), sb("b2", [P, DIM])
        weight_row = sb("weight_row", [P, TOKENS])
        weight = sb("weight", [P, NT])
        not_below = sb("not_below", [P, 2, TOKENS], BF16)
        count = sb("count", [P, NT])
        chosen, keep_scale, take_scale = sb("chosen", [P, NT]), sb("keep_scale", [P, NT]), sb("take_scale", [P, NT])
        ranks = sb("ranks", [P, 3, NT])
        onehot, onehot_t = sb("onehot", [P, NT, P]), sb("onehot_t", [P, NT, P])
        picked, picked_t = sb("picked", [P, DIM]), sb("picked_t", [P, ND, P])
        hidden = sb("hidden", [P, NF, P])
        block_out = sb("block_out", [P, DIM])
        bank = [ctx.enter_context(nc.psum_tensor(f"{tag}_bank{i}", [P, CH], F32)) for i in range(8)]
        norm = Norm(core, ctx, tag, xn, xn_t, bank)
        names = ("weights_loaded ffn_loaded wide_ready weight_bank row_ready weight_turned counted chosen_ready"
                 " prefix_done onehot_ready picked_done picked_copied picked_turned picked_t_ready hidden_done"
                 " hidden_ready block_done block_ready onehot_turned onehot_t_act onehot_t_dve scattered added").split()
        s = {n: core.sem(f"{tag}_{n}") for n in names}

        with nc.Block() as block:
            @block.sync
            def _(sp):
                sp.dma_start(w_r[:], inp["L0_ffn_W_r"].rearrange("(k p) o -> p (k o)", p=P),
                             allow_slow_non_contiguous=True).then_inc(s["weights_loaded"], 16)
                sp.dma_start(b_r[:], inp["L0_ffn_b_r"].partition_broadcast(P)).then_inc(s["weights_loaded"], 16)
                sp.dma_start(w1[:], inp["L0_ffn_W1"].rearrange("(k p) f -> p k f", p=P)).then_inc(s["ffn_loaded"], 16)
                sp.dma_start(w2[:], inp["L0_ffn_W2"].rearrange("(k p) d -> p k d", p=P)).then_inc(s["ffn_loaded"], 16)
                sp.dma_start(b1[:], inp["L0_ffn_b1"].rearrange("(k p) -> p k", p=P),
                             allow_slow_non_contiguous=True).then_inc(s["ffn_loaded"], 16)
                sp.dma_start(b2[:], inp["L0_ffn_b2"].partition_broadcast(P)).then_inc(s["ffn_loaded"], 16)

            @block.vector
            def _(dve):
                link = Link(core, dve, f"{tag}_dve_link")
                dve.wait_ge(s["weights_loaded"], 32)
                nc.vector.tensor_copy(w_r_wide[:], w_r[:].unsqueeze(2).broadcast_to([P, ND, P])).then_inc(s["wide_ready"], 1)
                norm.vector(dve, link)
                for c in range(NCH):
                    dve.wait_ge(s["weight_turned"], c + 1)
                    w = nc.vector.tensor_copy(weight[:, TPC * c:TPC * (c + 1)],
                                              bank[4 + c][:].rearrange("p (t q) -> p t q", q=P)[:, :, 0])
                link(w)
                for t in range(NT):
                    if t >= 2:
                        dve.wait_ge(s["counted"], t - 1)
                    nc.vector.tensor_scalar(not_below[:, t % 2], weight_row[:], weight[:, t:t + 1], None,
                                            ALU.is_ge, ALU.add, accum_out=count[:, t:t + 1]).then_inc(s["counted"], 1)
                dve.wait_ge(s["counted"], NT)
                nc.vector.tensor_scalar(chosen[:], count[:], CAPACITY - 0.5, None, ALU.is_lt).then_inc(s["chosen_ready"], 1)
                dve.wait_ge(s["chosen_ready"], 1)
                nc.vector.tensor_scalar(keep_scale[:], chosen[:], -0.5, 0.5, ALU.mult, ALU.add)
                link(nc.vector.tensor_scalar(take_scale[:], weight[:], 0.5, None, ALU.mult))
                dve.wait_ge(s["prefix_done"], 1)
                link(nc.vector.memset(ranks[:, 0, 0:1], 0.0))
                link(nc.vector.tensor_copy(ranks[:, 0, 1:NT], bank[1][:, 0:NT - 1]))
                src = 0
                for step in (1, 2, 4, 8):
                    link(nc.vector.tensor_copy(ranks[:, 1 - src, 0:step], ranks[:, src, 0:step]))
                    link(nc.vector.tensor_tensor(ranks[:, 1 - src, step:NT], ranks[:, src, step:NT],
                                                 ranks[:, src, 0:NT - step], ALU.add))
                    src = 1 - src
                link(nc.vector.tensor_tensor(ranks[:, 2, :], bank[0][:, 0:NT], ranks[:, src, :], ALU.add))
                for t in range(NT):
                    nc.vector.tensor_scalar(onehot[:, t, :], core.iota, ranks[:, 2, t:t + 1], chosen[:, t:t + 1],
                                            ALU.is_equal, ALU.mult).then_inc(s["onehot_ready"], 1)
                dve.wait_ge(s["picked_done"], 1)
                nc.vector.tensor_copy(picked[:], bank[2][:, 0:DIM]).then_inc(s["picked_copied"], 1)
                dve.wait_ge(s["picked_turned"], 1)
                nc.vector.tensor_copy(picked_t[:], bank[3][:, 0:DIM].rearrange("p (k q) -> p k q", q=P)).then_inc(s["picked_t_ready"], 1)
                for t in range(NT):
                    kept = nc.vector.scalar_tensor_tensor(x[:, t, :], xn[:, t, :], keep_scale[:, t:t + 1], x[:, t, :],
                                                          ALU.mult, ALU.add)
                link(kept)
                for c in range(0, NCH, 2):
                    dve.wait_ge(s["onehot_turned"], c + 1)
                    nc.vector.tensor_copy(onehot_t[:, TPC * c:TPC * (c + 1), :],
                                          bank[4 + c][:].rearrange("p (t q) -> p t q", q=P)).then_inc(s["onehot_t_dve"], 1)
                dve.wait_ge(s["block_done"], 1)
                dve.wait_ge(s["ffn_loaded"], 64)
                nc.vector.tensor_tensor(block_out[:], bank[2][:, 0:DIM], b2[:], ALU.add).then_inc(s["block_ready"], 1)
                for t in range(NT):
                    dve.wait_ge(s["scattered"], t // 2 + 1)
                    half = bank[(t // 2) % 2 * 4][:, (t % 2) * DIM:(t % 2 + 1) * DIM]
                    nc.vector.scalar_tensor_tensor(x[:, t, :], half, take_scale[:, t:t + 1], x[:, t, :],
                                                   ALU.mult, ALU.add).then_inc(s["added"], 1)
                dve.wait_ge(s["added"], NT)

            @block.scalar
            def _(act):
                norm.scalar(act)
                act.wait_ge(s["weights_loaded"], 32)
                for c in range(NCH):
                    act.wait_ge(s["weight_bank"], c + 1)
                    nc.scalar.activation(weight_row[:, c * CH:(c + 1) * CH], bank[c][:], ACT.Identity,
                                         bias=b_r[:, 0:1]).then_inc(s["row_ready"], 1)
                act.wait_ge(s["ffn_loaded"], 64)
                for h in range(2):
                    act.wait_ge(s["hidden_done"], h + 1)
                    for i in range(TPC):
                        f = TPC * h + i
                        nc.scalar.activation(hidden[:, f, :], bank[h][:, i * P:(i + 1) * P], ACT.Gelu_apprx_tanh,
                                             bias=b1[:, f:f + 1]).then_inc(s["hidden_ready"], 1)
                for c in range(1, NCH, 2):
                    act.wait_ge(s["onehot_turned"], c + 1)
                    nc.scalar.activation(onehot_t[:, TPC * c:TPC * (c + 1), :],
                                         bank[4 + c][:].rearrange("p (t q) -> p t q", q=P), ACT.Copy).then_inc(s["onehot_t_act"], 1)

            @block.tensor
            def _(pe):
                norm.tensor(pe)
                pe.wait_ge(s["wide_ready"], 1)
                for c in range(NCH):
                    norm.turn.wait_chunk(pe, c)
                    for k in range(ND):
                        last = nc.tensor.matmul(bank[c][:], w_r_wide[:, k, :], xn_t[:, k, c * CH:(c + 1) * CH],
                                                start=(k == 0), stop=(k == ND - 1))
                    last.then_inc(s["weight_bank"], 1)
                for c in range(NCH):
                    pe.wait_ge(s["row_ready"], c + 1)
                    for i in range(TPC):
                        last = nc.tensor.transpose(bank[4 + c][:, i * P:(i + 1) * P],
                                                   weight_row[:, c * CH + i * P:c * CH + (i + 1) * P], core.ident)
                    last.then_inc(s["weight_turned"], 1)
                pe.wait_ge(s["chosen_ready"], 1)
                nc.tensor.matmul(bank[0][:, 0:NT], core.before, chosen[:], start=True, stop=True)
                nc.tensor.matmul(bank[1][:, 0:NT], core.ones, chosen[:], start=True, stop=True).then_inc(s["prefix_done"], 1)
                for t in range(NT):
                    pe.wait_ge(s["onehot_ready"], t + 1)
                    last = nc.tensor.matmul(bank[2][:, 0:DIM], onehot[:, t, :], xn[:, t, :], start=(t == 0), stop=(t == NT - 1))
                last.then_inc(s["picked_done"], 1)
                for c in range(NCH):
                    for i in range(TPC):
                        last = nc.tensor.transpose(bank[4 + c][:, i * P:(i + 1) * P], onehot[:, TPC * c + i, :], core.ident)
                    last.then_inc(s["onehot_turned"], 1)
                pe.wait_ge(s["picked_copied"], 1)
                for k in range(ND):
                    last = nc.tensor.transpose(bank[3][:, k * P:(k + 1) * P], picked[:, k * P:(k + 1) * P], core.ident)
                last.then_inc(s["picked_turned"], 1)
                pe.wait_ge(s["picked_t_ready"], 1)
                pe.wait_ge(s["ffn_loaded"], 64)
                for h in range(2):
                    for i in range(TPC):
                        f = TPC * h + i
                        for k in range(ND):
                            last = nc.tensor.matmul(bank[h][:, i * P:(i + 1) * P], w1[:, k, f * P:(f + 1) * P], picked_t[:, k, :],
                                                    start=(k == 0), stop=(k == ND - 1))
                    last.then_inc(s["hidden_done"], 1)
                for f in range(NF):
                    pe.wait_ge(s["hidden_ready"], f + 1)
                    last = nc.tensor.matmul(bank[2][:, 0:DIM], hidden[:, f, :], w2[:, f, :], start=(f == 0), stop=(f == NF - 1))
                last.then_inc(s["block_done"], 1)
                pe.wait_ge(s["block_ready"], 1)
                pe.wait_ge(s["onehot_t_dve"], 2)
                pe.wait_ge(s["onehot_t_act"], 2)
                for t in range(NT):
                    if t >= 4 and t % 2 == 0:
                        pe.wait_ge(s["added"], t - 2)
                    last = nc.tensor.matmul(bank[(t // 2) % 2 * 4][:, (t % 2) * DIM:(t % 2 + 1) * DIM], onehot_t[:, t, :], block_out[:],
                                            start=True, stop=True)
                    if t % 2:
                        last.then_inc(s["scattered"], 1)
    core.end_step()


def mixed_ffn_stage(core, tag, out=None):
    nc, x, inp = core.nc, core.x, core.inp
    with ExitStack() as ctx:
        first = not core.mixed_ready
        core.mixed_ready = True
        factors = core.sb(f"{tag}_factors", [P, RANK, ND, DIM], F32, ctx) if first else None
        xn = core.sb(f"{tag}_xn", [P, NT, DIM], F32, ctx)
        xn_t = core.sb(f"{tag}_xn_t", [P, ND, TOKENS], F32, ctx)
        bank = [ctx.enter_context(nc.psum_tensor(f"{tag}_bank{i}", [P, CH], F32)) for i in range(8)]
        norm = Norm(core, ctx, tag, xn, xn_t, bank[:4])
        mixed_done, added, stored = (core.sem(f"{tag}_{n}") for n in ("mixed_done", "added", "stored"))
        factors_loaded, bias_loaded, summed = (core.sem(f"{tag}_{n}") for n in ("factors_loaded", "bias_loaded", "summed"))
        with nc.Block() as block:
            @block.gpsimd
            def _(pool):
                if first:
                    for r in range(1, RANK):
                        pool.wait_ge(factors_loaded, 16 * RANK)
                        earlier = factors[:, 0] if r == 1 else core.mixed[:]
                        if r > 1:
                            pool.wait_ge(summed, r - 1)
                        nc.gpsimd.tensor_tensor(core.mixed[:], earlier, factors[:, r], ALU.add).then_inc(summed, 1)

            @block.vector
            def _(dve):
                norm.vector(dve, Link(core, dve, f"{tag}_dve_link"))
                if first:
                    dve.wait_ge(bias_loaded, 16)
                    nc.vector.tensor_scalar(core.half_bias[:], core.half_bias[:], 0.5, None, ALU.mult).then_inc(bias_loaded, 1)
                    dve.wait_ge(bias_loaded, 17)
                dve.wait_ge(norm.xn_ready, NT)
                bias = core.half_bias[:].unsqueeze(1).broadcast_to([P, NT // 2, DIM])
                link = Link(core, dve, f"{tag}_biased")
                for h in range(2):
                    tiles = x[:, h * NT // 2:(h + 1) * NT // 2, :]
                    last = nc.vector.tensor_tensor(tiles, tiles, bias, ALU.add)
                link(last)
                for b in range(NT // 2):
                    dve.wait_ge(mixed_done, b + 1)
                    pair = x[:, 2 * b:2 * b + 2, :]
                    nc.vector.scalar_tensor_tensor(pair, bank[4 + b % 4][:].rearrange("p (t d) -> p t d", d=DIM),
                                                   0.5 / float(np.sqrt(RANK)), pair, ALU.mult, ALU.add).then_inc(added, 1)
                dve.wait_ge(added, NT // 2)

            @block.scalar
            def _(act):
                norm.scalar(act)

            @block.tensor
            def _(pe):
                norm.tensor(pe)
                if first:
                    pe.wait_ge(summed, RANK - 1)
                for b in range(NT // 2):
                    norm.turn.wait_chunk(pe, 2 * b // TPC)
                    if b >= 4:
                        pe.wait_ge(added, b - 3)
                    for i in range(2):
                        t = 2 * b + i
                        for k in range(ND):
                            last = nc.tensor.matmul(bank[4 + b % 4][:, i * DIM:(i + 1) * DIM], xn_t[:, k, t * P:(t + 1) * P],
                                                    core.mixed[:, k, :], start=(k == 0), stop=(k == ND - 1))
                    last.then_inc(mixed_done, 1)

            @block.sync
            def _(sp):
                if first:
                    for r in range(RANK):
                        sp.dma_start(factors[:, r], inp["L1_ffn_factors"][r].rearrange("(k p) e -> p k e", p=P)).then_inc(factors_loaded, 16)
                    sp.dma_start(core.half_bias[:], inp["L1_ffn_bias"].partition_broadcast(P)).then_inc(bias_loaded, 16)
                if out is not None:
                    rows = out[0].rearrange("(t p) d -> p t d", p=P)
                    for b in range(0, NT // 2, 2):
                        sp.wait_ge(added, b + 2)
                        sp.dma_start(rows[:, 2 * b:2 * b + 4, :], x[:, 2 * b:2 * b + 4, :]).then_inc(stored, 16)
                    sp.wait_ge(stored, 16 * (NT // 4))
    core.end_step()


def wait(engine, sem, value):
    if not isinstance(value, int) or value > 0:
        engine.wait_ge(sem, value)


def latent_attention_stage(core):
    with ExitStack() as ctx:
        def sb(name, shape, dt=F32):
            return core.sb(f"lat_{name}", shape, dt, ctx)
        qa_t = sb("qa_t", [P, 2, TOKENS])
        key_hi, key_lo = sb("key_hi", [P, TOKENS], F32R), sb("key_lo", [P, TOKENS], F32R)
        latent = sb("latent", [P, NT, P])
        latent_projections(core, qa_t, key_hi, key_lo, latent)
        latent_heads(core, qa_t, key_hi, key_lo, latent)


def latent_projections(core, qa_t, key_hi, key_lo, latent):
    nc, inp = core.nc, core.inp
    W = QL + KL + DR
    with ExitStack() as ctx:
        def sb(name, shape, dt=F32):
            return core.sb(f"latp_{name}", shape, dt, ctx)
        xn, xn_t = sb("xn", [P, NT, DIM]), sb("xn_t", [P, ND, TOKENS])
        w_down = sb("w_down", [P, ND, W])
        q_ln, kv_ln = sb("q_ln", [P, QL]), sb("kv_ln", [P, KL])
        rope = sb("rope", [P, 2, NT, DR // 2])
        down = sb("down", [P, NT, W])
        squares = sb("squares", [P, 2, QL])
        sums, mean_sq, root, rstd, scratch = (sb(n, [P, NT, 2]) for n in ("sums", "mean_sq", "root", "rstd", "scratch"))
        part = [sb(f"part{i}", [P, NT, DR // 2]) for i in range(4)]
        bank = [ctx.enter_context(nc.psum_tensor(f"latp_bank{i}", [P, CH], F32)) for i in range(8)]
        norm = Norm(core, ctx, "latn", xn, xn_t, bank[:4])
        names = ("loaded down_done down_copied squared mean_ready root_ready q_scaled latent_ready key_turned"
                 " key_hi_done key_lo_done q_turned q_turned_2 q_copied q_copied_2").split()
        s = {n: core.sem(f"latp_{n}") for n in names}
        with nc.Block() as block:
            @block.sync
            def _(sp):
                sp.dma_start(w_down[:, :, 0:QL], inp["L0_attn_w_q_a"].rearrange("(k p) e -> p k e", p=P)).then_inc(s["loaded"], 16)
                sp.dma_start(w_down[:, :, QL:W], inp["L0_attn_w_kv_a"].rearrange("(k p) e -> p k e", p=P)).then_inc(s["loaded"], 16)
                sp.dma_start(q_ln[:], inp["L0_attn_q_a_ln"].partition_broadcast(P)).then_inc(s["loaded"], 16)
                sp.dma_start(kv_ln[:], inp["L0_attn_kv_a_ln"].partition_broadcast(P)).then_inc(s["loaded"], 16)
                sp.dma_start(rope[:], inp["c_rope0_token"]).then_inc(s["loaded"], 16)

            @block.vector
            def _(dve):
                link = Link(core, dve, "latp_link")
                nc.vector.memset(qa_t[64:P, 1, :], 0.0)
                norm.vector(dve, link)
                for t in range(NT):
                    dve.wait_ge(s["down_done"], t + 1)
                    nc.vector.tensor_copy(down[:, t, :], bank[4 + t % 4][:, 0:W]).then_inc(s["down_copied"], 1)
                dve.wait_ge(s["loaded"], 80)
                dve.wait_ge(s["down_copied"], NT)
                even, odd = down[:, :, QL + KL:W:2], down[:, :, QL + KL + 1:W:2]
                cos, sin = rope[:, 0], rope[:, 1]
                for out, a, b in zip(part, (even, odd, odd, even), (cos, sin, cos, sin)):
                    last = nc.vector.tensor_tensor(out[:], a, b, ALU.mult)
                link(last)
                half = DR // 2
                nc.vector.tensor_tensor(latent[:, :, KL:KL + half], part[0][:], part[1][:], ALU.subtract)
                nc.vector.tensor_tensor(latent[:, :, KL + half:P], part[2][:], part[3][:], ALU.add)
                dve.wait_ge(s["squared"], 2 * NT)
                for i, width in enumerate((QL, KL)):
                    mean = nc.vector.tensor_scalar(mean_sq[:, :, i], sums[:, :, i], 1.0 / width, RMS_EPS, ALU.mult, ALU.add)
                mean.then_inc(s["mean_ready"], 1)
                dve.wait_ge(s["root_ready"], 1)
                reciprocal_of_root(nc, link, rstd[:], root[:], mean_sq[:], scratch[:])
                for t in range(NT):
                    nc.vector.scalar_tensor_tensor(latent[:, t, 0:KL], down[:, t, QL:QL + KL], rstd[:, t, 1:2], kv_ln[:],
                                                   ALU.mult, ALU.mult).then_inc(s["latent_ready"], 1)
                for t in range(NT):
                    nc.vector.scalar_tensor_tensor(down[:, t, 0:QL], down[:, t, 0:QL], rstd[:, t, 0:1], q_ln[:],
                                                   ALU.mult, ALU.mult).then_inc(s["q_scaled"], 1)
                for c in range(NCH):
                    dve.wait_ge(s["key_hi_done"], c + 1)
                    cols = slice(c * CH, (c + 1) * CH)
                    nc.vector.tensor_tensor(key_lo[:, cols], bank[c][:], key_hi[:, cols].bitcast(F32),
                                            ALU.subtract).then_inc(s["key_lo_done"], 1)
                for c in range(NCH):
                    dve.wait_ge(s["q_turned_2"], c + 1)
                    nc.vector.tensor_copy(qa_t[0:QL - P, 1, c * CH:(c + 1) * CH], bank[c][0:QL - P, :]).then_inc(s["q_copied_2"], 1)
                dve.wait_ge(s["q_copied_2"], NCH)

            @block.scalar
            def _(act):
                norm.scalar(act)
                for t in range(NT):
                    act.wait_ge(s["down_copied"], t + 1)
                    if t >= 1:
                        act.wait_ge(s["squared"], 2 * t)
                    nc.scalar.activation(squares[:, 0, 0:QL], down[:, t, 0:QL], ACT.Square,
                                         accum_out=sums[:, t, 0:1]).then_inc(s["squared"], 1)
                    nc.scalar.activation(squares[:, 1, 0:KL], down[:, t, QL:QL + KL], ACT.Square,
                                         accum_out=sums[:, t, 1:2]).then_inc(s["squared"], 1)
                act.wait_ge(s["mean_ready"], 1)
                nc.scalar.activation(root[:], mean_sq[:], ACT.Sqrt).then_inc(s["root_ready"], 1)
                for c in range(NCH):
                    act.wait_ge(s["key_turned"], c + 1)
                    nc.scalar.activation(key_hi[:, c * CH:(c + 1) * CH], bank[c][:], ACT.Copy).then_inc(s["key_hi_done"], 1)
                for c in range(NCH):
                    act.wait_ge(s["q_turned"], c + 1)
                    nc.scalar.activation(qa_t[:, 0, c * CH:(c + 1) * CH], bank[4 + c][:], ACT.Copy).then_inc(s["q_copied"], 1)
                act.wait_ge(s["q_copied"], NCH)

            @block.tensor
            def _(pe):
                norm.tensor(pe)
                pe.wait_ge(s["loaded"], 80)
                for t in range(NT):
                    norm.turn.wait_chunk(pe, t // TPC)
                    if t >= 4:
                        pe.wait_ge(s["down_copied"], t - 3)
                    for k in range(ND):
                        last = nc.tensor.matmul(bank[4 + t % 4][:, 0:W], xn_t[:, k, t * P:(t + 1) * P], w_down[:, k, :],
                                                start=(k == 0), stop=(k == ND - 1))
                    last.then_inc(s["down_done"], 1)
                for c in range(NCH):
                    pe.wait_ge(s["latent_ready"], TPC * (c + 1))
                    for i in range(TPC):
                        last = nc.tensor.transpose(bank[c][:, i * P:(i + 1) * P], latent[:, TPC * c + i, :], core.ident)
                    last.then_inc(s["key_turned"], 1)
                pe.wait_ge(s["down_copied"], NT)
                for c in range(NCH):
                    pe.wait_ge(s["q_scaled"], TPC * (c + 1))
                    for i in range(TPC):
                        last = nc.tensor.transpose(bank[4 + c][:, i * P:(i + 1) * P], down[:, TPC * c + i, 0:P], core.ident)
                    last.then_inc(s["q_turned"], 1)
                for c in range(NCH):
                    pe.wait_ge(s["key_lo_done"], c + 1)
                    for i in range(TPC):
                        last = nc.tensor.transpose(bank[c][0:QL - P, i * P:(i + 1) * P], down[:, TPC * c + i, P:QL], core.ident)
                    last.then_inc(s["q_turned_2"], 1)
    core.end_step()


def key_tiles(j):
    return TPC * (j + 1)


STEPS_BEFORE = [sum(key_tiles(i) for i in range(j)) for j in range(NCH)]


def latent_schedule(first, last):
    events, side_uses = [], 0

    def numbered(kind, *rest):
        nonlocal side_uses
        side_uses += 1
        return (kind, *rest, side_uses - 1)

    for j in range(NCH):
        steps = key_tiles(j)
        slots = [[] for _ in range(steps)]
        main = []
        if not (last and j == NCH - 1):
            nj = (j + 1) % NCH
            for h in range(2):
                main += [("maxima", j + 1, h, i, kc) for i in range(TPC) for kc in range(nj + 1)]
                main += [("shift", j + 1, h)]
        for n, event in enumerate(main):
            slots[n * steps // len(main)].append(event)
        side = []
        if not (first and j == 0):
            side += [("sums", j - 1)] + [("project", j - 1, i) for i in range(TPC)]
        if j == 0:
            side += [("fold_out",)]
        if not (last and j >= 2):
            side += [(kind, j + 2, h) for h in range(2) for kind in ("query", "split")]
        if j == 1 and not last:
            side += [("turn_q_weights",), ("turn_kv_weights",), ("fold_query",)]
        for n, event in enumerate(side):
            slots[2 + n * (steps - 2) // len(side)].append(event)
        if main:
            slots[-1] += [("spread", j + 1, 0), ("spread", j + 1, 1)]
        for kt in range(steps):
            events.append(("scores", j, kt))
            events += slots[kt][:len(slots[kt]) // 2] if kt % 2 else slots[kt]
            if kt % 2:
                if kt > 1:
                    events.append(("values", j, kt // 2 - 1))
                elif not (first and j == 0):
                    events += [("values", j - 1, key_tiles((j - 1) % NCH) // 2 - 1), ("drain", j - 1)]
                events += slots[kt][len(slots[kt]) // 2:]
    on_side = ("fold_out", "query", "turn_q_weights", "turn_kv_weights", "fold_query", "spread")
    return [numbered(*e) if e[0] in on_side else e for e in events]


LATENT_PROLOGUE = ([("turn_q_weights", 0), ("turn_kv_weights", 1), ("fold_query", 2)]
                   + [e for n in range(2) for h in range(2) for e in [("query", n, h, 3 + 2 * n + h), ("split", n, h)]]
                   + [e for h in range(2) for e in [("maxima", 0, h, i, 0) for i in range(TPC)] + [("shift", 0, h)]]
                   + [("spread", 0, 0, 7), ("spread", 0, 1, 8)])
PROLOGUE_SIDE = 9
LATENT_EPILOGUE = ([("values", -1, key_tiles(NCH - 1) // 2 - 1), ("drain", -1), ("sums", -1)]
                   + [("project", -1, i) for i in range(TPC)])


def latent_heads(core, qa_t, key_hi, key_lo, latent):
    nc, inp, x = core.nc, core.inp, core.x
    w_qb = inp["L0_attn_w_q_b"]
    w_kvb = inp["L0_attn_w_kv_b"]
    w_out = inp["L0_attn_w_out"]
    QW, KVW = 2 * DQ, 2 * (DN + DV)
    with ExitStack() as ctx:
        def sb(name, shape, dt=F32):
            return core.sb(f"lath_{name}", shape, dt, ctx)
        rope = sb("rope", [P, 2, TOKENS])
        ones_r, minus_ident = sb("ones_r", [P, P], F32R), sb("minus_ident", [P, P])
        zeros32 = sb("zeros32", [P, 32])
        raw_q, raw_kv, raw_out = sb("raw_q", [P, 2, QW]), sb("raw_kv", [P, KVW]), sb("raw_out", [P, 2, DIM])
        q_w_t, kv_w_t = sb("q_w_t", [P, 2, QL]), sb("kv_w_t", [P, 2, 2, KL])
        w_query = sb("w_query", [P, 2, 2, P])
        w_value = sb("w_value", [P, DIM])
        turn_a, turn_b = sb("turn_a", [P, CH]), sb("turn_b", [P, CH])
        query = sb("query", [P, CH])
        query_hi, query_lo = sb("query_hi", [P, NCH, 2, CH], F32R), sb("query_lo", [P, NCH, 2, CH], F32R)
        maxima = sb("maxima", [P, 2, TPC, NCH])
        row_max = sb("row_max", [P, 2, TPC])
        shift_diag = sb("shift_diag", [P, 2, TPC, P], F32R)
        shift = sb("shift", [P, 2, 2, CH])
        shifted = sb("shifted", [P, 4, CH])
        probs = sb("probs", [P, 8, CH])
        out_t = sb("out_t", [P, 2, CH])
        sums_t = sb("sums_t", [P, CH])
        total, inverse = sb("total", [P, TPC, 2]), sb("inverse", [P, TPC, 2])
        score_bank = [ctx.enter_context(nc.psum_tensor(f"lath_score{i}", [P, CH], F32)) for i in range(2)]
        max_bank = [ctx.enter_context(nc.psum_tensor(f"lath_max{i}", [P, CH], F32)) for i in range(2)]
        out_bank = ctx.enter_context(nc.psum_tensor("lath_out", [P, CH], F32))
        sum_bank = ctx.enter_context(nc.psum_tensor("lath_sum", [P, CH], F32))
        end_bank = ctx.enter_context(nc.psum_tensor("lath_end", [P, CH], F32))
        side_bank = ctx.enter_context(nc.psum_tensor("lath_side", [P, CH], F32))
        names = ("tables_loaded q_kv_loaded out_loaded vector_constants"
                 " scores_done shift_added exp_done values_done"
                 " maxima_done maxima_taken row_max_done diag_ready side_done side_free"
                 " cosine_done sine_done query_whole query_hi_done query_lo_done"
                 " rotation_weights_ready query_weights_ready"
                 " drained end_done end_free inverse_ready first_added").split()
        s = {n: core.sem(f"lath_{n}") for n in names}
        schedules = {"first": latent_schedule(True, False), "middle": latent_schedule(False, False),
                     "last": latent_schedule(False, True)}

        def pairs(engine, run):
            run(LATENT_PROLOGUE, 0, prologue=True)
            run(schedules["first"], 0)
            with engine.Fori(1, PAIRS - 1) as pair:
                run(schedules["middle"], pair)
            run(schedules["last"], PAIRS - 1)
            run(LATENT_EPILOGUE, PAIRS)

        def chunk(pair, j):
            return pair * NCH + j

        def score_unit(pair, j, kt, h):
            return pair * (2 * KT_PER_PAIR) + 2 * (KT_PER_PAIR * (j // NCH) + STEPS_BEFORE[j % NCH] + kt) + h

        def values_unit(pair, j, m):
            return pair * (KT_PER_PAIR // 2) + (KT_PER_PAIR * (j // NCH) + STEPS_BEFORE[j % NCH]) // 2 + m

        def maxima_unit(pair, j, h, i, kc):
            nj = j % NCH
            return (pair * (2 * KT_PER_PAIR) + 2 * (KT_PER_PAIR * (j // NCH) + STEPS_BEFORE[nj])
                    + h * key_tiles(nj) + i * (nj + 1) + kc)

        def side_use(pair, local, prologue):
            return local if prologue else pair * (NCH * 5) + PROLOGUE_SIDE + local

        with nc.Block() as block:
            @block.sync
            def _(sp):
                sp.dma_start(rope[64:P], inp["c_rope0_feature"][64:P]).then_inc(s["tables_loaded"], 16)
                sp.dma_start(raw_q[:, 0, :], w_qb[0:P, 0:QW]).then_inc(s["q_kv_loaded"], 16)
                sp.dma_start(raw_q[0:QL - P, 1, :], w_qb[P:QL, 0:QW]).then_inc(s["q_kv_loaded"], 16)
                sp.dma_start(raw_kv[0:KL, :], w_kvb[:, 0:KVW]).then_inc(s["q_kv_loaded"], 16)
                sp.dma_start(raw_out[:], w_out[0:2 * DV, :].rearrange("(h p) e -> p h e", p=P)).then_inc(s["out_loaded"], 16)
                with sp.Fori(1, PAIRS) as pair:
                    sp.wait_ge(s["query_weights_ready"], pair)
                    sp.wait_ge(s["rotation_weights_ready"], pair)
                    sp.dma_start(raw_q[:, 0, :], w_qb[0:P, bass.ds(pair * QW, QW)]).then_inc(s["q_kv_loaded"], 16)
                    sp.dma_start(raw_q[0:QL - P, 1, :], w_qb[P:QL, bass.ds(pair * QW, QW)]).then_inc(s["q_kv_loaded"], 16)
                    sp.dma_start(raw_kv[0:KL, :], w_kvb[:, bass.ds(pair * KVW, KVW)]).then_inc(s["q_kv_loaded"], 16)
                    sp.wait_ge(s["side_free"], side_use(pair - 1, 0, False) + 1)
                    sp.dma_start(raw_out[:], w_out[bass.ds(pair * 2 * DV, 2 * DV), :].rearrange("(h p) e -> p h e", p=P))\
                      .then_inc(s["out_loaded"], 16)

            @block.tensor
            def _(pe):
                def run(events, pair, prologue=False):
                    for kind, *a in events:
                        if kind == "scores":
                            j, kt = a
                            for h in range(2):
                                u = score_unit(pair, j, kt, h)
                                if h == 0 and kt == 0:
                                    wait(pe, s["query_lo_done"], 2 * chunk(pair, j) + 2)
                                wait(pe, s["shift_added"], u - 1)
                                diagonal = kt - TPC * j
                                q0 = max(diagonal, 0) * P
                                out = score_bank[h][:, q0:CH]
                                hi, lo = query_hi[:, j, h, q0:CH], query_lo[:, j, h, q0:CH]
                                keys = slice(kt * P, (kt + 1) * P)
                                nc.tensor.matmul(out, key_hi[:, keys], hi, start=True, stop=False)
                                nc.tensor.matmul(out, key_hi[:, keys], lo, start=False, stop=False)
                                if diagonal >= 0:
                                    nc.tensor.matmul(score_bank[h][:, q0:q0 + P], core.ident_b, core.mask_kq, start=False, stop=False)
                                nc.tensor.matmul(out, key_lo[:, keys], hi, start=False, stop=True).then_inc(s["scores_done"], 1)
                        elif kind == "values":
                            j, m = a
                            nj = j % NCH
                            steps = key_tiles(nj)
                            wait(pe, s["exp_done"], score_unit(pair, j, 2 * m + 1, 1) + 1)
                            if m == 0:
                                wait(pe, s["drained"], 3 * chunk(pair, j))
                            for kt in (2 * m, 2 * m + 1):
                                q0 = max(kt - TPC * nj, 0) * P
                                for h in range(2):
                                    nc.tensor.matmul(out_bank[64 * h:64 * h + 64, q0:CH], latent[:, kt, 0:KL],
                                                     probs[:, 2 * (kt % 4) + h, q0:CH], start=(kt == 0), stop=(kt == steps - 1))
                            for kt in (2 * m, 2 * m + 1):
                                q0 = max(kt - TPC * nj, 0) * P
                                for h in range(2):
                                    row = 32 * (2 * (kt % 2) + h)
                                    if nj == 0 and kt == 1:
                                        nc.tensor.matmul(sum_bank[row:row + 32, :], zeros32[:], probs[:, h, :], start=True, stop=False)
                                    last = nc.tensor.matmul(sum_bank[row:row + 32, q0:CH], core.ones[:, 0:32],
                                                            probs[:, 2 * (kt % 4) + h, q0:CH],
                                                            start=(kt == 0 or (kt == 1 and nj > 0)), stop=(kt >= steps - 2))
                            last.then_inc(s["values_done"], 1)
                        elif kind == "maxima":
                            j, h, i, kc = a
                            nj = j % NCH
                            v = maxima_unit(pair, j, h, i, kc)
                            if i == 0 and kc == 0:
                                wait(pe, s["query_hi_done"], 2 * chunk(pair, j) + h + 1)
                            wait(pe, s["maxima_taken"], v - 1)
                            width = (i + 1) * P if kc == nj else CH
                            bank = max_bank[(i * (nj + 1) + kc) % 2]
                            mm = nc.tensor.matmul(bank[:, 0:width], query_hi[:, nj, h, i * P:(i + 1) * P],
                                                  key_hi[:, kc * CH:kc * CH + width], start=True, stop=(kc < nj))
                            if kc == nj:
                                mm = nc.tensor.matmul(bank[:, width - P:width], core.ident_b, core.mask_qk, start=False, stop=True)
                            mm.then_inc(s["maxima_done"], 1)
                        elif kind == "spread":
                            j, h, local = a
                            d = 2 * chunk(pair, j) + h
                            wait(pe, s["side_free"], side_use(pair, local, prologue))
                            wait(pe, s["diag_ready"], d + 1)
                            nc.tensor.matmul(side_bank[:], ones_r[:], shift_diag[:, h].rearrange("p t q -> p (t q)"),
                                             start=True, stop=True).then_inc(s["side_done"], 1)
                        elif kind == "query":
                            n, h, local = a
                            if h == 0:
                                wait(pe, s["rotation_weights_ready"], pair + n // NCH + 1)
                            wait(pe, s["side_free"], side_use(pair, local, prologue))
                            cols = slice((n % NCH) * CH, (n % NCH + 1) * CH)
                            for k in range(2):
                                mm = nc.tensor.matmul(side_bank[:], w_query[:, k, h, :], qa_t[:, k, cols], start=(k == 0), stop=(k == 1))
                            mm.then_inc(s["side_done"], 1)
                        elif kind == "turn_q_weights":
                            wait(pe, s["q_kv_loaded"], 48 * (pair + 1) if prologue else 48 * (pair + 2))
                            wait(pe, s["side_free"], side_use(pair, a[0], prologue))
                            for h in range(2):
                                nc.tensor.transpose(side_bank[:, h * QL:h * QL + P], raw_q[:, 0, h * DQ:h * DQ + DN], core.ident)
                                mm = nc.tensor.transpose(side_bank[:, h * QL + P:(h + 1) * QL], raw_q[0:QL - P, 1, h * DQ:h * DQ + DN],
                                                         core.ident[0:QL - P, 0:QL - P])
                            mm.then_inc(s["side_done"], 1)
                        elif kind == "turn_kv_weights":
                            wait(pe, s["side_free"], side_use(pair, a[0], prologue))
                            for n in range(4):
                                mm = nc.tensor.transpose(side_bank[:, n * P:(n + 1) * P], raw_kv[:, n * P:(n + 1) * P], core.ident)
                            mm.then_inc(s["side_done"], 1)
                        elif kind == "fold_query":
                            wait(pe, s["side_free"], side_use(pair, a[0], prologue))
                            for h in range(2):
                                nc.tensor.matmul(side_bank[:, h * P:h * P + KL], q_w_t[:, h, 0:P], kv_w_t[:, h, 0, :], start=True, stop=True)
                                mm = nc.tensor.matmul(side_bank[0:QL - P, h * P + KL:(h + 1) * P], q_w_t[:, h, P:QL], kv_w_t[:, h, 0, :],
                                                      start=True, stop=True)
                            mm.then_inc(s["side_done"], 1)
                        elif kind == "fold_out":
                            wait(pe, s["out_loaded"], 16 * (pair + 1))
                            wait(pe, s["side_free"], side_use(pair, a[0], prologue))
                            for h in range(2):
                                mm = nc.tensor.matmul(side_bank[64 * h:64 * h + 64, 0:DIM], kv_w_t[:, h, 1, :], raw_out[:, h, :],
                                                      start=True, stop=True)
                            mm.then_inc(s["side_done"], 1)
                        elif kind == "sums":
                            n = chunk(pair, a[0])
                            wait(pe, s["drained"], 3 * n + 3)
                            wait(pe, s["end_free"], n * (TPC + 1))
                            for i in range(TPC):
                                mm = nc.tensor.transpose(end_bank[:, i * P:(i + 1) * P], sums_t[:, i * P:(i + 1) * P], core.ident)
                            mm.then_inc(s["end_done"], 1)
                        elif kind == "project":
                            j, i = a
                            n = chunk(pair, j)
                            wait(pe, s["end_free"], n * (TPC + 1) + 1 + i)
                            for h in range(2):
                                mm = nc.tensor.matmul(end_bank[:, h * DIM:(h + 1) * DIM], out_t[:, h, i * P:(i + 1) * P], w_value[:],
                                                      start=True, stop=True)
                            mm.then_inc(s["end_done"], 1)

                pe.wait_ge(s["vector_constants"], 1)
                pairs(pe, run)

            @block.scalar
            def _(act):
                def copy_side(use, out, columns, rows=P):
                    wait(act, s["side_done"], use + 1)
                    return nc.scalar.activation(out, side_bank[0:rows, columns], ACT.Copy)

                def run(events, pair, prologue=False):
                    for kind, *a in events:
                        if kind == "scores":
                            j, kt = a
                            for h in range(2):
                                u = score_unit(pair, j, kt, h)
                                q0 = max(kt - TPC * j, 0) * P
                                wait(act, s["shift_added"], u + 1)
                                wait(act, s["values_done"], values_unit(pair, j, kt // 2) - 1)
                                nc.scalar.activation(probs[:, 2 * (kt % 4) + h, q0:CH], shifted[:, 2 * (kt % 2) + h, q0:CH], ACT.Exp,
                                                     scale=SCALE0).then_inc(s["exp_done"], 1)
                        elif kind == "drain":
                            n = chunk(pair, a[0])
                            wait(act, s["values_done"], values_unit(pair, a[0], key_tiles(a[0] % NCH) // 2 - 1) + 1)
                            for h in range(2):
                                rows = slice(64 * h, 64 * h + 64)
                                nc.scalar.activation(out_t[rows, h, :], out_bank[rows, :], ACT.Copy).then_inc(s["drained"], 1)
                            nc.scalar.activation(sums_t[:], sum_bank[:], ACT.Copy).then_inc(s["drained"], 1)
                        elif kind == "spread":
                            j, h, local = a
                            copy_side(side_use(pair, local, prologue), shift[:, j % 2, h, :], slice(0, CH)).then_inc(s["side_free"], 1)
                        elif kind == "query":
                            n, h, local = a
                            r = 2 * chunk(pair, n) + h
                            wait(act, s["query_lo_done"], r)
                            copy_side(side_use(pair, local, prologue), query[:], slice(0, CH)).then_inc(s["side_free"], 1)
                        elif kind == "split":
                            n, h = a
                            r = 2 * chunk(pair, n) + h
                            wait(act, s["query_whole"], r + 1)
                            nc.scalar.activation(query_hi[:, n % NCH, h, :], query[:], ACT.Copy).then_inc(s["query_hi_done"], 1)
                        elif kind == "turn_q_weights":
                            copy_side(side_use(pair, a[0], prologue), q_w_t[:].rearrange("p h r -> p (h r)"), slice(0, 2 * QL)).then_inc(s["side_free"], 1)
                            if prologue:
                                act.wait_ge(s["vector_constants"], 1)
                            for k, rows in enumerate((P, QL - P)):
                                rotated = raw_q[0:rows, k, :].rearrange("p (h c) -> p h c", h=2)[:, :, DN:DQ]
                                for odd in range(2):
                                    last = nc.scalar.activation(w_query[0:rows, k, :, KL + odd * DR // 2:KL + (odd + 1) * DR // 2],
                                                                rotated[:, :, odd:DR:2], ACT.Copy)
                            last.then_inc(s["rotation_weights_ready"], 1)
                        elif kind == "turn_kv_weights":
                            wait(act, s["side_done"], side_use(pair, a[0], prologue) + 1)
                            nc.scalar.activation(kv_w_t[:].rearrange("p h s r -> p (h s) r"),
                                                 side_bank[:].rearrange("p (n r) -> p n r", r=P)[:, :, 0:KL], ACT.Copy).then_inc(s["side_free"], 1)
                        elif kind == "fold_query":
                            use = side_use(pair, a[0], prologue)
                            wait(act, s["side_done"], use + 1)
                            folded = side_bank[:, 0:2 * P].rearrange("p (h k r) -> p h k r", h=2, k=2)
                            nc.scalar.activation(w_query[:, 0, :, 0:KL], folded[:, :, 0, :], ACT.Copy).then_inc(s["query_weights_ready"], 1)
                            nc.scalar.activation(w_query[0:QL - P, 1, :, 0:KL], folded[0:QL - P, :, 1, :], ACT.Copy).then_inc(s["side_free"], 1)
                        elif kind == "fold_out":
                            use = side_use(pair, a[0], prologue)
                            copy_side(use, w_value[:], slice(0, DIM)).then_inc(s["side_free"], 1)

                pairs(act, run)

            @block.gpsimd
            def _(pool):
                def run(events, pair, prologue=False):
                    for kind, *a in events:
                        if kind == "query":
                            n, h, local = a
                            r = 2 * chunk(pair, n) + h
                            if prologue and r == 0:
                                pool.wait_ge(s["tables_loaded"], 16)
                            pool.wait_ge(s["side_free"], side_use(pair, local, prologue) + 1)
                            nc.gpsimd.tensor_tensor(turn_a[64:P], query[64:P], rope[64:P, 0, (n % NCH) * CH:(n % NCH + 1) * CH],
                                                    ALU.mult).then_inc(s["cosine_done"], 1)
                            pool.wait_ge(s["cosine_done"], r + 1)
                            pool.wait_ge(s["sine_done"], 2 * r + 2)
                            nc.gpsimd.tensor_tensor(query[64:P], turn_a[64:P], turn_b[64:P], ALU.add).then_inc(s["query_whole"], 1)
                        elif kind == "split":
                            n, h = a
                            r = 2 * chunk(pair, n) + h
                            pool.wait_ge(s["query_hi_done"], r + 1)
                            nc.gpsimd.tensor_tensor(query_lo[:, n % NCH, h, :], query[:], query_hi[:, n % NCH, h, :].bitcast(F32),
                                                    ALU.subtract).then_inc(s["query_lo_done"], 1)

                pairs(pool, run)

            @block.vector
            def _(dve):
                def run(events, pair, prologue=False):
                    for kind, *a in events:
                        if kind == "scores":
                            j, kt = a
                            for h in range(2):
                                u = score_unit(pair, j, kt, h)
                                q0 = max(kt - TPC * j, 0) * P
                                wait(dve, s["scores_done"], u + 1)
                                wait(dve, s["exp_done"], u - 3)
                                nc.vector.tensor_tensor(shifted[:, 2 * (kt % 2) + h, q0:CH], score_bank[h][:, q0:CH],
                                                        shift[:, j % 2, h, q0:CH], ALU.add).then_inc(s["shift_added"], 1)
                        elif kind == "maxima":
                            j, h, i, kc = a
                            nj = j % NCH
                            v = maxima_unit(pair, j, h, i, kc)
                            width = (i + 1) * P if kc == nj else CH
                            wait(dve, s["maxima_done"], v + 1)
                            nc.vector.reduce_max(maxima[:, h, i, kc:kc + 1], max_bank[(i * (nj + 1) + kc) % 2][:, 0:width],
                                                 AX.X).then_inc(s["maxima_taken"], 1)
                        elif kind == "shift":
                            j, h = a
                            nj = j % NCH
                            d = 2 * chunk(pair, j) + h
                            wait(dve, s["maxima_taken"], maxima_unit(pair, j, h, TPC - 1, nj) + 1)
                            nc.vector.reduce_max(row_max[:, h, :], maxima[:, h, :, 0:nj + 1], AX.X).then_inc(s["row_max_done"], 1)
                            wait(dve, s["row_max_done"], d + 1)
                            nc.vector.tensor_tensor(shift_diag[:, h], minus_ident[:].unsqueeze(1).broadcast_to([P, TPC, P]),
                                                    row_max[:, h, :].unsqueeze(2).broadcast_to([P, TPC, P]), ALU.mult).then_inc(s["diag_ready"], 1)
                        elif kind == "spread":
                            wait(dve, s["side_free"], side_use(pair, a[2], prologue) + 1)
                        elif kind == "query":
                            n, h, local = a
                            r = 2 * chunk(pair, n) + h
                            cols = slice((n % NCH) * CH, (n % NCH + 1) * CH)
                            if prologue and r == 0:
                                dve.wait_ge(s["tables_loaded"], 16)
                            wait(dve, s["side_free"], side_use(pair, local, prologue) + 1)
                            wait(dve, s["query_whole"], r)
                            nc.vector.tensor_tensor(turn_b[64:96], query[96:P], rope[96:P, 1, cols], ALU.mult).then_inc(s["sine_done"], 1)
                            nc.vector.tensor_tensor(turn_b[96:P], query[64:96], rope[64:96, 1, cols], ALU.mult).then_inc(s["sine_done"], 1)
                        elif kind == "sums":
                            n = chunk(pair, a[0])
                            wait(dve, s["end_done"], n * (TPC + 1) + 1)
                            four = end_bank[:].rearrange("p (t r h c) -> p t h r c", t=TPC, r=2, h=2)[:, :, :, :, 0]
                            nc.vector.reduce_sum(total[:], four, AX.X).then_inc(s["end_free"], 1)
                            wait(dve, s["end_free"], n * (TPC + 1) + 1)
                            nc.vector.reciprocal(inverse[:], total[:]).then_inc(s["inverse_ready"], 1)
                            wait(dve, s["inverse_ready"], n + 1)
                        elif kind == "project":
                            j, i = a
                            n = chunk(pair, j)
                            t = TPC * (j % NCH) + i
                            wait(dve, s["end_done"], n * (TPC + 1) + i + 2)
                            nc.vector.scalar_tensor_tensor(x[:, t, :], end_bank[:, 0:DIM], inverse[:, i, 0:1], x[:, t, :],
                                                           ALU.mult, ALU.add).then_inc(s["first_added"], 1)
                            wait(dve, s["first_added"], n * TPC + i + 1)
                            nc.vector.scalar_tensor_tensor(x[:, t, :], end_bank[:, DIM:2 * DIM], inverse[:, i, 1:2], x[:, t, :],
                                                           ALU.mult, ALU.add).then_inc(s["end_free"], 1)

                nc.vector.tensor_scalar(minus_ident[:], core.ident, -1.0, None, ALU.mult)
                nc.vector.memset(w_query[64:P, 1], 0.0)
                nc.vector.memset(zeros32[:], 0.0)
                nc.vector.memset(raw_kv[KL:P, :], 0.0)
                nc.vector.memset(out_t[64:P, 0, :], 0.0)
                nc.vector.memset(out_t[0:64, 1, :], 0.0)
                nc.vector.tensor_copy(ones_r[:], core.ones).then_inc(s["vector_constants"], 1)
                dve.wait_ge(s["vector_constants"], 1)
                pairs(dve, run)
    core.end_step()


def attention_stage(core):
    with ExitStack() as ctx:
        def sb(name, shape, dt=F32):
            return core.sb(f"att_{name}", shape, dt, ctx)
        qk = sb("qk", [P, NT, 2 * DIM])
        v = sb("v", [P, NT, DIM])
        w_o_t = sb("w_o_t", [P, ND, DIM])
        attended = sb("attended", [P, NT, DIM])
        attention_projections(core, qk, v, w_o_t)
        attention_heads(core, qk, v, attended)
        attention_output(core, attended, w_o_t)


def attention_projections(core, qk, v, w_o_t):
    nc, inp = core.nc, core.inp
    with ExitStack() as ctx:
        def sb(name, shape, dt=F32):
            return core.sb(f"attp_{name}", shape, dt, ctx)
        xn, xn_t = sb("xn", [P, NT, DIM]), sb("xn_t", [P, ND, TOKENS])
        raw = sb("raw", [P, 4, ND, DIM])
        w_qkv_t = sb("w_qkv_t", [P, ND, 3 * DIM])
        rope = sb("rope", [P, 2, NT, D1])
        by_cos, by_sin = sb("by_cos", [P, 2, 2 * DIM]), sb("by_sin", [P, 2, 2 * DIM])
        bank = [ctx.enter_context(nc.psum_tensor(f"attp_bank{i}", [P, CH], F32)) for i in range(8)]
        norm = Norm(core, ctx, "attn", xn, xn_t, bank[:4])
        names = "weights_loaded rope_loaded weights_turned weights_copied qk_done v_done products_done rotated v_copied".split()
        s = {n: core.sem(f"attp_{n}") for n in names}
        with nc.Block() as block:
            @block.sync
            def _(sp):
                for m, name in enumerate(("Wq", "Wk", "Wv", "Wo")):
                    sp.dma_start(raw[:, m], inp[f"L1_attn_{name}"].rearrange("(k p) d -> p k d", p=P)).then_inc(s["weights_loaded"], 16)
                sp.dma_start(rope[:], inp["c_rope1_token"]).then_inc(s["rope_loaded"], 16)

            @block.vector
            def _(dve):
                norm.vector(dve, Link(core, dve, "attp_link"))
                dve.wait_ge(s["rope_loaded"], 16)
                heads = 2 * H1
                for t in range(NT):
                    dve.wait_ge(s["qk_done"], t + 1)
                    if t >= 2:
                        dve.wait_ge(s["rotated"], 2 * (t - 1))
                    scores = bank[4 + t % 2][:].rearrange("p (h c) -> p h c", c=D1)
                    for out, table in ((by_cos, 0), (by_sin, 1)):
                        last = nc.vector.tensor_tensor(out[:, t % 2, :].rearrange("p (h c) -> p h c", c=D1), scores,
                                                       rope[:, table, t, :].unsqueeze(1).broadcast_to([P, heads, D1]), ALU.mult)
                    last.then_inc(s["products_done"], 1)

            @block.gpsimd
            def _(pool):
                for t in range(NT):
                    pool.wait_ge(s["products_done"], t + 1)
                    a, b = by_cos[:, t % 2, :], by_sin[:, t % 2, :]
                    nc.gpsimd.tensor_tensor(qk[:, t, 0:2 * DIM:2], a[:, 0:2 * DIM:2], b[:, 1:2 * DIM:2], ALU.subtract).then_inc(s["rotated"], 1)
                    nc.gpsimd.tensor_tensor(qk[:, t, 1:2 * DIM:2], b[:, 0:2 * DIM:2], a[:, 1:2 * DIM:2], ALU.add).then_inc(s["rotated"], 1)
                pool.wait_ge(s["rotated"], 2 * NT)

            @block.scalar
            def _(act):
                for m in range(4):
                    act.wait_ge(s["weights_turned"], m + 1)
                    to = w_o_t[:] if m == 3 else w_qkv_t[:, :, m * DIM:(m + 1) * DIM]
                    nc.scalar.activation(to, bank[4 + m][:].rearrange("p (k e) -> p k e", k=ND), ACT.Copy).then_inc(s["weights_copied"], 1)
                norm.scalar(act)
                for t in range(NT):
                    act.wait_ge(s["v_done"], t + 1)
                    nc.scalar.activation(v[:, t, :], bank[6 + t % 2][:, 0:DIM], ACT.Copy).then_inc(s["v_copied"], 1)
                act.wait_ge(s["v_copied"], NT)

            @block.tensor
            def _(pe):
                pe.wait_ge(s["weights_loaded"], 64)
                for m in range(4):
                    for k in range(ND):
                        for e in range(ND):
                            last = nc.tensor.transpose(bank[4 + m][:, k * DIM + e * P:k * DIM + (e + 1) * P],
                                                       raw[:, m, e, k * P:(k + 1) * P], core.ident)
                    last.then_inc(s["weights_turned"], 1)
                norm.tensor(pe)
                pe.wait_ge(s["weights_copied"], 4)
                for t in range(NT):
                    norm.turn.wait_chunk(pe, t // TPC)
                    if t >= 2:
                        pe.wait_ge(s["products_done"], t - 1)
                    for k in range(ND):
                        last = nc.tensor.matmul(bank[4 + t % 2][:], xn_t[:, k, t * P:(t + 1) * P], w_qkv_t[:, k, 0:2 * DIM],
                                                start=(k == 0), stop=(k == ND - 1))
                    last.then_inc(s["qk_done"], 1)
                    if t >= 2:
                        pe.wait_ge(s["v_copied"], t - 1)
                    for k in range(ND):
                        last = nc.tensor.matmul(bank[6 + t % 2][:, 0:DIM], xn_t[:, k, t * P:(t + 1) * P], w_qkv_t[:, k, 2 * DIM:3 * DIM],
                                                start=(k == 0), stop=(k == ND - 1))
                    last.then_inc(s["v_done"], 1)
    core.end_step()


LAG = 3
FINISH_AT = LAG
MAXIMA_STEPS = [(-11.0, -8.9), (-7.0, -0.8), (0.5, 8.6), (10.4, 22.8)]


def preparation(j):
    start, end = MAXIMA_STEPS[j]
    units = [[("maxima", j, h, i, kc) for i in range(TPC) for kc in range(j + 1)] for h in range(GROUP)]
    main = units[0] + units[1] + [("shift", j, 0)] + units[2] + units[3] + [("shift", j, 1)]
    each = (end - start) / len(main)
    out = [(start - 3, ("split", j)), (start + 2.2, ("split_values", j))]
    out += [(start + n * each, event) for n, event in enumerate(main)]

    def turn(step, kind, pair):
        halves = 1 if kind == "turn_keys" else 2
        return [[(step, (kind, j, pair))] + [(step + 0.24 * (n + 1), ("place", kind, j, pair, n)) for n in range(halves)]]
    middle = (start + end) / 2
    turns = turn(start - 1, "turn_keys", 0) + turn(start - 0.6, "turn_queries", 0)
    turns += turn(start + 0.2 * (middle - start), "turn_keys", 1) + turn(start + 0.5 * (middle - start), "turn_queries", 1)
    turns += turn(middle + 0.4, "turn_shifted", 0) + turn(end + 0.2, "turn_shifted", 1)
    return out, turns


def placed_events():
    placed = []
    for j in range(NCH):
        alone, turns = preparation(j)
        placed += [(step, j, [(step, event)]) for step, event in alone] + [(turn[0][0], j, turn) for turn in turns]
    placed += [(STEPS_BEFORE[j + 1] + FINISH_AT, j, [(STEPS_BEFORE[j + 1] + FINISH_AT, ("finish", j))]) for j in range(-1, NCH - 1)]
    placed.sort(key=lambda p: p[0])
    out, side_end = [], -KT_PER_PAIR
    for step, j, together in placed:
        if together[0][1][0].startswith("turn") or together[0][1][0] == "finish":
            late = max(side_end - step, 0)
            side_end = together[-1][0] + late + 0.01
            together = [(at + late, event) for at, event in together]
        out.append((step, j, together))
    return out


def in_chunk(event, j, to):
    at = event.index(j, 1)
    return (*event[:at], to, *event[at + 1:])


def attention_schedule(first, last):
    placed = []
    for step, j, together in placed_events():
        if step >= 0 and not (first and j < 0):
            placed += together
        elif step < 0 and not last:
            placed += [(at + KT_PER_PAIR, in_chunk(event, j, j + NCH)) for at, event in together]
    placed.sort(key=lambda e: e[0])
    events = []
    for j in range(NCH):
        for kt in range(key_tiles(j)):
            follow = (j, kt - LAG) if kt >= LAG else (j - 1, key_tiles((j - 1) % NCH) - LAG + kt)
            atoms = [[("scores", j, kt, h)] for h in range(GROUP)]
            if not (first and j == 0 and kt < LAG):
                for half in range(2):
                    atoms[2 * half + 1].append(("values", *follow, half))
                if kt == LAG - 1:
                    atoms[3].append(("drain", j - 1))
            for n, atom in enumerate(atoms):
                events += atom
                while placed and placed[0][0] < STEPS_BEFORE[j] + kt + (n + 1) / len(atoms):
                    events.append(placed.pop(0)[1])
    return events + [event for _, event in placed]


def attention_prologue():
    placed = [e for step, _, together in placed_events() if step < 0 for e in together]
    return [event for _, event in sorted(placed, key=lambda e: e[0])]


ATTENTION_EPILOGUE = ([("values", -1, key_tiles(NCH - 1) - LAG + i, half) for i in range(LAG) for half in range(2)]
                      + [("drain", -1), ("finish", -1)])
VECTOR_PLACES = (0, 1)
SIDE_PER_GROUP = 7 * NCH
SIDE_BEFORE = sum(e[0].startswith("turn") for e in attention_prologue()) - 1


def with_side_uses(events, start, earlier):
    out, uses = [], dict(earlier)
    for e in events:
        kind, j, *rest = e
        if kind == "place":
            e = (*e, uses[e[1:4]])
        elif kind.startswith("turn") or kind == "finish":
            if kind != "finish":
                uses[kind, j, rest[0]] = start
            e, start = (*e, start), start + 1
        elif kind == "split":
            e = (*e, uses.get(("turn_shifted", j - 2, 1)))
        elif kind == "maxima":
            e = (*e, uses["turn_queries", j, rest[0] // 2])
        elif kind == "scores":
            e = (*e, uses["turn_shifted", j, rest[1] // 2])
        out.append(e)
    return out, start, uses


def attention_heads(core, qk, v, attended):
    nc = core.nc
    prologue, _, uses = with_side_uses(attention_prologue(), -SIDE_BEFORE, {})
    first, _, uses = with_side_uses(attention_schedule(True, False), 1, uses)
    uses = {(kind, j - NCH, pair): use - SIDE_PER_GROUP for (kind, j, pair), use in uses.items()}
    middle, _, _ = with_side_uses(attention_schedule(False, False), 0, uses)
    final, side_end, _ = with_side_uses(attention_schedule(False, True), 0, uses)
    epilogue, _, _ = with_side_uses(ATTENTION_EPILOGUE, side_end - SIDE_PER_GROUP, {})
    with ExitStack() as ctx:
        def sb(name, shape, dt=F32):
            return core.sb(f"atth_{name}", shape, dt, ctx)
        q_slot, k_slot = sb("q_slot", [P, 2, TPC, GROUP, SLOT]), sb("k_slot", [P, 2, TPC, GROUP, SLOT])
        v_one = sb("v_one", [P, NT, GROUP, 32])
        key = sb("key", [P, 2, TOKENS], F32R)
        query = sb("query", [P, NCH, GROUP, CH], F32R)
        maxima = sb("maxima", [P, GROUP, TPC, NCH])
        row_max = sb("row_max", [P, GROUP, TPC])
        probs = sb("probs", [P, 4, GROUP, CH])
        out_t = sb("out_t", [P, CH])
        inverse = sb("inverse", [P, TPC, GROUP])
        score_bank = [ctx.enter_context(nc.psum_tensor(f"atth_score{i}", [P, CH], F32)) for i in range(3)]
        max_bank = [ctx.enter_context(nc.psum_tensor(f"atth_max{i}", [P, CH], F32)) for i in range(3)]
        out_bank = ctx.enter_context(nc.psum_tensor("atth_out", [P, CH], F32))
        side_bank = ctx.enter_context(nc.psum_tensor("atth_side", [P, CH], F32))
        names = ("constants_ready zeroed q_high_done q_low_done q_copied k_high_done k_low_done k_copied v_copied"
                 " side_done side_free maxima_done maxima_taken row_max_done"
                 " shift_high_done shift_ready scores_done exp_done values_done drained inverse_ready").split()
        s = {n: core.sem(f"atth_{n}") for n in names}

        def groups(engine, run):
            run(prologue, 0)
            run(first, 0)
            with engine.Fori(1, NG - 1) as group:
                run(middle, group)
            run(final, NG - 1)
            run(epilogue, NG)

        def chunk(group, j):
            return group * NCH + j

        def side_use(group, local):
            return group * SIDE_PER_GROUP + SIDE_BEFORE + local

        def step_unit(group, j, kt):
            return group * KT_PER_PAIR + KT_PER_PAIR * (j // NCH) + STEPS_BEFORE[j % NCH] + kt

        def score_unit(group, j, kt, h):
            return step_unit(group, j, kt) * GROUP + h

        def maxima_unit(group, j, h, i, kc):
            return step_unit(group, j, 0) * GROUP + (h * TPC + i) * (j % NCH + 1) + kc

        def maxima_place(j, h, i, kc):
            return GROUP * STEPS_BEFORE[j % NCH] + (h * TPC + i) * (j % NCH + 1) + kc

        def score_place(j, kt, h):
            return GROUP * (STEPS_BEFORE[j] + kt) + h

        def group_columns(group, j, base=0):
            start = (group + j // NCH) * (GROUP * D1) + base
            return slice(start, start + GROUP * D1) if isinstance(start, int) else bass.ds(start, GROUP * D1)

        def tiles(j):
            return slice(TPC * (j % NCH), TPC * (j % NCH) + TPC)

        def part(slot, j, n):
            return slot[:, j % 2, :, :, n * D1:(n + 1) * D1]

        def by_head(tensor, j, columns):
            return tensor[:, tiles(j), columns].rearrange("p t (h c) -> p t h c", c=D1)

        def rows_of(n):
            return slice(64 * n, 64 * n + 64)

        def placed_by_vector(place):
            kind, j, pair, n, _ = place
            return j % NCH in VECTOR_PLACES and (n == 1 or kind == "turn_keys")

        def place(engine, group, what, copy):
            kind, j, pair, n, local = what
            wait(engine, s["side_done"], side_use(group, local) + 1)
            if kind == "turn_keys":
                copy(key[:, pair, (j % NCH) * CH:(j % NCH + 1) * CH], side_bank[:]).then_inc(s["side_free"], 2)
            else:
                copy(query[rows_of(n), j % NCH, 2 * pair + n, :], side_bank[rows_of(n), :]).then_inc(s["side_free"], 1)

        with nc.Block() as block:
            @block.vector
            def _(dve):
                nc.vector.memset(q_slot[:], 0.0).then_inc(s["constants_ready"], 1)
                nc.vector.memset(k_slot[:, :, :, :, 3 * D1:SLOT], 0.0)
                nc.vector.memset(v_one[:, :, :, D1:32], 0.0)
                for h in range(GROUP):
                    last = nc.vector.memset(query[rows_of(1 - h % 2), :, h, :].bitcast(F32), 0.0)
                last.then_inc(s["constants_ready"], 1)
                dve.wait_ge(s["constants_ready"], 2)
                nc.vector.memset(k_slot[:, :, :, :, 3 * D1:3 * D1 + 2], 1.0)
                nc.vector.memset(v_one[:, :, :, D1:D1 + 1], 1.0).then_inc(s["constants_ready"], 1)

                def run(events, group):
                    for kind, *a in events:
                        if kind == "split":
                            j, before = a
                            if before is not None:
                                wait(dve, s["side_done"], side_use(group, before) + 1)
                            nc.vector.memset(q_slot[:, j % 2, :, :, 3 * D1:3 * D1 + 2], 0.0).then_inc(s["zeroed"], 1)
                        elif kind == "place" and placed_by_vector(a):
                            place(dve, group, a, nc.vector.tensor_copy)
                        elif kind == "maxima":
                            j, h, i, kc, turned = a
                            m = maxima_unit(group, j, h, i, kc)
                            nj = j % NCH
                            width = (i + 1) * P if kc == nj else CH
                            wait(dve, s["maxima_done"], m + 1)
                            nc.vector.reduce_max(maxima[:, h, i, kc:kc + 1], max_bank[maxima_place(j, h, i, kc) % 3][:, 0:width], AX.X)\
                              .then_inc(s["maxima_taken"], 1)
                        elif kind == "shift":
                            j, pair = a
                            nj, n = j % NCH, 2 * chunk(group, j) + pair
                            heads = slice(2 * pair, 2 * pair + 2)
                            wait(dve, s["maxima_taken"], maxima_unit(group, j, 2 * pair + 1, TPC - 1, nj) + 1)
                            nc.vector.reduce_max(row_max[:, heads, :], maxima[:, heads, :, 0:nj + 1], AX.X).then_inc(s["row_max_done"], 1)
                            wait(dve, s["row_max_done"], n + 1)
                            high, low = (q_slot[:, j % 2, :, heads, 3 * D1 + c].rearrange("p t h -> p h t") for c in range(2))
                            nc.vector.tensor_scalar(high.bitcast(F32R), row_max[:, heads, :], -1.0, None, ALU.mult).then_inc(s["shift_high_done"], 1)
                            wait(dve, s["shift_high_done"], n + 1)
                            nc.vector.scalar_tensor_tensor(low, row_max[:, heads, :], -1.0, high, ALU.mult, ALU.subtract).then_inc(s["shift_ready"], 1)
                        elif kind == "finish":
                            j, local = a
                            wait(dve, s["side_done"], side_use(group, local) + 1)
                            ended = side_bank[:].rearrange("p (t h c) -> p t h c", t=TPC, h=GROUP)
                            nc.vector.reciprocal(inverse[:], ended[:, :, :, D1]).then_inc(s["inverse_ready"], 1)
                            wait(dve, s["inverse_ready"], chunk(group, j) + 1)
                            nc.vector.tensor_tensor(by_head(attended, j, group_columns(group, j)), ended[:, :, :, 0:D1],
                                                    inverse[:].unsqueeze(3).broadcast_to([P, TPC, GROUP, D1]),
                                                    ALU.mult).then_inc(s["side_free"], 2)
                groups(dve, run)

            @block.gpsimd
            def _(pool):
                def run(events, group):
                    for kind, *a in events:
                        if kind == "split":
                            j, _ = a
                            n = chunk(group, j)
                            wait(pool, s["q_high_done"], n + 1)
                            nc.gpsimd.tensor_tensor(part(q_slot, j, 2), by_head(qk, j, group_columns(group, j)), part(q_slot, j, 0),
                                                    ALU.subtract).then_inc(s["q_low_done"], 1)
                            wait(pool, s["k_high_done"], n + 1)
                            nc.gpsimd.tensor_tensor(part(k_slot, j, 1), by_head(qk, j, group_columns(group, j, DIM)), part(k_slot, j, 0),
                                                    ALU.subtract).then_inc(s["k_low_done"], 1)
                groups(pool, run)

            @block.scalar
            def _(act):
                act.wait_ge(s["constants_ready"], 3)

                def run(events, group):
                    for kind, *a in events:
                        if kind == "split":
                            j, before = a
                            if before is not None:
                                wait(act, s["side_done"], side_use(group, before) + 1)
                            n = chunk(group, j)
                            nc.scalar.activation(part(q_slot, j, 0).bitcast(F32R), by_head(qk, j, group_columns(group, j)), ACT.Copy)\
                              .then_inc(s["q_high_done"], 1)
                            nc.scalar.activation(part(k_slot, j, 0).bitcast(F32R), by_head(qk, j, group_columns(group, j, DIM)), ACT.Copy)\
                              .then_inc(s["k_high_done"], 1)
                            wait(act, s["q_high_done"], n + 1)
                            nc.scalar.activation(part(q_slot, j, 1), part(q_slot, j, 0), ACT.Copy).then_inc(s["q_copied"], 1)
                            wait(act, s["k_high_done"], n + 1)
                            nc.scalar.activation(part(k_slot, j, 2), part(k_slot, j, 0), ACT.Copy).then_inc(s["k_copied"], 1)
                        elif kind == "split_values":
                            j, = a
                            if j >= NCH or not isinstance(group, int) or group > 0:
                                wait(act, s["values_done"], step_unit(group, j - j % NCH - 1, TPC * (j % NCH) + TPC - 1) + 1)
                            nc.scalar.activation(v_one[:, tiles(j), :, 0:D1], by_head(v, j, group_columns(group, j)), ACT.Copy)\
                              .then_inc(s["v_copied"], 1)
                        elif kind == "place" and not placed_by_vector(a):
                            place(act, group, a, lambda to, of: nc.scalar.activation(to, of, ACT.Copy))
                        elif kind == "scores":
                            j, kt, h, turned = a
                            q0 = max(kt - TPC * j, 0) * P
                            wait(act, s["scores_done"], score_unit(group, j, kt, h) + 1)
                            wait(act, s["values_done"], step_unit(group, j, kt) - 3)
                            nc.scalar.activation(probs[:, kt % 4, h, q0:CH], score_bank[score_place(j, kt, h) % 3][:, q0:CH], ACT.Exp,
                                                 scale=SCALE1).then_inc(s["exp_done"], 1)
                        elif kind == "drain":
                            j, = a
                            wait(act, s["values_done"], step_unit(group, j, key_tiles(j % NCH) - 1) + 1)
                            nc.scalar.activation(out_t[:], out_bank[:], ACT.Copy).then_inc(s["drained"], 1)
                groups(act, run)

            @block.tensor
            def _(pe):
                def turn(slot, j, pair):
                    for i in range(TPC):
                        last = nc.tensor.transpose(side_bank[:, i * P:(i + 1) * P], slot[:, j % 2, i, 2 * pair:2 * pair + 2, :]
                                                   .rearrange("p h c -> p (h c)"), core.ident)
                    last.then_inc(s["side_done"], 1)

                def run(events, group):
                    for kind, *a in events:
                        if kind.startswith("turn") or kind == "finish":
                            wait(pe, s["side_free"], side_use(group, a[-1]) * 2)
                        if kind == "turn_keys":
                            j, pair, local = a
                            wait(pe, s["k_low_done"], chunk(group, j) + 1)
                            wait(pe, s["k_copied"], chunk(group, j) + 1)
                            turn(k_slot, j, pair)
                        elif kind == "turn_queries":
                            j, pair, local = a
                            wait(pe, s["q_low_done"], chunk(group, j) + 1)
                            wait(pe, s["q_copied"], chunk(group, j) + 1)
                            wait(pe, s["zeroed"], chunk(group, j) + 1)
                            turn(q_slot, j, pair)
                        elif kind == "turn_shifted":
                            j, pair, local = a
                            wait(pe, s["shift_ready"], 2 * chunk(group, j) + pair + 1)
                            turn(q_slot, j, pair)
                        elif kind == "maxima":
                            j, h, i, kc, turned = a
                            m = maxima_unit(group, j, h, i, kc)
                            nj = j % NCH
                            if h % 2 == 0 and i == 0 and kc == 0:
                                wait(pe, s["side_free"], 2 * (side_use(group, turned) + 1))
                            wait(pe, s["maxima_taken"], m - 2 if maxima_place(j, h, i, kc) else m)
                            width = (i + 1) * P if kc == nj else CH
                            bank = max_bank[maxima_place(j, h, i, kc) % 3]
                            mm = nc.tensor.matmul(bank[:, 0:width], query[:, j % NCH, h, i * P:(i + 1) * P],
                                                  key[:, h // 2, kc * CH:kc * CH + width], start=True, stop=(kc < nj))
                            if kc == nj:
                                mm = nc.tensor.matmul(bank[:, width - P:width], core.ident_b, core.mask_qk, start=False, stop=True)
                            mm.then_inc(s["maxima_done"], 1)
                        elif kind == "scores":
                            j, kt, h, turned = a
                            u = score_unit(group, j, kt, h)
                            if kt == 0:
                                wait(pe, s["side_free"], 2 * (side_use(group, turned) + 1))
                            wait(pe, s["exp_done"], u - 2 if score_place(j, kt, h) else u)
                            diagonal = kt - TPC * j
                            q0 = max(diagonal, 0) * P
                            bank = score_bank[score_place(j, kt, h) % 3]
                            mm = nc.tensor.matmul(bank[:, q0:CH], key[:, h // 2, kt * P:(kt + 1) * P],
                                                  query[:, j % NCH, h, q0:CH], start=True, stop=(diagonal < 0))
                            if diagonal >= 0:
                                mm = nc.tensor.matmul(bank[:, q0:q0 + P], core.ident_b, core.mask_kq, start=False, stop=True)
                            mm.then_inc(s["scores_done"], 1)
                        elif kind == "values":
                            j, kt, half = a
                            nj = j % NCH
                            q0 = max(kt - TPC * nj, 0) * P
                            wait(pe, s["exp_done"], score_unit(group, j, kt, 2 * half + 1) + 1)
                            if kt % TPC == 0 and kt // TPC == nj and half == 0:
                                wait(pe, s["v_copied"], chunk(group, j) + 1)
                            if kt == 0 and half == 0:
                                wait(pe, s["drained"], chunk(group, j))
                            for h in (2 * half, 2 * half + 1):
                                mm = nc.tensor.matmul(out_bank[32 * h:32 * h + 32, q0:CH], v_one[:, kt, h, :],
                                                      probs[:, kt % 4, h, q0:CH],
                                                      start=(kt == 0), stop=(kt == key_tiles(nj) - 1))
                            if half:
                                mm.then_inc(s["values_done"], 1)
                        elif kind == "finish":
                            j, local = a
                            wait(pe, s["drained"], chunk(group, j) + 1)
                            for i in range(TPC):
                                last = nc.tensor.transpose(side_bank[:, i * P:(i + 1) * P], out_t[:, i * P:(i + 1) * P], core.ident)
                            last.then_inc(s["side_done"], 1)

                pe.wait_ge(s["constants_ready"], 3)
                groups(pe, run)
    core.end_step()


def attention_output(core, attended, w_o_t):
    nc, x = core.nc, core.x
    with ExitStack() as ctx:
        attended_t = core.sb("atto_attended_t", [P, ND, TOKENS], F32, ctx)
        bank = [ctx.enter_context(nc.psum_tensor(f"atto_bank{i}", [P, CH], F32)) for i in range(8)]
        turn = Turn(core, "atto", attended, attended_t, bank[:4], source_complete=True)
        projected, added = core.sem("atto_projected"), core.sem("atto_added")
        with nc.Block() as block:
            @block.vector
            def _(dve):
                turn.vector(dve)
                for b in range(NT // 2):
                    dve.wait_ge(projected, b + 1)
                    pair = x[:, 2 * b:2 * b + 2, :]
                    nc.vector.tensor_tensor(pair, bank[4 + b % 4][:].rearrange("p (t d) -> p t d", d=DIM), pair, ALU.add).then_inc(added, 1)
                dve.wait_ge(added, NT // 2)

            @block.scalar
            def _(act):
                turn.scalar(act)

            @block.tensor
            def _(pe):
                turn.tensor(pe)
                for b in range(NT // 2):
                    turn.wait_chunk(pe, 2 * b // TPC)
                    if b >= 4:
                        pe.wait_ge(added, b - 3)
                    for i in range(2):
                        t = 2 * b + i
                        for k in range(ND):
                            last = nc.tensor.matmul(bank[4 + b % 4][:, i * DIM:(i + 1) * DIM], attended_t[:, k, t * P:(t + 1) * P],
                                                    w_o_t[:, k, :], start=(k == 0), stop=(k == ND - 1))
                    last.then_inc(projected, 1)
    core.end_step()


def macaron_program(nc, inp, out):
    with ExitStack() as ctx:
        core = Core(nc, ctx, inp)
        load_stage(core)
        routed_ffn_stage(core, "ffn_a")
        latent_attention_stage(core)
        routed_ffn_stage(core, "ffn_b")
        mixed_ffn_stage(core, "mix_a")
        attention_stage(core)
        mixed_ffn_stage(core, "mix_b", out)


_INS = ['L0_attn_x', 'L0_attn_w_q_a', 'L0_attn_q_a_ln', 'L0_attn_w_q_b', 'L0_attn_w_kv_a', 'L0_attn_kv_a_ln',
        'L0_attn_w_kv_b', 'L0_attn_w_out', 'L0_ffn_W_r', 'L0_ffn_b_r', 'L0_ffn_W1', 'L0_ffn_b1', 'L0_ffn_W2',
        'L0_ffn_b2', 'L1_attn_Wq', 'L1_attn_Wk', 'L1_attn_Wv', 'L1_attn_Wo', 'L1_ffn_factors', 'L1_ffn_bias']


def kernel(**inputs):
    import concourse.bacc as bacc
    from concourse.bass_utils import run_bass_kernel_spmd

    nc = bacc.Bacc("TRN2", target_bir_lowering=False, num_devices=1)
    arrays = {name: np.ascontiguousarray(inputs[name]) for name in _INS}
    arrays.update(shape_constants())
    aps = {name: nc.dram_tensor(f"in_{name}", a.shape, mybir.dt.from_np(a.dtype), kind="ExternalInput").ap()
           for name, a in arrays.items()}
    out = nc.dram_tensor("out", (1, TOKENS, DIM), F32, kind="ExternalOutput").ap()
    macaron_program(nc, aps, out)
    result = run_bass_kernel_spmd(nc, [{f"in_{name}": a for name, a in arrays.items()}], core_ids=[0])
    return result.results[0]["out"]
```

```python
import numpy as np
from contextlib import ExitStack

import concourse.bass as bass
from concourse import mybir

F32 = mybir.dt.float32
F32R = mybir.dt.float32r
BF16 = mybir.dt.bfloat16
ALU = mybir.AluOpType
ACT = mybir.ActivationFunctionType
AX = mybir.AxisListType

P = 128
TOKENS = 2048
DIM = 256
NT = TOKENS // P
ND = DIM // P
CH = 512
NCH = TOKENS // CH
TPC = CH // P

DFF = 1024
NF = DFF // P
KEPT_BEFORE = 14
SCATTER_BANKS = (0, 4, 1, 5)
CAPACITY = 64

H0 = 16
QL, KL = 192, 64
DN, DR, DV = 128, 64, 128
DQ = DN + DR
SCALE0 = 1.0 / float(np.sqrt(DQ))
RMS_EPS = 1e-6
PAIRS = H0 // 2
KT_PER_PAIR = sum(TPC * (j + 1) for j in range(NCH))

H1, D1 = 16, 16
SCALE1 = 1.0 / float(np.sqrt(DIM))
GROUP = 4
NG = H1 // GROUP
SLOT = 64

RANK = 8
LN_EPS = 1e-5
MASKED = -1e30


def shape_constants():
    eye = np.eye(P, dtype=np.float32)
    row = np.arange(P)
    before = (row[:, None] < row[None, :]).astype(np.float32)
    iota = np.broadcast_to(row.astype(np.float32), (P, P))
    square = np.concatenate([eye, before, iota, np.ones((P, P), np.float32)], axis=1)
    ahead = np.where(row[None, :] > row[:, None], MASKED, 0.0)
    masks = np.concatenate([eye, ahead, ahead.T, np.ones((P, P))], axis=1).astype(np.float32)
    t = np.arange(TOKENS, dtype=np.float32)
    f0 = np.outer(t, (1.0 / 10000.0 ** (np.arange(0, DR, 2, dtype=np.float32) / DR)).astype(np.float32)).astype(np.float32)
    cos0, sin0 = np.cos(f0), np.sin(f0)
    half0 = DR // 2
    col0 = np.zeros((P, 2, TOKENS), np.float32)
    col0[0:DR, 0] = 1.0
    col0[DR:DR + half0, 0], col0[DR + half0:, 0] = cos0.T, cos0.T
    col0[DR:DR + half0, 1], col0[DR + half0:, 1] = sin0.T, -sin0.T
    tok0 = np.stack([cos0, sin0], axis=1).reshape(NT, P, 2, half0).transpose(1, 2, 0, 3)
    half1 = D1 // 2
    f1 = np.outer(t, (1.0 / 10000.0 ** (np.arange(half1, dtype=np.float32) / half1)).astype(np.float32)).astype(np.float32)
    both = np.stack([np.repeat(np.cos(f1), 2, axis=1), np.repeat(np.sin(f1), 2, axis=1)], axis=1)
    tok1 = both.reshape(NT, P, 2, D1).transpose(1, 2, 0, 3)
    return {"c_square": np.ascontiguousarray(square), "c_masks": masks,
            "c_rope0_feature": col0, "c_rope0_token": np.ascontiguousarray(tok0),
            "c_rope1_token": np.ascontiguousarray(tok1)}


class Core:

    def __init__(self, nc, ctx, inp):
        self.nc, self.ctx, self.inp = nc, ctx, inp
        self.step_semaphores = []
        self.mixed_ready = False
        self.x = self.sb("x", [P, NT, DIM], F32)
        self.square = self.sb("square", [P, 4, P], F32)
        self.masks = self.sb("masks", [P, 4, P], BF16)
        self.mixed = self.sb("mixed", [P, ND, DIM], F32)
        self.half_bias = self.sb("half_bias", [P, DIM], F32)
        self.ident = self.square[:, 0, :]
        self.before = self.square[:, 1, :]
        self.iota = self.square[:, 2, :]
        self.ones = self.square[:, 3, :]
        self.ident_b = self.masks[:, 0, :]
        self.mask_qk = self.masks[:, 1, :]
        self.mask_kq = self.masks[:, 2, :]
        self.ones_b = self.masks[:, 3, :]

    def sb(self, name, shape, dt, ctx=None):
        return (ctx or self.ctx).enter_context(self.nc.sbuf_tensor(name, shape, dt))

    def sem(self, name):
        s = self.nc.alloc_semaphore(name)
        self.step_semaphores.append(s)
        return s

    def end_step(self):
        self.nc.clear_and_free_semaphores(self.step_semaphores)
        self.nc.all_engine_barrier()
        self.step_semaphores = []


class Link:

    def __init__(self, core, engine, name):
        self.sem, self.engine, self.n = core.sem(name), engine, 0

    def __call__(self, instruction):
        instruction.then_inc(self.sem, 1)
        self.n += 1
        self.engine.wait_ge(self.sem, self.n)


class Loading:

    def __init__(self, core, ctx):
        self.core, self.inp = core, core.inp
        self.masks = core.sb("masks_whole", [P, 4, P], F32, ctx)
        self.x_loaded = [core.sem(f"x_loaded{c}") for c in range(NCH)]
        self.square_loaded, self.masks_loaded, self.masks_ready = (core.sem(n) for n in ("square_loaded", "masks_loaded", "masks_ready"))
        self.rows = self.inp["L0_attn_x"][0].rearrange("(t p) d -> p t d", p=P)

    def load_x(self, engine, c):
        tiles = slice(TPC * c, TPC * (c + 1))
        engine.dma_start(self.core.x[:, tiles, :], self.rows[:, tiles, :]).then_inc(self.x_loaded[c], 16)

    def sync(self, sp):
        self.load_x(sp, 0)
        sp.dma_start(self.core.square[:], self.inp["c_square"].rearrange("p (a b) -> p a b", b=P)).then_inc(self.square_loaded, 16)
        self.load_x(sp, 2)

    def scalar(self, act):
        self.load_x(act, 1)
        self.load_x(act, 3)
        act.dma_start(self.masks[:], self.inp["c_masks"].rearrange("p (a b) -> p a b", b=P)).then_inc(self.masks_loaded, 16)

    def vector(self, dve):
        dve.wait_ge(self.masks_loaded, 16)
        self.core.nc.vector.tensor_copy(self.core.masks[:], self.masks[:]).then_inc(self.masks_ready, 1)


class Turn:

    def __init__(self, core, tag, source, target, banks, source_complete=False):
        self.core, self.source, self.target, self.banks = core, source, target, banks
        self.source_ready = None if source_complete else core.sem(f"{tag}_source_ready")
        self.turned = core.sem(f"{tag}_turned")
        self.evac_dve = core.sem(f"{tag}_evac_dve")
        self.evac_act = core.sem(f"{tag}_evac_act")

    def place(self, b):
        c, d = divmod(b, ND)
        return self.target[:, d, c * CH:(c + 1) * CH]

    def vector(self, dve):
        for b in range(0, 2 * NCH, 2):
            dve.wait_ge(self.turned, b + 1)
            self.core.nc.vector.tensor_copy(self.place(b), self.banks[b % len(self.banks)][:]).then_inc(self.evac_dve, 1)

    def scalar(self, act):
        for b in range(1, 2 * NCH, 2):
            act.wait_ge(self.turned, b + 1)
            self.core.nc.scalar.activation(self.place(b), self.banks[b % len(self.banks)][:], ACT.Copy).then_inc(self.evac_act, 1)

    def tensor(self, pe):
        nc, n = self.core.nc, len(self.banks)
        for b in range(2 * NCH):
            c, d = divmod(b, ND)
            if self.source_ready is not None:
                pe.wait_ge(self.source_ready, TPC * (c + 1))
            if b >= n:
                pe.wait_ge(self.evac_act if b % 2 else self.evac_dve, (b - n) // 2 + 1)
            for i in range(TPC):
                last = nc.tensor.transpose(self.banks[b % n][:, i * P:(i + 1) * P],
                                           self.source[:, TPC * c + i, d * P:(d + 1) * P], self.core.ident)
            last.then_inc(self.turned, 1)

    def wait_chunk(self, engine, c):
        engine.wait_ge(self.evac_dve, c + 1)
        engine.wait_ge(self.evac_act, c + 1)


class Norm:

    def __init__(self, core, ctx, tag, xn, xn_t, banks, loading=None):
        self.core, self.xn, self.loading = core, xn, loading
        self.stats = core.sb(f"{tag}_stats", [P, NT, 6], F32, ctx)
        self.moments = core.sb(f"{tag}_moments", [P, NT, 2], F32, ctx)
        self.var = core.sb(f"{tag}_var", [P, NT], F32, ctx)
        self.root = core.sb(f"{tag}_root", [P, NT], F32, ctx)
        self.rstd = core.sb(f"{tag}_rstd", [P, NT], F32, ctx)
        self.scratch = core.sb(f"{tag}_scratch", [P, NT], F32, ctx)
        self.var_ready = core.sem(f"{tag}_var_ready")
        self.root_ready = core.sem(f"{tag}_root_ready")
        self.turn = Turn(core, tag, xn, xn_t, banks)
        self.xn_ready = self.turn.source_ready

    def vector(self, dve, link):
        nc, x = self.core.nc, self.core.x
        for t in range(NT):
            if self.loading and t % TPC == 0:
                dve.wait_ge(self.loading.x_loaded[t // TPC], 16)
            s = nc.vector.bn_stats(self.stats[:, t, :], x[:, t, :])
        link(s)
        for t in range(NT):
            s = nc.vector.bn_aggr(self.moments[:, t, :], self.stats[:, t, :])
        link(s)
        nc.vector.tensor_scalar(self.var[:], self.moments[:, :, 1], LN_EPS, None, ALU.add).then_inc(self.var_ready, 1)
        dve.wait_ge(self.root_ready, 1)
        reciprocal_of_root(nc, link, self.rstd[:], self.root[:], self.var[:], self.scratch[:])
        for t in range(NT):
            nc.vector.tensor_scalar(self.xn[:, t, :], x[:, t, :], self.moments[:, t, 0:1], self.rstd[:, t:t + 1],
                                    ALU.subtract, ALU.mult).then_inc(self.xn_ready, 1)
        self.turn.vector(dve)

    def scalar(self, act):
        act.wait_ge(self.var_ready, 1)
        self.core.nc.scalar.activation(self.root[:], self.var[:], ACT.Sqrt).then_inc(self.root_ready, 1)
        self.turn.scalar(act)

    def tensor(self, pe):
        if self.loading:
            pe.wait_ge(self.loading.square_loaded, 16)
        self.turn.tensor(pe)


def reciprocal_of_root(nc, link, out, root, value, scratch):
    link(nc.vector.reciprocal(out, root))
    link(nc.vector.tensor_tensor(scratch, out, out, ALU.mult))
    link(nc.vector.tensor_tensor(scratch, scratch, value, ALU.mult))
    link(nc.vector.tensor_scalar(scratch, scratch, -0.5, 1.5, ALU.mult, ALU.add))
    link(nc.vector.tensor_tensor(out, out, scratch, ALU.mult))


def routed_ffn_stage(core, tag, first=False):
    nc, inp, x = core.nc, core.inp, core.x
    with ExitStack() as ctx:
        def sb(name, shape, dt=F32):
            return core.sb(f"{tag}_{name}", shape, dt, ctx)
        xn, xn_t = sb("xn", [P, NT, DIM]), sb("xn_t", [P, ND, TOKENS])
        w_r, w_r_wide = sb("w_r", [P, ND]), sb("w_r_wide", [P, ND, P])
        b_r = sb("b_r", [P, 1])
        w1, w2 = sb("w1", [P, ND, DFF]), sb("w2", [P, NF, DIM])
        b1, b2 = sb("b1", [P, NF]), sb("b2", [P, DIM])
        weight_row = sb("weight_row", [P, TOKENS])
        weight = sb("weight", [P, NT])
        not_above = sb("not_above", [P, 3, TOKENS], BF16)
        chosen, keep_scale, take_scale = sb("chosen", [P, NT]), sb("keep_scale", [P, NT]), sb("take_scale", [P, NT])
        ranks = sb("ranks", [P, 3, NT])
        onehot, onehot_t = sb("onehot", [P, NT, P]), sb("onehot_t", [P, NT, P])
        picked_t = sb("picked_t", [P, ND, P])
        hidden = sb("hidden", [P, NF, P])
        block_out = sb("block_out", [P, DIM])
        table_scratch = sb("table_scratch", [P, 1])
        bank = [ctx.enter_context(nc.psum_tensor(f"{tag}_bank{i}", [P, CH], F32)) for i in range(8)]
        loading = Loading(core, ctx) if first else None
        norm = Norm(core, ctx, tag, xn, xn_t, bank, loading)
        names = ("weights_loaded ffn_loaded wide_ready weight_bank row_ready weight_turned compared counted chosen_ready"
                 " prefix_done onehot_ready picked_done picked_t_ready hidden_done"
                 " hidden_ready block_done block_ready onehot_turned onehot_t_act onehot_t_dve scattered added").split()
        s = {n: core.sem(f"{tag}_{n}") for n in names}

        with nc.Block() as block:
            @block.sync
            def _(sp):
                if first:
                    loading.sync(sp)
                sp.dma_start(w_r[:], inp["L0_ffn_W_r"].rearrange("(k p) o -> p (k o)", p=P),
                             allow_slow_non_contiguous=True).then_inc(s["weights_loaded"], 16)
                sp.dma_start(b_r[:], inp["L0_ffn_b_r"].partition_broadcast(P)).then_inc(s["weights_loaded"], 16)
                sp.dma_start(w1[:], inp["L0_ffn_W1"].rearrange("(k p) f -> p k f", p=P)).then_inc(s["ffn_loaded"], 16)
                sp.dma_start(w2[:], inp["L0_ffn_W2"].rearrange("(k p) d -> p k d", p=P)).then_inc(s["ffn_loaded"], 16)
                sp.dma_start(b1[:], inp["L0_ffn_b1"].rearrange("(k p) -> p k", p=P),
                             allow_slow_non_contiguous=True).then_inc(s["ffn_loaded"], 16)
                sp.dma_start(b2[:], inp["L0_ffn_b2"].partition_broadcast(P)).then_inc(s["ffn_loaded"], 16)

            @block.vector
            def _(dve):
                link = Link(core, dve, f"{tag}_dve_link")
                norm.vector(dve, link)
                dve.wait_ge(s["weights_loaded"], 32)
                nc.vector.tensor_copy(w_r_wide[:], w_r[:].unsqueeze(2).broadcast_to([P, ND, P])).then_inc(s["wide_ready"], 1)
                if first:
                    loading.vector(dve)
                    dve.wait_ge(loading.square_loaded, 16)
                for c in range(NCH):
                    dve.wait_ge(s["weight_turned"], c + 1)
                    w = nc.vector.tensor_copy(weight[:, TPC * c:TPC * (c + 1)],
                                              bank[4 + c][:].rearrange("p (t q) -> p t q", q=P)[:, :, 0])
                link(w)
                for t in range(NT):
                    if t >= 3:
                        dve.wait_ge(s["counted"], t - 2)
                    nc.vector.tensor_scalar(not_above[:, t % 3], weight_row[:], weight[:, t:t + 1], None,
                                            ALU.is_le).then_inc(s["compared"], 1)
                dve.wait_ge(s["counted"], NT)
                nc.vector.tensor_scalar(chosen[:], bank[0][:, 0:NT], CAPACITY - 0.5, None, ALU.is_lt).then_inc(s["chosen_ready"], 1)
                dve.wait_ge(s["chosen_ready"], 1)
                nc.vector.tensor_scalar(keep_scale[:], chosen[:], -0.5, 0.5, ALU.mult, ALU.add)
                link(nc.vector.tensor_scalar(take_scale[:], weight[:], 0.5, None, ALU.mult))
                dve.wait_ge(s["prefix_done"], 1)
                link(nc.vector.memset(ranks[:, 0, 0:1], 0.0))
                link(nc.vector.tensor_copy(ranks[:, 0, 1:NT], bank[1][:, 0:NT - 1]))
                src = 0
                for step in (1, 2, 4, 8):
                    link(nc.vector.tensor_copy(ranks[:, 1 - src, 0:step], ranks[:, src, 0:step]))
                    link(nc.vector.tensor_tensor(ranks[:, 1 - src, step:NT], ranks[:, src, step:NT],
                                                 ranks[:, src, 0:NT - step], ALU.add))
                    src = 1 - src
                link(nc.vector.tensor_tensor(ranks[:, 2, :], bank[0][:, 0:NT], ranks[:, src, :], ALU.add))
                for t in range(NT):
                    nc.vector.tensor_scalar(onehot[:, t, :], core.iota, ranks[:, 2, t:t + 1], chosen[:, t:t + 1],
                                            ALU.is_equal, ALU.mult).then_inc(s["onehot_ready"], 1)
                for t in range(NT):
                    kept = nc.vector.scalar_tensor_tensor(x[:, t, :], xn[:, t, :], keep_scale[:, t:t + 1], x[:, t, :],
                                                          ALU.mult, ALU.add)
                    if t == KEPT_BEFORE - 1:
                        dve.wait_ge(s["picked_done"], 1)
                        for k in range(ND):
                            last = nc.vector.tensor_copy(picked_t[:, k], bank[2 + k][:, 0:P])
                        last.then_inc(s["picked_t_ready"], 1)
                link(kept)
                for c in range(0, NCH, 2):
                    dve.wait_ge(s["onehot_turned"], c + 1)
                    nc.vector.tensor_copy(onehot_t[:, TPC * c:TPC * (c + 1), :],
                                          bank[4 + c][:].rearrange("p (t q) -> p t q", q=P)).then_inc(s["onehot_t_dve"], 1)
                dve.wait_ge(s["block_done"], 1)
                dve.wait_ge(s["ffn_loaded"], 64)
                nc.vector.tensor_tensor(block_out[:], bank[2][:, 0:DIM], b2[:], ALU.add).then_inc(s["block_ready"], 1)
                for t in range(NT):
                    dve.wait_ge(s["scattered"], t // 2 + 1)
                    half = bank[SCATTER_BANKS[t // 2 % 4]][:, (t % 2) * DIM:(t % 2 + 1) * DIM]
                    nc.vector.scalar_tensor_tensor(x[:, t, :], half, take_scale[:, t:t + 1], x[:, t, :],
                                                   ALU.mult, ALU.add).then_inc(s["added"], 1)
                dve.wait_ge(s["added"], NT)

            @block.scalar
            def _(act):
                if first:
                    loading.scalar(act)
                norm.scalar(act)
                act.wait_ge(s["weights_loaded"], 32)
                for c in range(NCH):
                    act.wait_ge(s["weight_bank"], c + 1)
                    nc.scalar.activation(weight_row[:, c * CH:(c + 1) * CH], bank[c][:], ACT.Identity,
                                         bias=b_r[:, 0:1]).then_inc(s["row_ready"], 1)
                act.wait_ge(s["ffn_loaded"], 64)
                nc.scalar.activation(table_scratch[:], b1[:, 0:1], ACT.Gelu_apprx_tanh)
                for h in range(2):
                    act.wait_ge(s["hidden_done"], h + 1)
                    for i in range(TPC):
                        f = TPC * h + i
                        nc.scalar.activation(hidden[:, f, :], bank[h][:, i * P:(i + 1) * P], ACT.Gelu_apprx_tanh,
                                             bias=b1[:, f:f + 1]).then_inc(s["hidden_ready"], 1)
                for c in range(1, NCH, 2):
                    act.wait_ge(s["onehot_turned"], c + 1)
                    nc.scalar.activation(onehot_t[:, TPC * c:TPC * (c + 1), :],
                                         bank[4 + c][:].rearrange("p (t q) -> p t q", q=P), ACT.Copy).then_inc(s["onehot_t_act"], 1)

            @block.tensor
            def _(pe):
                norm.tensor(pe)
                pe.wait_ge(s["wide_ready"], 1)
                for c in range(NCH):
                    norm.turn.wait_chunk(pe, c)
                    for k in range(ND):
                        last = nc.tensor.matmul(bank[c][:], w_r_wide[:, k, :], xn_t[:, k, c * CH:(c + 1) * CH],
                                                start=(k == 0), stop=(k == ND - 1))
                    last.then_inc(s["weight_bank"], 1)
                for c in range(NCH):
                    pe.wait_ge(s["row_ready"], c + 1)
                    for i in range(TPC):
                        last = nc.tensor.transpose(bank[4 + c][:, i * P:(i + 1) * P],
                                                   weight_row[:, c * CH + i * P:c * CH + (i + 1) * P], core.ident)
                    last.then_inc(s["weight_turned"], 1)
                if first:
                    pe.wait_ge(loading.masks_ready, 1)
                for t in range(NT):
                    pe.wait_ge(s["compared"], t + 1)
                    for i in range(NT):
                        last = nc.tensor.matmul(bank[0][:, i:i + 1], not_above[:, t % 3, i * P:(i + 1) * P], core.ones_b[:, 0:1],
                                                start=(t == 0 and i == 0), stop=(t == NT - 1 and i == NT - 1))
                    last.then_inc(s["counted"], 1)
                pe.wait_ge(s["chosen_ready"], 1)
                nc.tensor.matmul(bank[0][:, 0:NT], core.before, chosen[:], start=True, stop=True)
                nc.tensor.matmul(bank[1][:, 0:NT], core.ones, chosen[:], start=True, stop=True).then_inc(s["prefix_done"], 1)
                for t in range(NT):
                    pe.wait_ge(s["onehot_ready"], t + 1)
                    for k in range(ND):
                        last = nc.tensor.matmul(bank[2 + k][:, 0:P], xn[:, t, k * P:(k + 1) * P], onehot[:, t, :],
                                                start=(t == 0), stop=(t == NT - 1))
                last.then_inc(s["picked_done"], 1)
                for c in range(NCH):
                    for i in range(TPC):
                        last = nc.tensor.transpose(bank[4 + c][:, i * P:(i + 1) * P], onehot[:, TPC * c + i, :], core.ident)
                    last.then_inc(s["onehot_turned"], 1)
                pe.wait_ge(s["picked_t_ready"], 1)
                pe.wait_ge(s["ffn_loaded"], 64)
                for h in range(2):
                    for i in range(TPC):
                        f = TPC * h + i
                        for k in range(ND):
                            last = nc.tensor.matmul(bank[h][:, i * P:(i + 1) * P], w1[:, k, f * P:(f + 1) * P], picked_t[:, k, :],
                                                    start=(k == 0), stop=(k == ND - 1))
                    last.then_inc(s["hidden_done"], 1)
                for f in range(NF):
                    pe.wait_ge(s["hidden_ready"], f + 1)
                    last = nc.tensor.matmul(bank[2][:, 0:DIM], hidden[:, f, :], w2[:, f, :], start=(f == 0), stop=(f == NF - 1))
                last.then_inc(s["block_done"], 1)
                pe.wait_ge(s["block_ready"], 1)
                pe.wait_ge(s["onehot_t_dve"], 2)
                pe.wait_ge(s["onehot_t_act"], 2)
                for t in range(NT):
                    if t >= 8 and t % 2 == 0:
                        pe.wait_ge(s["added"], t - 6)
                    last = nc.tensor.matmul(bank[SCATTER_BANKS[t // 2 % 4]][:, (t % 2) * DIM:(t % 2 + 1) * DIM], onehot_t[:, t, :], block_out[:],
                                            start=True, stop=True)
                    if t % 2:
                        last.then_inc(s["scattered"], 1)
    core.end_step()


def mixed_ffn_stage(core, tag, out=None):
    nc, x, inp = core.nc, core.x, core.inp
    with ExitStack() as ctx:
        first = not core.mixed_ready
        core.mixed_ready = True
        factors = core.sb(f"{tag}_factors", [P, RANK, ND, DIM], F32, ctx) if first else None
        xn = core.sb(f"{tag}_xn", [P, NT, DIM], F32, ctx)
        xn_t = core.sb(f"{tag}_xn_t", [P, ND, TOKENS], F32, ctx)
        bank = [ctx.enter_context(nc.psum_tensor(f"{tag}_bank{i}", [P, CH], F32)) for i in range(8)]
        norm = Norm(core, ctx, tag, xn, xn_t, bank[:4])
        mixed_done, added, stored = (core.sem(f"{tag}_{n}") for n in ("mixed_done", "added", "stored"))
        factors_loaded, bias_loaded, summed = (core.sem(f"{tag}_{n}") for n in ("factors_loaded", "bias_loaded", "summed"))
        with nc.Block() as block:
            @block.gpsimd
            def _(pool):
                if first:
                    for r in range(1, RANK):
                        pool.wait_ge(factors_loaded, 16 * RANK)
                        earlier = factors[:, 0] if r == 1 else core.mixed[:]
                        if r > 1:
                            pool.wait_ge(summed, r - 1)
                        nc.gpsimd.tensor_tensor(core.mixed[:], earlier, factors[:, r], ALU.add).then_inc(summed, 1)

            @block.vector
            def _(dve):
                norm.vector(dve, Link(core, dve, f"{tag}_dve_link"))
                if first:
                    dve.wait_ge(bias_loaded, 16)
                    nc.vector.tensor_scalar(core.half_bias[:], core.half_bias[:], 0.5, None, ALU.mult).then_inc(bias_loaded, 1)
                    dve.wait_ge(bias_loaded, 17)
                dve.wait_ge(norm.xn_ready, NT)
                bias = core.half_bias[:].unsqueeze(1).broadcast_to([P, NT // 2, DIM])
                link = Link(core, dve, f"{tag}_biased")
                for h in range(2):
                    tiles = x[:, h * NT // 2:(h + 1) * NT // 2, :]
                    last = nc.vector.tensor_tensor(tiles, tiles, bias, ALU.add)
                link(last)
                for b in range(NT // 2):
                    dve.wait_ge(mixed_done, b + 1)
                    pair = x[:, 2 * b:2 * b + 2, :]
                    nc.vector.scalar_tensor_tensor(pair, bank[4 + b % 4][:].rearrange("p (t d) -> p t d", d=DIM),
                                                   0.5 / float(np.sqrt(RANK)), pair, ALU.mult, ALU.add).then_inc(added, 1)
                dve.wait_ge(added, NT // 2)

            @block.scalar
            def _(act):
                norm.scalar(act)

            @block.tensor
            def _(pe):
                norm.tensor(pe)
                if first:
                    pe.wait_ge(summed, RANK - 1)
                for b in range(NT // 2):
                    norm.turn.wait_chunk(pe, 2 * b // TPC)
                    if b >= 4:
                        pe.wait_ge(added, b - 3)
                    for i in range(2):
                        t = 2 * b + i
                        for k in range(ND):
                            last = nc.tensor.matmul(bank[4 + b % 4][:, i * DIM:(i + 1) * DIM], xn_t[:, k, t * P:(t + 1) * P],
                                                    core.mixed[:, k, :], start=(k == 0), stop=(k == ND - 1))
                    last.then_inc(mixed_done, 1)

            @block.sync
            def _(sp):
                if first:
                    for r in range(RANK):
                        sp.dma_start(factors[:, r], inp["L1_ffn_factors"][r].rearrange("(k p) e -> p k e", p=P)).then_inc(factors_loaded, 16)
                    sp.dma_start(core.half_bias[:], inp["L1_ffn_bias"].partition_broadcast(P)).then_inc(bias_loaded, 16)
                if out is not None:
                    rows = out[0].rearrange("(t p) d -> p t d", p=P)
                    for b in range(0, NT // 2, 2):
                        sp.wait_ge(added, b + 2)
                        sp.dma_start(rows[:, 2 * b:2 * b + 4, :], x[:, 2 * b:2 * b + 4, :]).then_inc(stored, 16)
                    sp.wait_ge(stored, 16 * (NT // 4))
    core.end_step()


def wait(engine, sem, value):
    if not isinstance(value, int) or value > 0:
        engine.wait_ge(sem, value)


class QueryLatents:

    def __init__(self, hi, lo, rest):
        self.hi, self.lo, self.rest = hi, lo, rest


def latent_attention_stage(core):
    with ExitStack() as ctx:
        def sb(name, shape, dt=F32):
            return core.sb(f"lat_{name}", shape, dt, ctx)
        qa_t = QueryLatents(sb("qa_hi", [P, TOKENS], F32R), sb("qa_lo", [P, TOKENS], F32R), sb("qa_rest", [P, TOKENS], F32R))
        key_hi, key_lo = sb("key_hi", [P, TOKENS], F32R), sb("key_lo", [P, TOKENS], F32R)
        latent = sb("latent", [P, NT, P])
        rope = sb("rope", [P, 2, TOKENS])
        raw = (sb("raw_q", [P, 2, 2 * DQ]), sb("raw_kv", [P, 2 * (DN + DV)]), sb("raw_out", [P, 2, DIM]))
        latent_projections(core, qa_t, key_hi, key_lo, latent, rope, raw)
        latent_heads(core, qa_t, key_hi, key_lo, latent, rope, raw)


def latent_projections(core, qa_t, key_hi, key_lo, latent, rope_feature, raw):
    nc, inp = core.nc, core.inp
    W = QL + KL + DR
    with ExitStack() as ctx:
        def sb(name, shape, dt=F32):
            return core.sb(f"latp_{name}", shape, dt, ctx)
        xn, xn_t = sb("xn", [P, NT, DIM]), sb("xn_t", [P, ND, TOKENS])
        w_down = sb("w_down", [P, ND, W])
        q_ln, kv_ln = sb("q_ln", [P, QL]), sb("kv_ln", [P, KL])
        rope = sb("rope", [P, 2, NT, DR // 2])
        down = sb("down", [P, NT, W])
        squares = sb("squares", [P, 2, QL])
        sums, mean_sq, root, rstd, scratch = (sb(n, [P, NT, 2]) for n in ("sums", "mean_sq", "root", "rstd", "scratch"))
        part = [sb(f"part{i}", [P, NT, DR // 2]) for i in range(4)]
        bank = [ctx.enter_context(nc.psum_tensor(f"latp_bank{i}", [P, CH], F32)) for i in range(8)]
        norm = Norm(core, ctx, "latn", xn, xn_t, bank[:4])
        names = ("loaded heads_loaded down_done down_copied squared mean_ready root_ready q_scaled latent_ready key_turned"
                 " key_hi_done key_lo_done q_turned q_turned_2 q_copied q_copied_2 q_low_done").split()
        s = {n: core.sem(f"latp_{n}") for n in names}
        with nc.Block() as block:
            @block.sync
            def _(sp):
                sp.dma_start(w_down[:, :, 0:QL], inp["L0_attn_w_q_a"].rearrange("(k p) e -> p k e", p=P)).then_inc(s["loaded"], 16)
                sp.dma_start(w_down[:, :, QL:W], inp["L0_attn_w_kv_a"].rearrange("(k p) e -> p k e", p=P)).then_inc(s["loaded"], 16)
                sp.dma_start(q_ln[:], inp["L0_attn_q_a_ln"].partition_broadcast(P)).then_inc(s["loaded"], 16)
                sp.dma_start(kv_ln[:], inp["L0_attn_kv_a_ln"].partition_broadcast(P)).then_inc(s["loaded"], 16)
                sp.dma_start(rope[:], inp["c_rope0_token"]).then_inc(s["loaded"], 16)
                raw_q, raw_kv, raw_out = raw
                sp.dma_start(raw_q[:, 0, :], inp["L0_attn_w_q_b"][0:P, 0:2 * DQ]).then_inc(s["heads_loaded"], 16)
                sp.dma_start(raw_q[0:QL - P, 1, :], inp["L0_attn_w_q_b"][P:QL, 0:2 * DQ]).then_inc(s["heads_loaded"], 16)
                sp.dma_start(raw_kv[0:KL, :], inp["L0_attn_w_kv_b"][:, 0:2 * (DN + DV)]).then_inc(s["heads_loaded"], 16)
                sp.dma_start(raw_out[:], inp["L0_attn_w_out"][0:2 * DV, :].rearrange("(h p) e -> p h e", p=P)).then_inc(s["heads_loaded"], 16)
                sp.dma_start(rope_feature[:], inp["c_rope0_feature"]).then_inc(s["heads_loaded"], 16)
                sp.wait_ge(s["heads_loaded"], 80)

            @block.vector
            def _(dve):
                link = Link(core, dve, "latp_link")
                norm.vector(dve, link)
                for t in range(NT):
                    dve.wait_ge(s["down_done"], t + 1)
                    nc.vector.tensor_copy(down[:, t, :], bank[4 + t % 4][:, 0:W]).then_inc(s["down_copied"], 1)
                dve.wait_ge(s["loaded"], 80)
                dve.wait_ge(s["down_copied"], NT)
                even, odd = down[:, :, QL + KL:W:2], down[:, :, QL + KL + 1:W:2]
                cos, sin = rope[:, 0], rope[:, 1]
                for out, a, b in zip(part, (even, odd, odd, even), (cos, sin, cos, sin)):
                    last = nc.vector.tensor_tensor(out[:], a, b, ALU.mult)
                link(last)
                half = DR // 2
                nc.vector.tensor_tensor(latent[:, :, KL:KL + half], part[0][:], part[1][:], ALU.subtract)
                nc.vector.tensor_tensor(latent[:, :, KL + half:P], part[2][:], part[3][:], ALU.add)
                dve.wait_ge(s["squared"], 2 * NT)
                for i, width in enumerate((QL, KL)):
                    mean = nc.vector.tensor_scalar(mean_sq[:, :, i], sums[:, :, i], 1.0 / width, RMS_EPS, ALU.mult, ALU.add)
                mean.then_inc(s["mean_ready"], 1)
                dve.wait_ge(s["root_ready"], 1)
                reciprocal_of_root(nc, link, rstd[:], root[:], mean_sq[:], scratch[:])
                for t in range(NT):
                    nc.vector.scalar_tensor_tensor(latent[:, t, 0:KL], down[:, t, QL:QL + KL], rstd[:, t, 1:2], kv_ln[:],
                                                   ALU.mult, ALU.mult).then_inc(s["latent_ready"], 1)
                for t in range(NT):
                    nc.vector.scalar_tensor_tensor(down[:, t, 0:QL], down[:, t, 0:QL], rstd[:, t, 0:1], q_ln[:],
                                                   ALU.mult, ALU.mult).then_inc(s["q_scaled"], 1)
                for c in range(NCH):
                    dve.wait_ge(s["key_hi_done"], c + 1)
                    cols = slice(c * CH, (c + 1) * CH)
                    nc.vector.tensor_tensor(key_lo[:, cols], bank[c][:], key_hi[:, cols].bitcast(F32),
                                            ALU.subtract).then_inc(s["key_lo_done"], 1)
                for c in range(NCH):
                    cols = slice(c * CH, (c + 1) * CH)
                    dve.wait_ge(s["q_copied"], c + 1)
                    nc.vector.tensor_tensor(qa_t.lo[:, cols], bank[4 + c][:], qa_t.hi[:, cols].bitcast(F32), ALU.subtract)\
                      .then_inc(s["q_low_done"], 1)
                for c in range(NCH):
                    cols = slice(c * CH, (c + 1) * CH)
                    dve.wait_ge(s["q_copied_2"], c + 1)
                    nc.vector.tensor_tensor(qa_t.rest[64:P, cols], bank[c][0:64, :], qa_t.rest[0:64, cols].bitcast(F32), ALU.subtract)\
                      .then_inc(s["q_low_done"], 1)
                dve.wait_ge(s["q_low_done"], 2 * NCH)

            @block.scalar
            def _(act):
                norm.scalar(act)
                for t in range(NT):
                    act.wait_ge(s["down_copied"], t + 1)
                    if t >= 1:
                        act.wait_ge(s["squared"], 2 * t)
                    nc.scalar.activation(squares[:, 0, 0:QL], down[:, t, 0:QL], ACT.Square,
                                         accum_out=sums[:, t, 0:1]).then_inc(s["squared"], 1)
                    nc.scalar.activation(squares[:, 1, 0:KL], down[:, t, QL:QL + KL], ACT.Square,
                                         accum_out=sums[:, t, 1:2]).then_inc(s["squared"], 1)
                act.wait_ge(s["mean_ready"], 1)
                nc.scalar.activation(root[:], mean_sq[:], ACT.Sqrt).then_inc(s["root_ready"], 1)
                for c in range(NCH):
                    act.wait_ge(s["key_turned"], c + 1)
                    nc.scalar.activation(key_hi[:, c * CH:(c + 1) * CH], bank[c][:], ACT.Copy).then_inc(s["key_hi_done"], 1)
                for c in range(NCH):
                    act.wait_ge(s["q_turned"], c + 1)
                    nc.scalar.activation(qa_t.hi[:, c * CH:(c + 1) * CH], bank[4 + c][:], ACT.Copy).then_inc(s["q_copied"], 1)
                for c in range(NCH):
                    act.wait_ge(s["q_turned_2"], c + 1)
                    nc.scalar.activation(qa_t.rest[0:64, c * CH:(c + 1) * CH], bank[c][0:64, :], ACT.Copy).then_inc(s["q_copied_2"], 1)
                act.wait_ge(s["q_copied_2"], NCH)

            @block.tensor
            def _(pe):
                norm.tensor(pe)
                pe.wait_ge(s["loaded"], 80)
                for t in range(NT):
                    norm.turn.wait_chunk(pe, t // TPC)
                    if t >= 4:
                        pe.wait_ge(s["down_copied"], t - 3)
                    for k in range(ND):
                        last = nc.tensor.matmul(bank[4 + t % 4][:, 0:W], xn_t[:, k, t * P:(t + 1) * P], w_down[:, k, :],
                                                start=(k == 0), stop=(k == ND - 1))
                    last.then_inc(s["down_done"], 1)
                for c in range(NCH):
                    pe.wait_ge(s["latent_ready"], TPC * (c + 1))
                    for i in range(TPC):
                        last = nc.tensor.transpose(bank[c][:, i * P:(i + 1) * P], latent[:, TPC * c + i, :], core.ident)
                    last.then_inc(s["key_turned"], 1)
                pe.wait_ge(s["down_copied"], NT)
                for c in range(NCH):
                    pe.wait_ge(s["q_scaled"], TPC * (c + 1))
                    for i in range(TPC):
                        last = nc.tensor.transpose(bank[4 + c][:, i * P:(i + 1) * P], down[:, TPC * c + i, 0:P], core.ident)
                    last.then_inc(s["q_turned"], 1)
                for c in range(NCH):
                    pe.wait_ge(s["key_lo_done"], c + 1)
                    for i in range(TPC):
                        last = nc.tensor.transpose(bank[c][0:QL - P, i * P:(i + 1) * P], down[:, TPC * c + i, P:QL], core.ident)
                    last.then_inc(s["q_turned_2"], 1)
    core.end_step()


def key_tiles(j):
    return TPC * (j + 1)


STEPS_BEFORE = [sum(key_tiles(i) for i in range(j)) for j in range(NCH)]


def in_chunk(event, j, to):
    at = event.index(j, 1)
    return (*event[:at], to, *event[at + 1:])


LATENT_MAXIMA_STEPS = [(-12.0, -2.0), (0.2, 3.15), (3.5, 11.25), (12.2, 22.7)]
LATENT_QUERY_STEPS = [(-21.0, -18.0), (-15.0, -13.0), (-5.8, -2.5), (8.5, 10.4)]
FIRST_QUERY_STEPS = [(-21.0, -20.6), (-17.0, -15.9), (-6.0, -5.6), (8.5, 10.5)]
SUMS_STEPS = (0.5, 1.0, 1.5, 2.35, 3.5)
FIRST_HEAD_SHARE = (0.5, 0.5, 0.5, 0.5)
SPREAD_AFTER = [(0.5, 0.5), (0.25, 0.25), (0.3, 0.3), (0.5, 0.5)]
WEIGHT_STEPS = (-25.9, -25.3, -23.0, 5.85)
QUERY_AFTER = (0.3, 0.9, 1.7)
LATENT_LAG = 2
PROB_SLOTS = 5


def latent_preparation(query_steps=LATENT_QUERY_STEPS):
    out = []

    def on_tensor(step, kind, j, *rest, after=0.5):
        out.extend([(step, j, (kind, j, *rest)), (step + after, j, (kind + "_out", j, *rest))])

    on_tensor(WEIGHT_STEPS[0], "turn_q_weights", 0)
    on_tensor(WEIGHT_STEPS[1], "turn_kv_weights", 0)
    on_tensor(WEIGHT_STEPS[2], "fold_query", 0)
    out += [(WEIGHT_STEPS[2] + 0.7, 0, ("split_weights", 0)), (WEIGHT_STEPS[2] + 1.2, 0, ("split_weights_low", 0))]
    on_tensor(WEIGHT_STEPS[3], "fold_out", 0)
    for j in range(NCH):
        for h in range(2):
            at = query_steps[j][h]
            on_tensor(at, "query", j, h, after=QUERY_AFTER[0])
            out += [(at + QUERY_AFTER[1], j, ("rotate", j, h)), (at + QUERY_AFTER[2], j, ("split", j, h))]
        start, end = LATENT_MAXIMA_STEPS[j]
        main = [[("maxima", j, h, i, kc) for i in range(TPC) for kc in range(j + 1)] for h in range(2)]
        middle = start + FIRST_HEAD_SHARE[j] * (end - start)
        for h, (begun, done) in enumerate(((start, middle), (middle, end))):
            out += [(begun + n * (done - begun) / len(main[h]), j, event) for n, event in enumerate(main[h])]
            out.append((done - 0.01, j, ("shift", j, h)))
            on_tensor(done + SPREAD_AFTER[j][h], "spread", j, h, after=0.3)
        done = (STEPS_BEFORE[j] + key_tiles(j)) % KT_PER_PAIR + LATENT_LAG
        m = j if j < NCH - 1 else -1
        on_tensor(done + SUMS_STEPS[0], "sums", m, after=0.3)
        on_tensor(done + SUMS_STEPS[1], "turn_sums", m, after=0.3)
        on_tensor(done + SUMS_STEPS[2], "spread_inverse", m, after=0.3)
        for n in range(2):
            on_tensor(done + SUMS_STEPS[3 + n], "project", m, n, after=0.3)
    return sorted(out, key=lambda e: e[0])


def latent_schedule(first, last):
    placed = []
    for step, _, event in latent_preparation():
        j = event[1]
        if step >= 0 and not (first and j < 0):
            placed.append((step, event))
        elif step < 0 and not last:
            placed.append((step + KT_PER_PAIR, in_chunk(event, j, j + NCH)))
    placed.sort(key=lambda e: e[0])
    events = []
    for j in range(NCH):
        for kt in range(key_tiles(j)):
            lag = LATENT_LAG
            follow = (j, kt - lag) if kt >= lag else (j - 1, key_tiles((j - 1) % NCH) - lag + kt)
            atoms = [[("scores", j, kt, 0)], [("scores", j, kt, 1)], []]
            if not (first and j == 0 and kt < lag):
                for h in range(2):
                    atoms[1 + h].append(("values", *follow, h))
                if kt == lag - 1:
                    atoms[2].append(("drain", j - 1))
            for n, atom in enumerate(atoms):
                events += atom
                while placed and placed[0][0] < STEPS_BEFORE[j] + kt + (n + 1) / len(atoms):
                    events.append(placed.pop(0)[1])
    return events + [event for _, event in placed]


LATENT_PROLOGUE = [event for step, _, event in latent_preparation(FIRST_QUERY_STEPS) if step < 0]
LATENT_EPILOGUE = ([("values", -1, key_tiles(NCH - 1) - LATENT_LAG + i, h) for i in range(LATENT_LAG) for h in range(2)] + [("drain", -1)]
                   + [(kind + out, -1) for kind in ("sums", "turn_sums", "spread_inverse") for out in ("", "_out")]
                   + [("project" + out, -1, n) for n in range(2) for out in ("", "_out")])
ON_SIDE = ("turn_q_weights", "turn_kv_weights", "fold_query", "fold_out", "query", "spread")
LATENT_SIDE_PER_PAIR = sum(event[0] in ON_SIDE for _, _, event in latent_preparation())
LATENT_SIDE_BEFORE = sum(event[0] in ON_SIDE for event in LATENT_PROLOGUE)


def with_latent_uses(events, start, earlier=()):
    out, uses = [], dict(earlier)
    for e in events:
        if e[0] in ON_SIDE:
            uses[e] = start
            e, start = (*e, start), start + 1
        elif e[0][-4:] == "_out" and e[0][:-4] in ON_SIDE:
            e = (*e, uses[(e[0][:-4], *e[1:])])
        elif e[0] == "split_weights":
            e = (*e, uses["fold_query", e[1]])
        elif e[0] == "rotate":
            e = (*e, uses["query", e[1], e[2]])
        elif e[0] == "scores":
            e = (*e, uses["spread", e[1], e[3]])
        out.append(e)
    return out, {in_chunk(e, e[1], e[1] - NCH): use - LATENT_SIDE_PER_PAIR for e, use in uses.items()}


def latent_heads(core, qa_t, key_hi, key_lo, latent, rope, raw):
    nc, inp, x = core.nc, core.inp, core.x
    w_qb = inp["L0_attn_w_q_b"]
    w_kvb = inp["L0_attn_w_kv_b"]
    w_out = inp["L0_attn_w_out"]
    QW, KVW = 2 * DQ, 2 * (DN + DV)
    with ExitStack() as ctx:
        def sb(name, shape, dt=F32):
            return core.sb(f"lath_{name}", shape, dt, ctx)
        ones_r, minus_ident = sb("ones_r", [P, P], F32R), sb("minus_ident", [P, P])
        zero = sb("zero", [P, 1])
        raw_q, raw_kv, raw_out = raw
        q_w_t, kv_w_t = sb("q_w_t", [P, 2, QL]), sb("kv_w_t", [P, 2, 2, KL])
        w_query = sb("w_query", [P, 2, 2, P])
        w_hi, w_lo = sb("w_hi", [P, 2, P], F32R), sb("w_lo", [P, 2, P], F32R)
        w_rest_hi, w_rest_lo = sb("w_rest_hi", [P, 2, P], F32R), sb("w_rest_lo", [P, 2, P], F32R)
        w_value = sb("w_value", [P, DIM])
        turn_a, turn_b = sb("turn_a", [P, 2, CH]), sb("turn_b", [P, 2, CH])
        query = sb("query", [P, 2, CH])
        query_hi, query_lo = sb("query_hi", [P, NCH, 2, CH], F32R), sb("query_lo", [P, NCH, 2, CH], F32R)
        maxima = sb("maxima", [P, 2, TPC, NCH])
        row_max = sb("row_max", [P, 2, TPC])
        shift_diag = sb("shift_diag", [P, 2, TPC, P], F32R)
        shift = sb("shift", [P, 2, 2, CH])
        shifted = sb("shifted", [P, 4, CH])
        probs = sb("probs", [P, PROB_SLOTS, 2, CH])
        summed = sb("summed", [P, 2, 2, CH])
        out_whole, out_t, sums_t = sb("out_whole", [P, CH]), sb("out_t", [P, CH]), sb("sums_t", [P, CH])
        inverse = sb("inverse", [P, TPC, 2])
        wide = sums_t[:].rearrange("p (t h c) -> p t h c", t=TPC, h=2)
        score_bank = [ctx.enter_context(nc.psum_tensor(f"lath_score{i}", [P, CH], F32)) for i in range(3)]
        max_bank = [ctx.enter_context(nc.psum_tensor(f"lath_max{i}", [P, CH], F32)) for i in range(2)]
        out_bank = ctx.enter_context(nc.psum_tensor("lath_out", [P, CH], F32))
        end_bank = ctx.enter_context(nc.psum_tensor("lath_end", [P, CH], F32))
        side_bank = ctx.enter_context(nc.psum_tensor("lath_side", [P, CH], F32))
        names = ("q_kv_loaded out_loaded vector_constants"
                 " scores_done shift_added exp_done values_done"
                 " maxima_done maxima_taken row_max_done diag_ready side_done side_free"
                 " cosine_done sine_done query_whole query_hi_done query_lo_done"
                 " rotation_weights_ready query_weights_ready weights_high_done weights_split"
                 " drained tiles_summed end_done end_free inverse_wide").split()
        s = {n: core.sem(f"lath_{n}") for n in names}
        prologue, before = with_latent_uses(LATENT_PROLOGUE, -LATENT_SIDE_BEFORE)
        before = {in_chunk(e, e[1], e[1] + NCH): use + LATENT_SIDE_PER_PAIR for e, use in before.items()}
        first, uses = with_latent_uses(latent_schedule(True, False), 0, before)
        middle, _ = with_latent_uses(latent_schedule(False, False), 0, uses)
        final, _ = with_latent_uses(latent_schedule(False, True), 0, uses)
        fold_out_use = next(e[-1] for e in middle if e[0] == "fold_out")

        def pairs(engine, run):
            run(prologue, 0)
            run(first, 0)
            with engine.Fori(1, PAIRS - 1) as pair:
                run(middle, pair)
            run(final, PAIRS - 1)
            run(LATENT_EPILOGUE, PAIRS)

        def chunk(pair, j):
            return pair * NCH + j

        def step_unit(pair, j, kt):
            return pair * KT_PER_PAIR + KT_PER_PAIR * (j // NCH) + STEPS_BEFORE[j % NCH] + kt

        def score_unit(pair, j, kt, h):
            return step_unit(pair, j, kt) * 2 + h

        def score_place(j, kt, h):
            return 2 * (STEPS_BEFORE[j] + kt) + h

        def prob_slot(j, kt):
            return (STEPS_BEFORE[j % NCH] + kt) % PROB_SLOTS

        def sums_unit(pair, step):
            whole, step = divmod(step, KT_PER_PAIR)
            j = max(n for n in range(NCH) if STEPS_BEFORE[n] <= step)
            kt = step - STEPS_BEFORE[j]
            return (pair + whole) * (KT_PER_PAIR - (NCH - 1)) + STEPS_BEFORE[j] - max(j - 1, 0) + (max(kt, 1) if j else kt + 1)

        def maxima_unit(pair, j, h, i, kc):
            return step_unit(pair, j, 0) * 2 + (h * TPC + i) * (j % NCH + 1) + kc

        def end_use(pair, j, n):
            return 5 * chunk(pair, j) + n

        def side_use(pair, local):
            return pair * LATENT_SIDE_PER_PAIR + LATENT_SIDE_BEFORE + local

        with nc.Block() as block:
            @block.sync
            def _(sp):
                with sp.Fori(1, PAIRS) as pair:
                    sp.wait_ge(s["query_weights_ready"], pair)
                    sp.wait_ge(s["rotation_weights_ready"], pair)
                    sp.dma_start(raw_q[:, 0, :], w_qb[0:P, bass.ds(pair * QW, QW)]).then_inc(s["q_kv_loaded"], 16)
                    sp.dma_start(raw_q[0:QL - P, 1, :], w_qb[P:QL, bass.ds(pair * QW, QW)]).then_inc(s["q_kv_loaded"], 16)
                    sp.dma_start(raw_kv[0:KL, :], w_kvb[:, bass.ds(pair * KVW, KVW)]).then_inc(s["q_kv_loaded"], 16)
                    sp.wait_ge(s["side_free"], side_use(pair - 1, fold_out_use) + 1)
                    sp.dma_start(raw_out[:], w_out[bass.ds(pair * 2 * DV, 2 * DV), :].rearrange("(h p) e -> p h e", p=P))\
                      .then_inc(s["out_loaded"], 16)

            @block.tensor
            def _(pe):
                def run(events, pair):
                    for kind, *a in events:
                        if kind in ON_SIDE:
                            wait(pe, s["side_free"], side_use(pair, a[-1]))
                        if kind == "scores":
                            j, kt, h, use = a
                            u, place = score_unit(pair, j, kt, h), score_place(j, kt, h)
                            if kt == 0:
                                wait(pe, s["query_lo_done"], 2 * chunk(pair, j) + h + 1)
                            wait(pe, s["shift_added"], u - 2 if place >= 2 else u - 1)
                            diagonal = kt - TPC * j
                            q0 = max(diagonal, 0) * P
                            bank = score_bank[place % 3]
                            out = bank[:, q0:CH]
                            hi, lo = query_hi[:, j, h, q0:CH], query_lo[:, j, h, q0:CH]
                            keys = slice(kt * P, (kt + 1) * P)
                            nc.tensor.matmul(out, key_hi[:, keys], hi, start=True, stop=False)
                            nc.tensor.matmul(out, key_hi[:, keys], lo, start=False, stop=False)
                            if diagonal >= 0:
                                nc.tensor.matmul(bank[:, q0:q0 + P], core.ident_b, core.mask_kq, start=False, stop=False)
                            nc.tensor.matmul(out, key_lo[:, keys], hi, start=False, stop=True).then_inc(s["scores_done"], 1)
                        elif kind == "values":
                            j, kt, h = a
                            nj = j % NCH
                            wait(pe, s["exp_done"], score_unit(pair, j, kt, h) + 1)
                            if kt == 0 and h == 0:
                                wait(pe, s["drained"], chunk(pair, j))
                            q0 = max(kt - TPC * nj, 0) * P
                            mm = nc.tensor.matmul(out_bank[64 * h:64 * h + 64, q0:CH], latent[:, kt, 0:KL],
                                                  probs[:, prob_slot(j, kt), h, q0:CH], start=(kt == 0), stop=(kt == key_tiles(nj) - 1))
                            if h:
                                mm.then_inc(s["values_done"], 1)
                        elif kind == "maxima":
                            j, h, i, kc = a
                            nj = j % NCH
                            v = maxima_unit(pair, j, h, i, kc)
                            if i == 0 and kc == 0:
                                wait(pe, s["query_hi_done"], 2 * chunk(pair, j) + h + 1)
                            wait(pe, s["maxima_taken"], v - 1)
                            width = (i + 1) * P if kc == nj else CH
                            bank = max_bank[(i * (nj + 1) + kc) % 2]
                            mm = nc.tensor.matmul(bank[:, 0:width], query_hi[:, nj, h, i * P:(i + 1) * P],
                                                  key_hi[:, kc * CH:kc * CH + width], start=True, stop=(kc < nj))
                            if kc == nj:
                                mm = nc.tensor.matmul(bank[:, width - P:width], core.ident_b, core.mask_qk, start=False, stop=True)
                            mm.then_inc(s["maxima_done"], 1)
                        elif kind == "spread":
                            j, h, _ = a
                            wait(pe, s["diag_ready"], 2 * chunk(pair, j) + h + 1)
                            nc.tensor.matmul(side_bank[:], ones_r[:], shift_diag[:, h].rearrange("p t q -> p (t q)"),
                                             start=True, stop=True).then_inc(s["side_done"], 1)
                        elif kind == "query":
                            n, h, _ = a
                            if h == 0:
                                wait(pe, s["weights_split"], 2 * (pair + n // NCH + 1))
                            cols = slice((n % NCH) * CH, (n % NCH + 1) * CH)
                            products = ((w_hi, qa_t.hi), (w_hi, qa_t.lo), (w_lo, qa_t.hi), (w_rest_hi, qa_t.rest), (w_rest_lo, qa_t.rest))
                            for k, (w, q) in enumerate(products):
                                mm = nc.tensor.matmul(side_bank[:], w[:, h, :], q[:, cols], start=(k == 0), stop=(k == len(products) - 1))
                            mm.then_inc(s["side_done"], 1)
                        elif kind == "turn_q_weights":
                            wait(pe, s["q_kv_loaded"], 48 * (pair + a[0] // NCH))
                            for h in range(2):
                                nc.tensor.transpose(side_bank[:, h * QL:h * QL + P], raw_q[:, 0, h * DQ:h * DQ + DN], core.ident)
                                mm = nc.tensor.transpose(side_bank[:, h * QL + P:(h + 1) * QL], raw_q[0:QL - P, 1, h * DQ:h * DQ + DN],
                                                         core.ident[0:QL - P, 0:QL - P])
                            mm.then_inc(s["side_done"], 1)
                        elif kind == "turn_kv_weights":
                            for n in range(4):
                                mm = nc.tensor.transpose(side_bank[:, n * P:(n + 1) * P], raw_kv[:, n * P:(n + 1) * P], core.ident)
                            mm.then_inc(s["side_done"], 1)
                        elif kind == "fold_query":
                            for h in range(2):
                                nc.tensor.matmul(side_bank[:, h * P:h * P + KL], q_w_t[:, h, 0:P], kv_w_t[:, h, 0, :], start=True, stop=True)
                                mm = nc.tensor.matmul(side_bank[0:QL - P, h * P + KL:(h + 1) * P], q_w_t[:, h, P:QL], kv_w_t[:, h, 0, :],
                                                      start=True, stop=True)
                            mm.then_inc(s["side_done"], 1)
                        elif kind == "fold_out":
                            wait(pe, s["out_loaded"], 16 * pair)
                            for h in range(2):
                                mm = nc.tensor.matmul(side_bank[64 * h:64 * h + 64, 0:DIM], kv_w_t[:, h, 1, :], raw_out[:, h, :],
                                                      start=True, stop=True)
                            mm.then_inc(s["side_done"], 1)
                        elif kind == "sums":
                            j, = a
                            wait(pe, s["tiles_summed"], sums_unit(pair, KT_PER_PAIR * (j // NCH) + STEPS_BEFORE[j % NCH] + key_tiles(j % NCH) - 1))
                            wait(pe, s["end_free"], end_use(pair, j, 0))
                            for h in range(2):
                                mm = nc.tensor.matmul(end_bank[64 * h:64 * h + 64, :], core.ones[:, 0:64], summed[:, j % 2, h, :],
                                                      start=True, stop=True)
                            mm.then_inc(s["end_done"], 1)
                        elif kind == "turn_sums":
                            j, = a
                            wait(pe, s["end_free"], end_use(pair, j, 1))
                            for i in range(TPC):
                                mm = nc.tensor.transpose(end_bank[:, i * P:(i + 1) * P], sums_t[:, i * P:(i + 1) * P], core.ident)
                            mm.then_inc(s["end_done"], 1)
                        elif kind == "spread_inverse":
                            j, = a
                            wait(pe, s["end_free"], end_use(pair, j, 2))
                            wait(pe, s["inverse_wide"], chunk(pair, j) + 1)
                            for i in range(TPC):
                                mm = nc.tensor.transpose(end_bank[:, i * P:(i + 1) * P],
                                                         sums_t[:, i * P:(i + 1) * P], core.ident)
                            mm.then_inc(s["end_done"], 1)
                        elif kind == "project":
                            j, n = a
                            wait(pe, s["end_free"], end_use(pair, j, 3 + n))
                            for i in range(2):
                                mm = nc.tensor.matmul(end_bank[:, i * DIM:(i + 1) * DIM], out_t[:, (2 * n + i) * P:(2 * n + i + 1) * P], w_value[:],
                                                      start=True, stop=True)
                            mm.then_inc(s["end_done"], 1)

                pe.wait_ge(s["vector_constants"], 1)
                pairs(pe, run)

            @block.scalar
            def _(act):
                def copy_side(pair, use, out, columns):
                    wait(act, s["side_done"], side_use(pair, use) + 1)
                    return nc.scalar.activation(out, side_bank[:, columns], ACT.Copy)

                act.wait_ge(s["vector_constants"], 1)

                def run(events, pair):
                    for kind, *a in events:
                        if kind == "scores":
                            j, kt, h, use = a
                            q0 = max(kt - TPC * j, 0) * P
                            wait(act, s["shift_added"], score_unit(pair, j, kt, h) + 1)
                            wait(act, s["values_done"], step_unit(pair, j, kt) - PROB_SLOTS + 1)
                            if not (isinstance(pair, int) and step_unit(pair, j, kt) < PROB_SLOTS):
                                wait(act, s["tiles_summed"], sums_unit(pair, STEPS_BEFORE[j] + kt - PROB_SLOTS))
                            nc.scalar.activation(probs[:, prob_slot(j, kt), h, q0:CH], shifted[:, 2 * (kt % 2) + h, q0:CH], ACT.Exp,
                                                 scale=SCALE0).then_inc(s["exp_done"], 1)
                        elif kind == "drain":
                            j, = a
                            wait(act, s["values_done"], step_unit(pair, j, key_tiles(j % NCH) - 1) + 1)
                            wait(act, s["end_free"], end_use(pair, j - 1, 3))
                            nc.scalar.activation(out_whole[:], out_bank[:], ACT.Copy).then_inc(s["drained"], 1)
                        elif kind == "sums_out":
                            wait(act, s["end_done"], end_use(pair, a[0], 0) + 1)
                            nc.scalar.activation(sums_t[:], end_bank[:], ACT.Copy).then_inc(s["end_free"], 1)
                        elif kind == "turn_sums_out":
                            j, = a
                            wait(act, s["end_free"], end_use(pair, j, 2))
                            nc.scalar.activation(wide, inverse[:].unsqueeze(3).broadcast_to([P, TPC, 2, 64]), ACT.Copy)\
                              .then_inc(s["inverse_wide"], 1)
                        elif kind == "spread_out":
                            j, h, use = a
                            copy_side(pair, use, shift[:, j % 2, h, :], slice(0, CH)).then_inc(s["side_free"], 1)
                        elif kind == "query_out":
                            n, h, use = a
                            wait(act, s["query_lo_done"], 2 * chunk(pair, n) + h - 1)
                            copy_side(pair, use, query[:, h], slice(0, CH)).then_inc(s["side_free"], 1)
                        elif kind == "split":
                            n, h = a
                            wait(act, s["query_whole"], 2 * chunk(pair, n) + h + 1)
                            nc.scalar.activation(query_hi[:, n % NCH, h, :], query[:, h], ACT.Copy).then_inc(s["query_hi_done"], 1)
                        elif kind == "turn_q_weights_out":
                            copy_side(pair, a[-1], q_w_t[:].rearrange("p h r -> p (h r)"), slice(0, 2 * QL)).then_inc(s["side_free"], 1)
                            wait(act, s["weights_split"], 2 * (pair + a[0] // NCH))
                            for k, rows in enumerate((P, QL - P)):
                                rotated = raw_q[0:rows, k, :].rearrange("p (h c) -> p h c", h=2)[:, :, DN:DQ]
                                for odd in range(2):
                                    last = nc.scalar.activation(w_query[0:rows, k, :, KL + odd * DR // 2:KL + (odd + 1) * DR // 2],
                                                                rotated[:, :, odd:DR:2], ACT.Copy)
                            last.then_inc(s["rotation_weights_ready"], 1)
                        elif kind == "turn_kv_weights_out":
                            wait(act, s["side_done"], side_use(pair, a[-1]) + 1)
                            nc.scalar.activation(kv_w_t[:].rearrange("p h s r -> p (h s) r"),
                                                 side_bank[:].rearrange("p (n r) -> p n r", r=P)[:, :, 0:KL], ACT.Copy).then_inc(s["side_free"], 1)
                        elif kind == "fold_query_out":
                            wait(act, s["side_done"], side_use(pair, a[-1]) + 1)
                            folded = side_bank[:, 0:2 * P].rearrange("p (h k r) -> p h k r", h=2, k=2)
                            nc.scalar.activation(w_query[:, 0, :, 0:KL], folded[:, :, 0, :], ACT.Copy).then_inc(s["query_weights_ready"], 1)
                            nc.scalar.activation(w_query[0:QL - P, 1, :, 0:KL], folded[0:QL - P, :, 1, :], ACT.Copy).then_inc(s["side_free"], 1)
                        elif kind == "split_weights":
                            wait(act, s["rotation_weights_ready"], pair + a[0] // NCH + 1)
                            wait(act, s["side_free"], side_use(pair, a[-1]) + 1)
                            for to, of in ((w_hi[:], w_query[:, 0]), (w_rest_hi[0:64], w_query[0:64, 1]), (w_rest_hi[64:P], w_query[0:64, 1])):
                                last = nc.scalar.activation(to, of, ACT.Copy)
                            last.then_inc(s["weights_high_done"], 1)
                        elif kind == "fold_out_out":
                            copy_side(pair, a[-1], w_value[:], slice(0, DIM)).then_inc(s["side_free"], 1)

                pairs(act, run)

            @block.gpsimd
            def _(pool):
                def run(events, pair):
                    for kind, *a in events:
                        if kind == "values":
                            j, kt, head = a
                            nj = j % NCH
                            q0 = max(kt - TPC * nj, 0) * P
                            if head == 0 or kt == 0 and nj:
                                continue
                            if kt == (1 if nj else 0) and not (isinstance(pair, int) and chunk(pair, j) < 2):
                                wait(pool, s["end_done"], end_use(pair, j - 2, 0) + 1)
                            wait(pool, s["exp_done"], score_unit(pair, j, kt, 1) + 1)
                            if kt > (1 if nj else 0):
                                wait(pool, s["tiles_summed"], sums_unit(pair, KT_PER_PAIR * (j // NCH) + STEPS_BEFORE[nj] + kt - 1))
                            for h in range(2):
                                so_far = summed[:, j % 2, h, q0:CH]
                                if kt == 0:
                                    so_far = zero[:].broadcast_to([P, CH])
                                elif kt == 1 and nj:
                                    so_far = probs[:, prob_slot(j, 0), h, :]
                                last = nc.gpsimd.tensor_tensor(summed[:, j % 2, h, q0:CH], so_far, probs[:, prob_slot(j, kt), h, q0:CH], ALU.add)
                            last.then_inc(s["tiles_summed"], 1)
                        elif kind == "rotate":
                            n, h, use = a
                            r = 2 * chunk(pair, n) + h
                            pool.wait_ge(s["side_free"], side_use(pair, use) + 1)
                            nc.gpsimd.tensor_tensor(turn_a[:, h], query[:, h], rope[:, 0, (n % NCH) * CH:(n % NCH + 1) * CH],
                                                    ALU.mult).then_inc(s["cosine_done"], 1)
                            pool.wait_ge(s["cosine_done"], r + 1)
                            pool.wait_ge(s["sine_done"], 2 * r + 2)
                            nc.gpsimd.tensor_tensor(query[:, h], turn_a[:, h], turn_b[:, h], ALU.add).then_inc(s["query_whole"], 1)
                        elif kind == "split":
                            n, h = a
                            r = 2 * chunk(pair, n) + h
                            pool.wait_ge(s["query_hi_done"], r + 1)
                            nc.gpsimd.tensor_tensor(query_lo[:, n % NCH, h, :], query[:, h], query_hi[:, n % NCH, h, :].bitcast(F32),
                                                    ALU.subtract).then_inc(s["query_lo_done"], 1)

                pool.wait_ge(s["vector_constants"], 1)
                pairs(pool, run)

            @block.vector
            def _(dve):
                def run(events, pair):
                    for kind, *a in events:
                        if kind == "scores":
                            j, kt, h, use = a
                            u = score_unit(pair, j, kt, h)
                            q0 = max(kt - TPC * j, 0) * P
                            if kt == 0:
                                wait(dve, s["side_free"], side_use(pair, use) + 1)
                            wait(dve, s["scores_done"], u + 1)
                            wait(dve, s["exp_done"], u - 3)
                            nc.vector.tensor_tensor(shifted[:, 2 * (kt % 2) + h, q0:CH], score_bank[score_place(j, kt, h) % 3][:, q0:CH],
                                                    shift[:, j % 2, h, q0:CH], ALU.add).then_inc(s["shift_added"], 1)
                        elif kind == "maxima":
                            j, h, i, kc = a
                            nj = j % NCH
                            width = (i + 1) * P if kc == nj else CH
                            wait(dve, s["maxima_done"], maxima_unit(pair, j, h, i, kc) + 1)
                            nc.vector.reduce_max(maxima[:, h, i, kc:kc + 1], max_bank[(i * (nj + 1) + kc) % 2][:, 0:width],
                                                 AX.X).then_inc(s["maxima_taken"], 1)
                        elif kind == "shift":
                            j, h = a
                            nj = j % NCH
                            d = 2 * chunk(pair, j) + h
                            wait(dve, s["maxima_taken"], maxima_unit(pair, j, h, TPC - 1, nj) + 1)
                            nc.vector.reduce_max(row_max[:, h, :], maxima[:, h, :, 0:nj + 1], AX.X).then_inc(s["row_max_done"], 1)
                            wait(dve, s["row_max_done"], d + 1)
                            nc.vector.tensor_tensor(shift_diag[:, h], minus_ident[:].unsqueeze(1).broadcast_to([P, TPC, P]),
                                                    row_max[:, h, :].unsqueeze(2).broadcast_to([P, TPC, P]), ALU.mult).then_inc(s["diag_ready"], 1)
                        elif kind == "rotate":
                            n, h, use = a
                            cols = slice((n % NCH) * CH, (n % NCH + 1) * CH)
                            wait(dve, s["side_free"], side_use(pair, use) + 1)
                            wait(dve, s["query_whole"], 2 * chunk(pair, n) + h - 1)
                            nc.vector.tensor_tensor(turn_b[64:96, h], query[96:P, h], rope[96:P, 1, cols], ALU.mult).then_inc(s["sine_done"], 1)
                            nc.vector.tensor_tensor(turn_b[96:P, h], query[64:96, h], rope[64:96, 1, cols], ALU.mult).then_inc(s["sine_done"], 1)
                        elif kind == "split_weights_low":
                            wait(dve, s["weights_high_done"], pair + a[0] // NCH + 1)
                            nc.vector.tensor_tensor(w_lo[:], w_query[:, 0], w_hi[:].bitcast(F32), ALU.subtract).then_inc(s["weights_split"], 1)
                            nc.vector.tensor_tensor(w_rest_lo[0:64], w_query[0:64, 1], w_rest_hi[0:64].bitcast(F32), ALU.subtract)\
                              .then_inc(s["weights_split"], 1)
                        elif kind == "turn_sums_out":
                            j, = a
                            wait(dve, s["end_done"], end_use(pair, j, 1) + 1)
                            nc.vector.reciprocal(inverse[:], end_bank[:].rearrange("p (t h c) -> p t h c", t=TPC, h=2)[:, :, :, 0])\
                              .then_inc(s["end_free"], 1)
                        elif kind == "spread_inverse_out":
                            j, = a
                            wait(dve, s["end_done"], end_use(pair, j, 2) + 1)
                            wait(dve, s["drained"], chunk(pair, j) + 1)
                            nc.vector.tensor_tensor(out_t[:], out_whole[:], end_bank[:], ALU.mult).then_inc(s["end_free"], 1)
                        elif kind == "project_out":
                            j, half = a
                            t = TPC * (j % NCH) + 2 * half
                            wait(dve, s["end_done"], end_use(pair, j, 3 + half) + 1)
                            tiles = x[:, t:t + 2, :]
                            nc.vector.tensor_tensor(tiles, end_bank[:].rearrange("p (t d) -> p t d", d=DIM), tiles, ALU.add).then_inc(s["end_free"], 1)

                nc.vector.tensor_scalar(minus_ident[:], core.ident, -1.0, None, ALU.mult)
                nc.vector.memset(w_rest_lo[64:P].bitcast(F32), 0.0)
                nc.vector.memset(zero[:], 0.0)
                nc.vector.memset(turn_b[0:64], 0.0)
                nc.vector.memset(raw_kv[KL:P, :], 0.0)
                nc.vector.tensor_copy(ones_r[:], core.ones).then_inc(s["vector_constants"], 1)
                dve.wait_ge(s["vector_constants"], 1)
                pairs(dve, run)
    core.end_step()


def attention_stage(core):
    with ExitStack() as ctx:
        def sb(name, shape, dt=F32):
            return core.sb(f"att_{name}", shape, dt, ctx)
        qk = sb("qk", [P, NT, 2 * DIM])
        v = sb("v", [P, NT, DIM])
        w_o_t = sb("w_o_t", [P, ND, DIM])
        attended = sb("attended", [P, NT, DIM])
        attention_projections(core, qk, v, w_o_t)
        attention_heads(core, qk, v, attended)
        attention_output(core, attended, w_o_t)


def attention_projections(core, qk, v, w_o_t):
    nc, inp = core.nc, core.inp
    with ExitStack() as ctx:
        def sb(name, shape, dt=F32):
            return core.sb(f"attp_{name}", shape, dt, ctx)
        xn, xn_t = sb("xn", [P, NT, DIM]), sb("xn_t", [P, ND, TOKENS])
        raw = sb("raw", [P, 4, ND, DIM])
        w_qkv_t = sb("w_qkv_t", [P, ND, 3 * DIM])
        rope = sb("rope", [P, 2, NT, D1])
        by_cos, by_sin = sb("by_cos", [P, 2, 2 * DIM]), sb("by_sin", [P, 2, 2 * DIM])
        bank = [ctx.enter_context(nc.psum_tensor(f"attp_bank{i}", [P, CH], F32)) for i in range(8)]
        norm = Norm(core, ctx, "attn", xn, xn_t, bank[:4])
        names = "weights_loaded rope_loaded weights_turned weights_copied qk_done v_done products_done rotated v_copied".split()
        s = {n: core.sem(f"attp_{n}") for n in names}
        with nc.Block() as block:
            @block.sync
            def _(sp):
                for m, name in enumerate(("Wq", "Wk", "Wv", "Wo")):
                    sp.dma_start(raw[:, m], inp[f"L1_attn_{name}"].rearrange("(k p) d -> p k d", p=P)).then_inc(s["weights_loaded"], 16)
                sp.dma_start(rope[:], inp["c_rope1_token"]).then_inc(s["rope_loaded"], 16)

            @block.vector
            def _(dve):
                norm.vector(dve, Link(core, dve, "attp_link"))
                dve.wait_ge(s["rope_loaded"], 16)
                heads = 2 * H1
                for t in range(NT):
                    dve.wait_ge(s["qk_done"], t + 1)
                    if t >= 2:
                        dve.wait_ge(s["rotated"], 2 * (t - 1))
                    scores = bank[4 + t % 2][:].rearrange("p (h c) -> p h c", c=D1)
                    for out, table in ((by_cos, 0), (by_sin, 1)):
                        last = nc.vector.tensor_tensor(out[:, t % 2, :].rearrange("p (h c) -> p h c", c=D1), scores,
                                                       rope[:, table, t, :].unsqueeze(1).broadcast_to([P, heads, D1]), ALU.mult)
                    last.then_inc(s["products_done"], 1)

            @block.gpsimd
            def _(pool):
                for t in range(NT):
                    pool.wait_ge(s["products_done"], t + 1)
                    a, b = by_cos[:, t % 2, :], by_sin[:, t % 2, :]
                    nc.gpsimd.tensor_tensor(qk[:, t, 0:2 * DIM:2], a[:, 0:2 * DIM:2], b[:, 1:2 * DIM:2], ALU.subtract).then_inc(s["rotated"], 1)
                    nc.gpsimd.tensor_tensor(qk[:, t, 1:2 * DIM:2], b[:, 0:2 * DIM:2], a[:, 1:2 * DIM:2], ALU.add).then_inc(s["rotated"], 1)
                pool.wait_ge(s["rotated"], 2 * NT)

            @block.scalar
            def _(act):
                for m in range(4):
                    act.wait_ge(s["weights_turned"], m + 1)
                    to = w_o_t[:] if m == 3 else w_qkv_t[:, :, m * DIM:(m + 1) * DIM]
                    nc.scalar.activation(to, bank[4 + m][:].rearrange("p (k e) -> p k e", k=ND), ACT.Copy).then_inc(s["weights_copied"], 1)
                norm.scalar(act)
                for t in range(NT):
                    act.wait_ge(s["v_done"], t + 1)
                    nc.scalar.activation(v[:, t, :], bank[6 + t % 2][:, 0:DIM], ACT.Copy).then_inc(s["v_copied"], 1)
                act.wait_ge(s["v_copied"], NT)

            @block.tensor
            def _(pe):
                pe.wait_ge(s["weights_loaded"], 64)
                for m in range(4):
                    for k in range(ND):
                        for e in range(ND):
                            last = nc.tensor.transpose(bank[4 + m][:, k * DIM + e * P:k * DIM + (e + 1) * P],
                                                       raw[:, m, e, k * P:(k + 1) * P], core.ident)
                    last.then_inc(s["weights_turned"], 1)
                norm.tensor(pe)
                pe.wait_ge(s["weights_copied"], 4)
                for t in range(NT):
                    norm.turn.wait_chunk(pe, t // TPC)
                    if t >= 2:
                        pe.wait_ge(s["products_done"], t - 1)
                    for k in range(ND):
                        last = nc.tensor.matmul(bank[4 + t % 2][:], xn_t[:, k, t * P:(t + 1) * P], w_qkv_t[:, k, 0:2 * DIM],
                                                start=(k == 0), stop=(k == ND - 1))
                    last.then_inc(s["qk_done"], 1)
                    if t >= 2:
                        pe.wait_ge(s["v_copied"], t - 1)
                    for k in range(ND):
                        last = nc.tensor.matmul(bank[6 + t % 2][:, 0:DIM], xn_t[:, k, t * P:(t + 1) * P], w_qkv_t[:, k, 2 * DIM:3 * DIM],
                                                start=(k == 0), stop=(k == ND - 1))
                    last.then_inc(s["v_done"], 1)
    core.end_step()


LAG = 2
FINISH_AT = (3.8, 2.95, 3.3, 2.85)
MAXIMA_STEPS = [(-11.1, -8.55), (-6.9, -0.4), (-0.5, 9.7), (9.4, 22.8)]
TURN_STEPS = [(1.25, 0.6, -0.3, 0.5, 0.4, -0.1), (1.25, 1.2, 0.2, 0.5, 0.4, 0.2), (1.25, 0.6, 0.2, 0.5, 0.75, 0.2), (1.25, 0.6, 0.2, 0.5, 0.5, 0.2)]


def preparation(j):
    start, end = MAXIMA_STEPS[j]
    units = [[("maxima", j, h, i, kc) for i in range(TPC) for kc in range(j + 1)] for h in range(GROUP)]
    main = units[0] + units[1] + [("shift", j, 0)] + units[2] + units[3] + [("shift", j, 1)]
    each = (end - start) / len(main)
    out = [(start - 3, ("split", j)), (start + 2.2, ("split_values", j))]
    out += [(start + n * each, event) for n, event in enumerate(main)]

    def turn(step, kind, pair):
        halves = 1 if kind == "turn_keys" else 2
        return [[(step, (kind, j, pair))] + [(step + 0.24 * (n + 1), ("place", kind, j, pair, n)) for n in range(halves)]]
    middle = (start + end) / 2
    turns = turn(start - TURN_STEPS[j][0], "turn_keys", 0) + turn(start - TURN_STEPS[j][1], "turn_queries", 0)
    turns += turn(start + TURN_STEPS[j][2] * (middle - start), "turn_keys", 1) + turn(start + TURN_STEPS[j][3] * (middle - start), "turn_queries", 1)
    turns += turn(middle + TURN_STEPS[j][4], "turn_shifted", 0) + turn(end + TURN_STEPS[j][5], "turn_shifted", 1)
    return out, turns


def placed_events():
    placed = []
    for j in range(NCH):
        alone, turns = preparation(j)
        placed += [(step, j, [(step, event)]) for step, event in alone] + [(turn[0][0], j, turn) for turn in turns]
    for j in range(-1, NCH - 1):
        step = STEPS_BEFORE[j + 1] + FINISH_AT[j + 1]
        placed.append((step, j, [(step, ("finish", j))]))
    placed.sort(key=lambda p: p[0])
    out, side_end = [], -KT_PER_PAIR
    for step, j, together in placed:
        if together[0][1][0].startswith("turn") or together[0][1][0] == "finish":
            late = max(side_end - step, 0)
            side_end = together[-1][0] + late + 0.01
            together = [(at + late, event) for at, event in together]
        out.append((step, j, together))
    return out


def attention_schedule(first, last):
    placed = []
    for step, j, together in placed_events():
        if step >= 0 and not (first and j < 0):
            placed += together
        elif step < 0 and not last:
            placed += [(at + KT_PER_PAIR, in_chunk(event, j, j + NCH)) for at, event in together]
    placed.sort(key=lambda e: e[0])
    events = []
    for j in range(NCH):
        for kt in range(key_tiles(j)):
            follow = (j, kt - LAG) if kt >= LAG else (j - 1, key_tiles((j - 1) % NCH) - LAG + kt)
            atoms = [[("scores", j, kt, 0)], [("scores", j, kt, 1)], [("scores", j, kt, 2)], [("scores", j, kt, 3)], []]
            if not (first and j == 0 and kt < LAG):
                for half in range(2):
                    atoms[2 * half + 2].append(("values", *follow, half))
                if kt == LAG - 1:
                    atoms[4].append(("drain", j - 1))
            for n, atom in enumerate(atoms):
                events += atom
                while placed and placed[0][0] < STEPS_BEFORE[j] + kt + (n + 1) / len(atoms):
                    events.append(placed.pop(0)[1])
    return events + [event for _, event in placed]


def attention_prologue():
    placed = [e for step, _, together in placed_events() if step < 0 for e in together]
    return [event for _, event in sorted(placed, key=lambda e: e[0])]


ATTENTION_EPILOGUE = ([("values", -1, key_tiles(NCH - 1) - LAG + i, half) for i in range(LAG) for half in range(2)]
                      + [("drain", -1), ("finish", -1)])
VECTOR_PLACES = (0, 1)
SIDE_PER_GROUP = 7 * NCH
SIDE_BEFORE = sum(e[0].startswith("turn") for e in attention_prologue()) - 1


def with_side_uses(events, start, earlier):
    out, uses = [], dict(earlier)
    for e in events:
        kind, j, *rest = e
        if kind == "place":
            e = (*e, uses[e[1:4]])
        elif kind.startswith("turn") or kind == "finish":
            if kind != "finish":
                uses[kind, j, rest[0]] = start
            e, start = (*e, start), start + 1
        elif kind == "split":
            e = (*e, uses.get(("turn_shifted", j - 2, 1)))
        elif kind == "maxima":
            e = (*e, uses["turn_queries", j, rest[0] // 2])
        elif kind == "scores":
            e = (*e, uses["turn_shifted", j, rest[1] // 2])
        out.append(e)
    return out, start, uses


def attention_heads(core, qk, v, attended):
    nc = core.nc
    prologue, _, uses = with_side_uses(attention_prologue(), -SIDE_BEFORE, {})
    first, _, uses = with_side_uses(attention_schedule(True, False), 1, uses)
    uses = {(kind, j - NCH, pair): use - SIDE_PER_GROUP for (kind, j, pair), use in uses.items()}
    middle, _, _ = with_side_uses(attention_schedule(False, False), 0, uses)
    final, side_end, _ = with_side_uses(attention_schedule(False, True), 0, uses)
    epilogue, _, _ = with_side_uses(ATTENTION_EPILOGUE, side_end - SIDE_PER_GROUP, {})
    with ExitStack() as ctx:
        def sb(name, shape, dt=F32):
            return core.sb(f"atth_{name}", shape, dt, ctx)
        q_slot, k_slot = sb("q_slot", [P, 2, TPC, GROUP, SLOT]), sb("k_slot", [P, 2, TPC, GROUP, SLOT])
        v_one = sb("v_one", [P, NT, GROUP, 32])
        key = sb("key", [P, 2, TOKENS], F32R)
        query = sb("query", [P, NCH, GROUP, CH], F32R)
        maxima = sb("maxima", [P, GROUP, TPC, NCH])
        row_max = sb("row_max", [P, GROUP, TPC])
        probs = sb("probs", [P, 4, GROUP, CH])
        out_t = sb("out_t", [P, CH])
        inverse = sb("inverse", [P, TPC, GROUP])
        score_bank = [ctx.enter_context(nc.psum_tensor(f"atth_score{i}", [P, CH], F32)) for i in range(3)]
        max_bank = [ctx.enter_context(nc.psum_tensor(f"atth_max{i}", [P, CH], F32)) for i in range(3)]
        out_bank = ctx.enter_context(nc.psum_tensor("atth_out", [P, CH], F32))
        side_bank = ctx.enter_context(nc.psum_tensor("atth_side", [P, CH], F32))
        names = ("constants_ready zeroed_by_pool zeroed q_high_done q_low_done q_copied k_high_done k_low_done k_copied v_copied"
                 " side_done side_free maxima_done maxima_taken row_max_done"
                 " shift_high_done shift_ready scores_done exp_done values_done drained inverse_ready").split()
        s = {n: core.sem(f"atth_{n}") for n in names}

        def groups(engine, run):
            run(prologue, 0)
            run(first, 0)
            with engine.Fori(1, NG - 1) as group:
                run(middle, group)
            run(final, NG - 1)
            run(epilogue, NG)

        def chunk(group, j):
            return group * NCH + j

        def side_use(group, local):
            return group * SIDE_PER_GROUP + SIDE_BEFORE + local

        def step_unit(group, j, kt):
            return group * KT_PER_PAIR + KT_PER_PAIR * (j // NCH) + STEPS_BEFORE[j % NCH] + kt

        def score_unit(group, j, kt, h):
            return step_unit(group, j, kt) * GROUP + h

        def maxima_unit(group, j, h, i, kc):
            return step_unit(group, j, 0) * GROUP + (h * TPC + i) * (j % NCH + 1) + kc

        def maxima_place(j, h, i, kc):
            return GROUP * STEPS_BEFORE[j % NCH] + (h * TPC + i) * (j % NCH + 1) + kc

        def score_place(j, kt, h):
            return GROUP * (STEPS_BEFORE[j] + kt) + h

        def group_columns(group, j, base=0):
            start = (group + j // NCH) * (GROUP * D1) + base
            return slice(start, start + GROUP * D1) if isinstance(start, int) else bass.ds(start, GROUP * D1)

        def tiles(j):
            return slice(TPC * (j % NCH), TPC * (j % NCH) + TPC)

        def part(slot, j, n):
            return slot[:, j % 2, :, :, n * D1:(n + 1) * D1]

        def by_head(tensor, j, columns):
            return tensor[:, tiles(j), columns].rearrange("p t (h c) -> p t h c", c=D1)

        def rows_of(n):
            return slice(64 * n, 64 * n + 64)

        def placed_by_vector(place):
            kind, j, pair, n, _ = place
            return j % NCH in VECTOR_PLACES and (n == 1 or kind == "turn_keys")

        def place(engine, group, what, copy):
            kind, j, pair, n, local = what
            wait(engine, s["side_done"], side_use(group, local) + 1)
            if kind == "turn_keys":
                copy(key[:, pair, (j % NCH) * CH:(j % NCH + 1) * CH], side_bank[:]).then_inc(s["side_free"], 2)
            else:
                copy(query[rows_of(n), j % NCH, 2 * pair + n, :], side_bank[rows_of(n), :]).then_inc(s["side_free"], 1)

        with nc.Block() as block:
            @block.vector
            def _(dve):
                nc.vector.memset(q_slot[:, :, :, :, 3 * D1:SLOT], 0.0)
                nc.vector.memset(k_slot[:, :, :, :, 3 * D1:SLOT], 0.0).then_inc(s["constants_ready"], 1)
                dve.wait_ge(s["constants_ready"], 1)
                nc.vector.memset(k_slot[:, :, :, :, 3 * D1:3 * D1 + 2], 1.0)
                for h in range(GROUP):
                    last = nc.vector.memset(query[rows_of(1 - h % 2), 0, h, :].bitcast(F32), 0.0)
                last.then_inc(s["constants_ready"], 1)

                def run(events, group):
                    for kind, *a in events:
                        if kind == "split":
                            j, before = a
                            if before is not None:
                                wait(dve, s["side_done"], side_use(group, before) + 1)
                            nc.vector.memset(q_slot[:, j % 2, :, :, 3 * D1:3 * D1 + 2], 0.0).then_inc(s["zeroed"], 1)
                        elif kind == "place" and placed_by_vector(a):
                            place(dve, group, a, nc.vector.tensor_copy)
                        elif kind == "maxima":
                            j, h, i, kc, turned = a
                            m = maxima_unit(group, j, h, i, kc)
                            nj = j % NCH
                            width = (i + 1) * P if kc == nj else CH
                            wait(dve, s["maxima_done"], m + 1)
                            nc.vector.reduce_max(maxima[:, h, i, kc:kc + 1], max_bank[maxima_place(j, h, i, kc) % 3][:, 0:width], AX.X)\
                              .then_inc(s["maxima_taken"], 1)
                        elif kind == "shift":
                            j, pair = a
                            nj, n = j % NCH, 2 * chunk(group, j) + pair
                            heads = slice(2 * pair, 2 * pair + 2)
                            wait(dve, s["maxima_taken"], maxima_unit(group, j, 2 * pair + 1, TPC - 1, nj) + 1)
                            nc.vector.reduce_max(row_max[:, heads, :], maxima[:, heads, :, 0:nj + 1], AX.X).then_inc(s["row_max_done"], 1)
                            wait(dve, s["row_max_done"], n + 1)
                            high, low = (q_slot[:, j % 2, :, heads, 3 * D1 + c].rearrange("p t h -> p h t") for c in range(2))
                            nc.vector.tensor_scalar(high.bitcast(F32R), row_max[:, heads, :], -1.0, None, ALU.mult).then_inc(s["shift_high_done"], 1)
                            wait(dve, s["shift_high_done"], n + 1)
                            nc.vector.scalar_tensor_tensor(low, row_max[:, heads, :], -1.0, high, ALU.mult, ALU.subtract).then_inc(s["shift_ready"], 1)
                        elif kind == "finish":
                            j, local = a
                            wait(dve, s["side_done"], side_use(group, local) + 1)
                            ended = side_bank[:].rearrange("p (t h c) -> p t h c", t=TPC, h=GROUP)
                            nc.vector.reciprocal(inverse[:], ended[:, :, :, D1]).then_inc(s["inverse_ready"], 1)
                            wait(dve, s["inverse_ready"], chunk(group, j) + 1)
                            nc.vector.tensor_tensor(by_head(attended, j, group_columns(group, j)), ended[:, :, :, 0:D1],
                                                    inverse[:].unsqueeze(3).broadcast_to([P, TPC, GROUP, D1]),
                                                    ALU.mult).then_inc(s["side_free"], 2)
                groups(dve, run)

            @block.gpsimd
            def _(pool):
                def run(events, group):
                    for kind, *a in events:
                        if kind == "split":
                            j, _ = a
                            n = chunk(group, j)
                            wait(pool, s["q_high_done"], n + 1)
                            nc.gpsimd.tensor_tensor(part(q_slot, j, 2), by_head(qk, j, group_columns(group, j)), part(q_slot, j, 0),
                                                    ALU.subtract).then_inc(s["q_low_done"], 1)
                            wait(pool, s["k_high_done"], n + 1)
                            nc.gpsimd.tensor_tensor(part(k_slot, j, 1), by_head(qk, j, group_columns(group, j, DIM)), part(k_slot, j, 0),
                                                    ALU.subtract).then_inc(s["k_low_done"], 1)
                nc.gpsimd.memset(v_one[:, :, :, D1:32], 0.0).then_inc(s["zeroed_by_pool"], 1)
                pool.wait_ge(s["zeroed_by_pool"], 1)
                nc.gpsimd.memset(v_one[:, :, :, D1:D1 + 1], 1.0).then_inc(s["zeroed_by_pool"], 1)
                for n, h in enumerate((0, 2, 1, 3)):
                    pool.wait_ge(s["zeroed_by_pool"], n + 2)
                    nc.gpsimd.memset(query[rows_of(1 - h % 2), 1:NCH, h, :].bitcast(F32), 0.0).then_inc(s["zeroed_by_pool"], 1)
                pool.wait_ge(s["zeroed_by_pool"], 6)
                groups(pool, run)

            @block.scalar
            def _(act):
                act.wait_ge(s["constants_ready"], 2)

                def run(events, group):
                    for kind, *a in events:
                        if kind == "split":
                            j, before = a
                            if before is not None:
                                wait(act, s["side_done"], side_use(group, before) + 1)
                            n = chunk(group, j)
                            nc.scalar.activation(part(q_slot, j, 0).bitcast(F32R), by_head(qk, j, group_columns(group, j)), ACT.Copy)\
                              .then_inc(s["q_high_done"], 1)
                            nc.scalar.activation(part(k_slot, j, 0).bitcast(F32R), by_head(qk, j, group_columns(group, j, DIM)), ACT.Copy)\
                              .then_inc(s["k_high_done"], 1)
                            wait(act, s["q_high_done"], n + 1)
                            nc.scalar.activation(part(q_slot, j, 1), part(q_slot, j, 0), ACT.Copy).then_inc(s["q_copied"], 1)
                            wait(act, s["k_high_done"], n + 1)
                            nc.scalar.activation(part(k_slot, j, 2), part(k_slot, j, 0), ACT.Copy).then_inc(s["k_copied"], 1)
                        elif kind == "split_values":
                            j, = a
                            if j >= NCH or not isinstance(group, int) or group > 0:
                                wait(act, s["values_done"], step_unit(group, j - j % NCH - 1, TPC * (j % NCH) + TPC - 1) + 1)
                            nc.scalar.activation(v_one[:, tiles(j), :, 0:D1], by_head(v, j, group_columns(group, j)), ACT.Copy)\
                              .then_inc(s["v_copied"], 1)
                        elif kind == "place" and not placed_by_vector(a):
                            place(act, group, a, lambda to, of: nc.scalar.activation(to, of, ACT.Copy))
                        elif kind == "scores":
                            j, kt, h, turned = a
                            q0 = max(kt - TPC * j, 0) * P
                            wait(act, s["scores_done"], score_unit(group, j, kt, h) + 1)
                            wait(act, s["values_done"], step_unit(group, j, kt) - 3)
                            nc.scalar.activation(probs[:, kt % 4, h, q0:CH], score_bank[score_place(j, kt, h) % 3][:, q0:CH], ACT.Exp,
                                                 scale=SCALE1).then_inc(s["exp_done"], 1)
                        elif kind == "drain":
                            j, = a
                            wait(act, s["values_done"], step_unit(group, j, key_tiles(j % NCH) - 1) + 1)
                            nc.scalar.activation(out_t[:], out_bank[:], ACT.Copy).then_inc(s["drained"], 1)
                groups(act, run)

            @block.tensor
            def _(pe):
                def turn(slot, j, pair):
                    for i in range(TPC):
                        last = nc.tensor.transpose(side_bank[:, i * P:(i + 1) * P], slot[:, j % 2, i, 2 * pair:2 * pair + 2, :]
                                                   .rearrange("p h c -> p (h c)"), core.ident)
                    last.then_inc(s["side_done"], 1)

                def run(events, group):
                    for kind, *a in events:
                        if kind.startswith("turn") or kind == "finish":
                            wait(pe, s["side_free"], side_use(group, a[-1]) * 2)
                        if kind == "turn_keys":
                            j, pair, local = a
                            wait(pe, s["k_low_done"], chunk(group, j) + 1)
                            wait(pe, s["k_copied"], chunk(group, j) + 1)
                            turn(k_slot, j, pair)
                        elif kind == "turn_queries":
                            j, pair, local = a
                            wait(pe, s["q_low_done"], chunk(group, j) + 1)
                            wait(pe, s["q_copied"], chunk(group, j) + 1)
                            wait(pe, s["zeroed"], chunk(group, j) + 1)
                            turn(q_slot, j, pair)
                        elif kind == "turn_shifted":
                            j, pair, local = a
                            wait(pe, s["shift_ready"], 2 * chunk(group, j) + pair + 1)
                            turn(q_slot, j, pair)
                        elif kind == "maxima":
                            j, h, i, kc, turned = a
                            m = maxima_unit(group, j, h, i, kc)
                            nj = j % NCH
                            if h % 2 == 0 and i == 0 and kc == 0:
                                wait(pe, s["side_free"], 2 * (side_use(group, turned) + 1))
                            wait(pe, s["maxima_taken"], m - 2 if maxima_place(j, h, i, kc) else m)
                            width = (i + 1) * P if kc == nj else CH
                            bank = max_bank[maxima_place(j, h, i, kc) % 3]
                            mm = nc.tensor.matmul(bank[:, 0:width], query[:, j % NCH, h, i * P:(i + 1) * P],
                                                  key[:, h // 2, kc * CH:kc * CH + width], start=True, stop=(kc < nj))
                            if kc == nj:
                                mm = nc.tensor.matmul(bank[:, width - P:width], core.ident_b, core.mask_qk, start=False, stop=True)
                            mm.then_inc(s["maxima_done"], 1)
                        elif kind == "scores":
                            j, kt, h, turned = a
                            u = score_unit(group, j, kt, h)
                            if kt == 0:
                                wait(pe, s["side_free"], 2 * (side_use(group, turned) + 1))
                            wait(pe, s["exp_done"], u - 2 if score_place(j, kt, h) else u)
                            diagonal = kt - TPC * j
                            q0 = max(diagonal, 0) * P
                            bank = score_bank[score_place(j, kt, h) % 3]
                            mm = nc.tensor.matmul(bank[:, q0:CH], key[:, h // 2, kt * P:(kt + 1) * P],
                                                  query[:, j % NCH, h, q0:CH], start=True, stop=(diagonal < 0))
                            if diagonal >= 0:
                                mm = nc.tensor.matmul(bank[:, q0:q0 + P], core.ident_b, core.mask_kq, start=False, stop=True)
                            mm.then_inc(s["scores_done"], 1)
                        elif kind == "values":
                            j, kt, half = a
                            nj = j % NCH
                            q0 = max(kt - TPC * nj, 0) * P
                            wait(pe, s["exp_done"], score_unit(group, j, kt, 2 * half + 1) + 1)
                            if kt % TPC == 0 and kt // TPC == nj and half == 0:
                                wait(pe, s["v_copied"], chunk(group, j) + 1)
                            if kt == 0 and half == 0:
                                wait(pe, s["drained"], chunk(group, j))
                            for h in (2 * half, 2 * half + 1):
                                mm = nc.tensor.matmul(out_bank[32 * h:32 * h + 32, q0:CH], v_one[:, kt, h, :],
                                                      probs[:, kt % 4, h, q0:CH],
                                                      start=(kt == 0), stop=(kt == key_tiles(nj) - 1))
                            if half:
                                mm.then_inc(s["values_done"], 1)
                        elif kind == "finish":
                            j, local = a
                            wait(pe, s["drained"], chunk(group, j) + 1)
                            for i in range(TPC):
                                last = nc.tensor.transpose(side_bank[:, i * P:(i + 1) * P], out_t[:, i * P:(i + 1) * P], core.ident)
                            last.then_inc(s["side_done"], 1)

                pe.wait_ge(s["constants_ready"], 2)
                groups(pe, run)
    core.end_step()


def attention_output(core, attended, w_o_t):
    nc, x = core.nc, core.x
    with ExitStack() as ctx:
        attended_t = core.sb("atto_attended_t", [P, ND, TOKENS], F32, ctx)
        bank = [ctx.enter_context(nc.psum_tensor(f"atto_bank{i}", [P, CH], F32)) for i in range(8)]
        turn = Turn(core, "atto", attended, attended_t, bank[:4], source_complete=True)
        projected, added = core.sem("atto_projected"), core.sem("atto_added")
        with nc.Block() as block:
            @block.vector
            def _(dve):
                turn.vector(dve)
                for b in range(NT // 2):
                    dve.wait_ge(projected, b + 1)
                    pair = x[:, 2 * b:2 * b + 2, :]
                    nc.vector.tensor_tensor(pair, bank[4 + b % 4][:].rearrange("p (t d) -> p t d", d=DIM), pair, ALU.add).then_inc(added, 1)
                dve.wait_ge(added, NT // 2)

            @block.scalar
            def _(act):
                turn.scalar(act)

            @block.tensor
            def _(pe):
                turn.tensor(pe)
                for b in range(NT // 2):
                    turn.wait_chunk(pe, 2 * b // TPC)
                    if b >= 4:
                        pe.wait_ge(added, b - 3)
                    for i in range(2):
                        t = 2 * b + i
                        for k in range(ND):
                            last = nc.tensor.matmul(bank[4 + b % 4][:, i * DIM:(i + 1) * DIM], attended_t[:, k, t * P:(t + 1) * P],
                                                    w_o_t[:, k, :], start=(k == 0), stop=(k == ND - 1))
                    last.then_inc(projected, 1)
    core.end_step()


def macaron_program(nc, inp, out):
    with ExitStack() as ctx:
        core = Core(nc, ctx, inp)
        routed_ffn_stage(core, "ffn_a", first=True)
        latent_attention_stage(core)
        routed_ffn_stage(core, "ffn_b")
        mixed_ffn_stage(core, "mix_a")
        attention_stage(core)
        mixed_ffn_stage(core, "mix_b", out)


_INS = ['L0_attn_x', 'L0_attn_w_q_a', 'L0_attn_q_a_ln', 'L0_attn_w_q_b', 'L0_attn_w_kv_a', 'L0_attn_kv_a_ln',
        'L0_attn_w_kv_b', 'L0_attn_w_out', 'L0_ffn_W_r', 'L0_ffn_b_r', 'L0_ffn_W1', 'L0_ffn_b1', 'L0_ffn_W2',
        'L0_ffn_b2', 'L1_attn_Wq', 'L1_attn_Wk', 'L1_attn_Wv', 'L1_attn_Wo', 'L1_ffn_factors', 'L1_ffn_bias']


def kernel(**inputs):
    import concourse.bacc as bacc
    from concourse.bass_utils import run_bass_kernel_spmd

    nc = bacc.Bacc("TRN2", target_bir_lowering=False, num_devices=1)
    arrays = {name: np.ascontiguousarray(inputs[name]) for name in _INS}
    arrays.update(shape_constants())
    aps = {name: nc.dram_tensor(f"in_{name}", a.shape, mybir.dt.from_np(a.dtype), kind="ExternalInput").ap()
           for name, a in arrays.items()}
    out = nc.dram_tensor("out", (1, TOKENS, DIM), F32, kind="ExternalOutput").ap()
    macaron_program(nc, aps, out)
    result = run_bass_kernel_spmd(nc, [{f"in_{name}": a for name, a in arrays.items()}], core_ids=[0])
    return result.results[0]["out"]
```
